# Optimizing a Trainium2 kernel written in Bass

```python
import numpy as np
import jax
import jax.numpy as jnp

def _softmax(x, axis=-1):
    return jax.nn.softmax(x, axis=axis)

def _gelu(x):
    return jax.nn.gelu(x, approximate=True)

def _silu(x):
    return jax.nn.silu(x)

def _sigmoid(x):
    return jax.nn.sigmoid(x)

def _layernorm(x, axis=-1, eps=1e-05):
    m = jnp.mean(x, axis=axis, keepdims=True)
    v = jnp.var(x, axis=axis, keepdims=True)
    return (x - m) / jnp.sqrt(v + eps)

def _scatter_add(tgt, idx, src, axis=0):
    return tgt.at[idx].add(src)

def _segment_sum(src, seg, n):
    return jax.ops.segment_sum(src, seg, n)
kernel_name = 'mk_decoder_postln_d1_seqx_r8_881c36'

def setup_inputs(seed: int=0):
    np.random.seed(seed)
    _w = jnp.asarray

    def _rec_inputs():
        import jax
        import jax.numpy as jnp
        _rk = jax.random.key(seed)
        x = -0.0002928 + 1 * jax.random.normal(jax.random.fold_in(_rk, 1), (64, 128, 128), jnp.float32)
        _lenS = 128 - jax.random.randint(jax.random.fold_in(_rk, 7), (64,), 0, max(1, 128 // 4) + 1, jnp.int32)
        _lenS2 = 120 - jax.random.randint(jax.random.fold_in(_rk, 8), (64,), 0, max(1, 120 // 4) + 1, jnp.int32)
        _ctx_768P = jax.random.normal(jax.random.fold_in(_rk, 11), (64, 16, 96), jnp.float32)
        _ctx_768c = jax.random.dirichlet(jax.random.fold_in(_rk, 511), 0.3 * jnp.ones((16,), jnp.float32), (64, 120))
        _ctx_768t = jnp.einsum('bsk,bkd->bsd', _ctx_768c, _ctx_768P)
        _ctx_768t = _ctx_768t * jax.lax.rsqrt(jnp.mean(jnp.square(_ctx_768t)) + 1e-12) * 0.953939
        ctx_768 = 2.09791e-05 + 1.00001 * (_ctx_768t + 0.3 * jax.random.normal(jax.random.fold_in(_rk, 611), (64, 120, 96), jnp.float32))
        _validS = jnp.arange(128)[None, :] < _lenS[:, None]
        _validS2 = jnp.arange(120)[None, :] < _lenS2[:, None]
        _causal = jnp.tril(jnp.ones((128, 128), dtype=bool))
        mask_BxS2_bf1 = jnp.ones((64, 120), dtype=bool)
        return (x, ctx_768, mask_BxS2_bf1)
    x, ctx_768, mask_BxS2_bf1 = _rec_inputs()

    def _L0_attn_setup():
        import jax, jax.numpy as jnp
        import numpy as np
        D_MODEL = 128
        key = jax.random.key(seed)
        k1, k2, k3, k4 = jax.random.split(key, 4)
        B, T, D, E = (8, 256, 128, 128)
        x = jax.random.normal(k1, (B, T, D), dtype=jnp.float32)
        Wq = jax.random.normal(k2, (D, E), dtype=jnp.float32) * (1.0 / np.sqrt(D))
        Wk = jax.random.normal(k3, (D, E), dtype=jnp.float32) * (1.0 / np.sqrt(D))
        Wv = jax.random.normal(k4, (D, E), dtype=jnp.float32) * (1.0 / np.sqrt(D))
        return {'x': x, 'Wq': Wq, 'Wk': Wk, 'Wv': Wv}
    _L0_attn_all = _L0_attn_setup()
    _L0_attn_in = {k: v for k, v in _L0_attn_all.items() if k in ('Wq', 'Wk', 'Wv')}
    del _L0_attn_all

    def _L0_xattn_setup():
        import jax, jax.numpy as jnp
        import numpy as np
        import math
        B, N, M = (4, 128, 128)
        DIM, CTX_DIM = (128, 96)
        HEADS, DIM_HEAD = (16, 64)
        INNER = HEADS * DIM_HEAD

        def layer_norm(t, g, eps=1e-05):
            mean = jnp.mean(t, axis=-1, keepdims=True)
            var = jnp.mean((t - mean) ** 2, axis=-1, keepdims=True)
            return (t - mean) * jax.lax.rsqrt(var + eps) * g
        key = jax.random.key(seed)
        ks = jax.random.split(key, 8)
        return {'x': jax.random.normal(ks[0], (B, N, DIM), jnp.float32), 'context': jax.random.normal(ks[1], (B, M, CTX_DIM), jnp.float32), 'mask': jnp.ones((B, M), dtype=bool), 'g_norm': jnp.ones((DIM,), jnp.float32), 'null_kv': jax.random.normal(ks[2], (2, DIM_HEAD), jnp.float32), 'Wq': jax.random.normal(ks[3], (DIM, INNER), jnp.float32) * DIM ** (-0.5), 'Wkv': jax.random.normal(ks[4], (CTX_DIM, 2 * INNER), jnp.float32) * CTX_DIM ** (-0.5), 'Wout': jax.random.normal(ks[5], (INNER, DIM), jnp.float32) * INNER ** (-0.5), 'g_out': jnp.ones((DIM,), jnp.float32)}
    _L0_xattn_all = _L0_xattn_setup()
    _L0_xattn_in = {k: v for k, v in _L0_xattn_all.items() if k in ('g_norm', 'null_kv', 'Wq', 'Wkv', 'Wout', 'g_out')}
    del _L0_xattn_all

    def _L0_ffn_setup():
        import jax, jax.numpy as jnp
        import numpy as np
        B, C, D = (2, 256, 128)
        I = 256
        E, K = (8, 2)
        CF = 1.25
        key = jax.random.key(seed)
        k1, k2, k3, k4 = jax.random.split(key, 4)
        scale = 0.02
        return {'hidden_states': jax.random.normal(k1, (B, C, D), jnp.float32), 'Wg': jax.random.normal(k2, (E, D), jnp.float32) * scale, 'W1': jax.random.normal(k3, (E, D, 2 * I), jnp.float32) * scale, 'W2': jax.random.normal(k4, (E, I, D), jnp.float32) * scale}
    _L0_ffn_all = _L0_ffn_setup()
    _L0_ffn_in = {k: v for k, v in _L0_ffn_all.items() if k in ('Wg', 'W1', 'W2')}
    del _L0_ffn_all
    return {'x': x, 'ctx_768': ctx_768, 'mask_BxS2_bf1': mask_BxS2_bf1, 'L0_attn_Wq': _L0_attn_in['Wq'], 'L0_attn_Wk': _L0_attn_in['Wk'], 'L0_attn_Wv': _L0_attn_in['Wv'], 'L0_xattn_g_norm': _L0_xattn_in['g_norm'], 'L0_xattn_null_kv': _L0_xattn_in['null_kv'], 'L0_xattn_Wq': _L0_xattn_in['Wq'], 'L0_xattn_Wkv': _L0_xattn_in['Wkv'], 'L0_xattn_Wout': _L0_xattn_in['Wout'], 'L0_xattn_g_out': _L0_xattn_in['g_out'], 'L0_ffn_Wg': _L0_ffn_in['Wg'], 'L0_ffn_W1': _L0_ffn_in['W1'], 'L0_ffn_W2': _L0_ffn_in['W2']}

def reference(x, ctx_768, mask_BxS2_bf1, L0_attn_Wq, L0_attn_Wk, L0_attn_Wv, L0_xattn_g_norm, L0_xattn_null_kv, L0_xattn_Wq, L0_xattn_Wkv, L0_xattn_Wout, L0_xattn_g_out, L0_ffn_Wg, L0_ffn_W1, L0_ffn_W2):
    import jax
    import jax.numpy as jnp

    def _L0_attn_ref(x, Wq, Wk, Wv):
        import jax, jax.numpy as jnp
        import numpy as np
        D_MODEL = 128
        T = x.shape[1]
        Q = x @ Wq
        K = x @ Wk
        V = x @ Wv
        scale = 1.0 / jnp.sqrt(jnp.asarray(D_MODEL, dtype=x.dtype))
        w = jnp.einsum('bte,bse->bts', Q, K) * scale
        causal = jnp.tril(jnp.ones((T, T), dtype=bool))
        w = jnp.where(causal, w, -jnp.inf)
        w = jax.nn.softmax(w, axis=-1)
        return w @ V

    def _L0_xattn_ref(x, context, mask, g_norm, null_kv, Wq, Wkv, Wout, g_out):
        import jax, jax.numpy as jnp
        import numpy as np
        import math
        B, N, M = (4, 128, 128)
        DIM, CTX_DIM = (128, 96)
        HEADS, DIM_HEAD = (16, 64)
        INNER = HEADS * DIM_HEAD

        def layer_norm(t, g, eps=1e-05):
            mean = jnp.mean(t, axis=-1, keepdims=True)
            var = jnp.mean((t - mean) ** 2, axis=-1, keepdims=True)
            return (t - mean) * jax.lax.rsqrt(var + eps) * g
        b = x.shape[0]
        scale = DIM_HEAD ** (-0.5)
        sqrt_scale = math.sqrt(scale)
        x = layer_norm(x, g_norm)
        q = x @ Wq
        kv = context @ Wkv
        k, v = jnp.split(kv, 2, axis=-1)

        def to_heads(t):
            return t.reshape(b, t.shape[1], HEADS, DIM_HEAD).transpose(0, 2, 1, 3)
        q, k, v = (to_heads(q), to_heads(k), to_heads(v))
        nk = jnp.broadcast_to(null_kv[0], (b, HEADS, 1, DIM_HEAD))
        nv = jnp.broadcast_to(null_kv[1], (b, HEADS, 1, DIM_HEAD))
        k = jnp.concatenate([nk, k], axis=2)
        v = jnp.concatenate([nv, v], axis=2)
        q = q * sqrt_scale
        k = k * sqrt_scale
        sim = jnp.einsum('bhid,bhjd->bhij', q, k)
        max_neg = -jnp.finfo(sim.dtype).max
        full_mask = jnp.pad(mask, ((0, 0), (1, 0)), constant_values=True)
        sim = jnp.where(full_mask[:, None, None, :], sim, max_neg)
        attn = jax.nn.softmax(sim.astype(jnp.float32), axis=-1).astype(sim.dtype)
        out = jnp.einsum('bhij,bhjd->bhid', attn, v)
        out = out.transpose(0, 2, 1, 3).reshape(b, -1, INNER)
        out = out @ Wout
        return layer_norm(out, g_out)

    def _L0_ffn_ref(hidden_states, Wg, W1, W2):
        import jax, jax.numpy as jnp
        import numpy as np
        B, C, D = (2, 256, 128)
        I = 256
        E, K = (8, 2)
        CF = 1.25
        Bx, Cx, d = hidden_states.shape
        N = Bx * Cx
        cap = int(N * K * CF / E)
        x = hidden_states.reshape(N, d)
        logits = x @ Wg.T
        top_v, top_i = jax.lax.top_k(logits, K)
        gates = jax.nn.softmax(top_v, axis=-1)
        flat_e = top_i.reshape(N * K)
        gates_f = gates.reshape(N * K)
        tok = jnp.repeat(jnp.arange(N), K)
        onehot = jax.nn.one_hot(flat_e, E, dtype=jnp.int32)
        pos = jnp.cumsum(onehot, axis=0) - 1
        pos_f = jnp.take_along_axis(pos, flat_e[:, None], axis=1)[:, 0]
        keep = pos_f < cap
        pos_safe = jnp.where(keep, pos_f, cap)
        exp_batches = jnp.zeros((E, cap, d), x.dtype).at[flat_e, pos_safe].set(x[tok], mode='drop')
        h = jnp.einsum('ecd,edf->ecf', exp_batches, W1)
        inp, gate = jnp.split(h, 2, axis=-1)
        h = jax.nn.gelu(inp, approximate=False) * gate
        exp_out = jnp.einsum('eci,eid->ecd', h, W2)
        gathered = exp_out[flat_e, jnp.minimum(pos_safe, cap - 1)]
        contrib = jnp.where(keep, gates_f, 0.0)[:, None] * gathered
        out = jax.ops.segment_sum(contrib, tok, num_segments=N)
        return out.reshape(Bx, Cx, d)
    x = _layernorm(x + _L0_attn_ref(x, L0_attn_Wq, L0_attn_Wk, L0_attn_Wv), axis=-1)
    x = _layernorm(x + _L0_xattn_ref(x, ctx_768, mask_BxS2_bf1, L0_xattn_g_norm, L0_xattn_null_kv, L0_xattn_Wq, L0_xattn_Wkv, L0_xattn_Wout, L0_xattn_g_out), axis=-1)
    x = _layernorm(x + _L0_ffn_ref(x, L0_ffn_Wg, L0_ffn_W1, L0_ffn_W2), axis=-1)
    return x

_drawn_inputs = setup_inputs


def setup_inputs(seed=0):
    import zlib

    import numpy as np

    out = dict(_drawn_inputs(seed))
    spreads = {'L0_xattn_g_norm': (1.0, 0.2), 'L0_xattn_g_out': (1.0, 0.2)}
    factors = {'L0_ffn_Wg': 8.0, 'L0_ffn_W1': 8.0, 'L0_ffn_W2': 8.0}
    for name, (base, spread) in spreads.items():
        noise = np.random.default_rng([zlib.crc32(name.encode()), seed]).standard_normal(out[name].shape)
        drawn = base * np.exp(spread * noise) if base else spread * noise
        out[name] = jnp.asarray(drawn.astype(out[name].dtype))
    for name, factor in factors.items():
        out[name] = (out[name] * factor).astype(out[name].dtype)
    return out
```

```python
from contextlib import ExitStack

import concourse.bass as bass
from concourse import mybir

F32 = mybir.dt.float32
F32R = mybir.dt.float32r
BF16 = mybir.dt.bfloat16
I32 = mybir.dt.int32
U8 = mybir.dt.uint8
ALU = mybir.AluOpType
ACT = mybir.ActivationFunctionType
AX_X = mybir.AxisListType.X

B, T, D = 64, 128, 128
S2, C = 120, 96
H, E = 16, 64
KEYS = S2 + 1
CA = C + 2
NULL_ROW, MASK_ROW = C, C + 1
GB = 4
NG = B // GB
HH = H // 2
HB = HH // 2
X, K2, FI = 8, 2, 256
TOKENS = B * T
CAP = int(TOKENS * K2 * 1.25 / X)
SLOTS = X * CAP
SG = 512
GPX = CAP // SG
MASKED = -float(2 ** 100)
SKIP = float(2 * SLOTS)
EPS = 1e-5
BANK = 512
assert CAP % SG == 0 and GPX % 2 == 1


class Chain:

    def __init__(self, eng, sem):
        self.eng, self.sem, self.n, self.loop = eng, sem, 0, None

    def enter(self, i, start, per):
        self.loop = (i, start, per, self.n)

    def leave(self, turns):
        i, start, per, n0 = self.loop
        assert self.n - n0 == per, (self.n - n0, per)
        self.n, self.loop = n0 + per * turns, None

    def link(self, ins):
        ins.then_inc(self.sem, 1)
        self.n += 1
        if self.loop is None:
            self.eng.wait_ge(self.sem, self.n)
        else:
            i, start, per, _ = self.loop
            self.eng.wait_ge(self.sem, i * per + (self.n - start * per))


def wait(eng, sem, value):
    if not isinstance(value, int) or value > 0:
        eng.wait_ge(sem, value)


def decoder(nc, x, ctx_in, mask, wq_s, wk_s, wv_s, g_norm, null_kv, wq_c, wkv, wout, g_out, wg, w1, w2, out):
    with ExitStack() as stack:
        def sb(name, shape, dt=F32):
            return stack.enter_context(nc.sbuf_tensor(name, shape, dt))

        def pair(name):
            return stack.enter_context(nc.psum_tensor(name, [128, 2, BANK], F32))

        def sem(name):
            return stack.enter_context(nc.semaphore(name))

        xs_d = nc.dram_tensor("routed_rows", [SLOTS, D], F32, kind="Internal").ap()
        ys_d = nc.dram_tensor("expert_rows", [SLOTS, D], F32, kind="Internal").ap()
        x2_d = nc.dram_tensor("tokens_x2", [TOKENS, D], F32, kind="Internal").ap()

        ps_s, ps_t, ps_0, ps_1 = pair("ps_scores"), pair("ps_turned"), pair("ps_0"), pair("ps_1")

        ident = sb("ident", [128, 128])
        causal = sb("causal", [T, T])
        before = sb("before", [128, 128], BF16)
        ones_b = sb("ones_b", [128, 128], BF16)
        rev = sb("rev", [128, X])
        neg_half = sb("neg_half", [128, GB])
        zeros = sb("zeros", [128, 2048])
        row_bias = sb("row_bias", [CA, 1])
        wqk = sb("wqk", [D, D])
        wv_self = sb("wv_self", [D, D])
        G_hi, G_lo = sb("G_hi", [D, H, CA], F32R), sb("G_lo", [D, H, CA], F32R)
        wv_aug = sb("wv_aug", [CA, H * E])
        wv_hi, wv_lo = sb("wv_hi", [CA, H * E], F32R), sb("wv_lo", [CA, H * E], F32R)
        wout_sb = sb("wout_sb", [128, H * E // 128, D])
        g_col = sb("g_col", [D, 1])
        g_out_bc = sb("g_out_bc", [T, D])
        wgT = sb("wgT", [D, X])
        mask_u8 = sb("mask_u8", [B, S2], U8)
        mask_f = sb("mask_f", [B, S2])
        maskT = sb("maskT", [S2, B])
        w1_all = sb("w1_all", [D, X, 2 * FI])
        w2_all = sb("w2_all", [128, X, FI // 128, D])
        x_raw = sb("x_raw", [T, GB, D])
        xT = sb("xT", [D, GB, T])
        sA = sb("sA", [D, GB, T])
        sV = sb("sV", [T, GB, D])
        sS = sb("sS", [T, GB, T])
        sP = sb("sP", [T, GB, T])
        sPT = sb("sPT", [T, GB, T])
        s_nmax, s_sum, s_rec = sb("s_nmax", [T, GB]), sb("s_sum", [T, GB]), sb("s_rec", [T, GB])
        r1 = sb("r1", [T, GB, D])
        st6 = sb("st6", [T, GB, 6])
        mv1 = sb("mv1", [T, GB, 2])
        rs1, rn1 = sb("rs1", [T, GB]), sb("rn1", [T, 2, GB])
        lnt = sb("lnt", [T, 3, GB])
        x1, x1_late = sb("x1", [T, GB, D]), sb("x1_late", [T, 3, D])
        x1T = sb("x1T", [D, GB, T])
        x1T_hi, x1T_lo = sb("x1T_hi", [D, GB, T], F32R), sb("x1T_lo", [D, GB, T], F32R)
        rn_late = sb("rn_late", [T, 1])

        ctx_rows = sb("ctx_rows", [KEYS, GB, CA])
        ctxT = sb("ctxT", [CA, GB, KEYS])
        ctxT_hi, ctxT_lo = sb("ctxT_hi", [CA, GB, KEYS], F32R), sb("ctxT_lo", [CA, GB, KEYS], F32R)
        A = [sb(f"A{i}", [CA, H, T]) for i in range(2)]
        V = [sb(f"V{i}", [KEYS, H, E + 1]) for i in range(2)]
        top = sb("top", [T, 2, HB])
        shifted = [sb(f"shifted{i}", [T, 2, HB, KEYS]) for i in range(2)]
        P = [sb(f"P{i}", [T, H, KEYS]) for i in range(2)]
        PT = sb("PT", [KEYS, HH, T])
        rec = sb("rec", [T, 2, HB])
        O = sb("O", [T, H, E])
        OT = sb("OT", [128, 8, T])
        st_o, mv_o, rs_o, lne_o = sb("st_o", [T, 6]), sb("mv_o", [T, 2]), sb("rs_o", [T, 1]), sb("lne_o", [T, 1])
        centred = sb("centred", [T, D])
        r2, mv2, rs2, lne2 = sb("r2", [T, GB, D]), sb("mv2", [T, GB, 2]), sb("rs2", [T, GB]), sb("lne2", [T, GB])

        x2 = sb("x2", [T, GB, D])
        x2T = sb("x2T", [D, GB, T])
        m12 = sb("m12", [T, 2, GB])
        eq, L2 = sb("eq", [T, GB, X]), sb("L2", [T, GB, X])
        r12 = sb("r12", [T, 2, GB])
        oh = sb("oh", [T, 2, GB, X])
        picked = sb("picked", [T, GB, X], BF16)
        dlt, ex, gate = sb("dlt", [T, GB]), sb("ex", [T, GB]), sb("gate", [T, 2, GB])
        pos, taken = sb("pos", [T, GB, X]), sb("taken", [T, X])
        at = sb("at", [T, 2, GB, X])
        place, first, over = sb("place", [T, 2, GB]), sb("first", [T, 2, GB]), sb("over", [T, 2, GB])
        slot_f = sb("slot_f", [T, 2, GB])
        slot = sb("slot", [T, 2, GB], I32)
        back_all = sb("back_all", [T, NG, 2 * GB])
        gate_all = sb("gate_all", [T, NG, 2 * GB])

        s = {}
        for name in """weights_in small_in mask_in zero_set consts setup_T setup_Ts setup_qk setup_G setup_Gs setup_mask setup_done
                       x_in ctx_in xs_zeroed x2_saved scattered
                       scores_done v_done PT_done a_done pv_done OT_done wout_done
                       xT_done sA_done sV_done sS_done sPT_done sPV_done x1T_done ctxT_done x2T_done logits_done rank_done
                       shifted_done heads_scaled out_centred out_var r2_done
                       sS_masked r1_done r1_var x1_done x2_done mask_col logits_read picked_done rank_read slots_done dlt_done r2_var
                       probs_done v_kept PT_kept a_kept OT_kept
                       xT_kept sA_kept sV_kept sP_done sPT_kept x1T_kept ctxT_kept x2T_kept ex_done
                       out_rstd x1_rstd x2_rstd x1_saved x1T_split ctxT_split scatters_sent
                       dve_chain pool_chain act_chain waited""".split():
            s[name] = sem(name)

        with ExitStack() as early:
            def eb(name, shape, dt=F32):
                return early.enter_context(nc.sbuf_tensor(name, shape, dt))

            wq_a, wk_a = eb("wq_a", [D, D]), eb("wk_a", [D, D])
            wqT_a, wkT_a = eb("wqT_a", [D, D]), eb("wkT_a", [D, D])
            wq_sb = eb("wq_sb", [D, H * E])
            wk_aug = eb("wk_aug", [CA, H * E])
            wg_sb = eb("wg_sb", [X, D])
            wqT, wkT = eb("wqT", [128, 8, D]), eb("wkT", [128, 8, CA])

        xg = [sb(f"xg{i}", [128, 4, D]) for i in range(2)]
        xgT_hi, xgT_lo = sb("xgT_hi", [D, SG], F32R), sb("xgT_lo", [D, SG], F32R)
        w1_hi = [sb(f"w1_hi{i}", [D, 2 * FI], F32R) for i in range(2)]
        w1_lo = [sb(f"w1_lo{i}", [D, 2 * FI], F32R) for i in range(2)]
        w2_e = [sb(f"w2_e{i}", [128, 2, D]) for i in range(2)]
        act_u = sb("act_u", [128, 2, SG])
        hid = [sb(f"hid{i}", [128, 2, SG]) for i in range(2)]
        yg = [sb(f"yg{i}", [128, 4, D]) for i in range(2)]
        for name in """xg_in0 xg_in1 xgT_done xg_hi_kept xg_lo_kept inp_done gates_done gelu_done hid_done y_done y_kept yg_out0 yg_out1 w_split
                       x2_back0 x2_back1 y_back0 y_back1 idx_set r3_var r3_rstd out_ready out_saved0 out_saved1 gathers_sent""".split():
            s[name] = sem(name)
        idx = [sb(f"idx{i}", [T, 2 * GB], I32) for i in range(2)]
        flat_P = [P[i][:].rearrange("p h j -> p (h j)") for i in range(2)]
        yb = [flat_P[i][:, 0:2 * GB * D].rearrange("p (j b d) -> p j b d", j=2, b=GB) for i in range(2)]
        final = [flat_P[i][:, 2 * GB * D:3 * GB * D].rearrange("p (b d) -> p b d", b=GB) for i in range(2)]
        x2b = [shifted[i][:].rearrange("p b h j -> p (b h j)")[:, 0:GB * D].rearrange("p (b d) -> p b d", b=GB) for i in range(2)]
        r3 = O[:, 0:HH, :].rearrange("p (b u) e -> p b (u e)", b=GB)
        gate_t = sb("gate_t", [T, 2 * GB])
        mv3, rs3, lne3 = sb("mv3", [T, GB, 2]), sb("rs3", [T, GB]), sb("lne3", [T, GB])

        block = stack.enter_context(nc.Block())

        def live(g, k):
            if not isinstance(g, int):
                return True, True, True, True
            c = GB * g + k
            return c < B, 1 <= c <= B, 2 <= c < B + 2, c + 1 < B

        def more(g):
            return not isinstance(g, int) or g + 1 < NG

        def routes(g):
            return not isinstance(g, int) or 1 <= g <= NG

        def all_groups(eng, group, chain=None, links=0):
            group(0)
            group(1)
            with eng.Fori(2, NG - 1) as g:
                if chain:
                    chain.enter(g, 2, links)
                group(g)
            if chain:
                chain.leave(NG - 3)
            group(NG - 1)
            group(NG)

        def alone(eng):
            eng.sem_inc(s["waited"], 1)

        def heads4(ps, rows, width):
            return ps[:rows, :, 0:HB * width].rearrange("p b (h e) -> p b h e", h=HB)

        @block.sync
        def _(sp):
            sp.dma_start(x_raw[:], x[0:GB].rearrange("b t d -> t b d")).then_inc(s["x_in"], 16)
            for dst, src in ((wq_a[:], wq_s), (wk_a[:], wk_s), (wv_self[:], wv_s), (wq_sb[:], wq_c),
                             (wk_aug[0:C, :], wkv[:, 0:H * E]), (wv_aug[0:C, :], wkv[:, H * E:2 * H * E]),
                             (wout_sb[:], wout.rearrange("(j p) d -> p j d", p=128)),
                             (w1_all[:], w1.rearrange("e d f -> d e f")),
                             (w2_all[:], w2.rearrange("e (i p) d -> p e i d", p=128))):
                sp.dma_start(dst, src).then_inc(s["weights_in"], 16)
            sp.wait_ge(s["zero_set"], 1)
            sp.dma_start(ctx_rows[0:S2, :, 0:C], ctx_in[0:GB].rearrange("b j c -> j b c")).then_inc(s["ctx_in"], 16)
            for dst, kv in ((wk_aug, 0), (wv_aug, 1)):
                sp.dma_start(dst[NULL_ROW:NULL_ROW + 1, :].rearrange("o (h e) -> o h e", h=H),
                             null_kv[kv:kv + 1, :].unsqueeze(1).broadcast_to([1, H, E])).then_inc(s["small_in"], 16)
            sp.dma_start(g_col[:], g_norm.rearrange("(d o) -> d o", o=1)).then_inc(s["small_in"], 16)
            sp.dma_start(g_out_bc[:], g_out.rearrange("(o d) -> o d", o=1).broadcast_to([T, D])).then_inc(s["small_in"], 16)
            sp.dma_start(wg_sb[:], wg).then_inc(s["small_in"], 16)
            sp.dma_start(mask_u8[:], mask).then_inc(s["mask_in"], 16)
            rows = 2048 * 128 // D
            for z in range(SLOTS // rows):
                sp.dma_start(xs_d[z * rows:(z + 1) * rows].rearrange("(p r) d -> p (r d)", p=128), zeros[:]).then_inc(s["xs_zeroed"], 16)
            sp.wait_ge(s["r1_done"], 1)
            sp.dma_start(x_raw[:], x[GB:2 * GB].rearrange("b t d -> t b d")).then_inc(s["x_in"], 16)

            def group(g):
                def batches(dram, i):
                    part = dram[i * GB:(i + 1) * GB] if isinstance(i, int) else dram[bass.ds(i * GB, GB)]
                    return part.rearrange("b j c -> j b c")

                if more(g):
                    sp.wait_ge(s["ctxT_done"], g + 1)
                    sp.dma_start(ctx_rows[0:S2, :, 0:C], batches(ctx_in, g + 1)).then_inc(s["ctx_in"], 16)
                if routes(g):
                    sp.wait_ge(s["x2_done"], g)
                    at_row = (g - 1) * (GB * T)
                    rows2 = x2_d[at_row:at_row + GB * T] if isinstance(g, int) else x2_d[bass.ds(at_row, GB * T)]
                    sp.dma_start(rows2.rearrange("(b t) d -> t b d", t=T), x2[:]).then_inc(s["x2_saved"], 16)
                if not isinstance(g, int) or g + 2 < NG:
                    sp.wait_ge(s["r1_done"], g + 2)
                    sp.dma_start(x_raw[:], batches(x, g + 2)).then_inc(s["x_in"], 16)

            group(0)
            group(1)
            with sp.Fori(2, NG - 2) as g:
                group(g)
            group(NG - 2)
            group(NG - 1)
            group(NG)

            sp.wait_ge(s["scattered"], 16 * 2 * GB * NG)

            def rows_of(dram, t):
                part = dram[t * SG:(t + 1) * SG] if isinstance(t, int) else dram[bass.ds(t * SG, SG)]
                return part.rearrange("(p r) d -> p r d", p=128)

            def expert_pair(i):
                for u in range(2 * GPX):
                    t = 2 * GPX * i + u
                    if not isinstance(t, int) or t >= 2:
                        sp.wait_ge(s["xgT_done"], t - 1)
                    sp.dma_start(xg[u % 2][:], rows_of(xs_d, t)).then_inc(s[f"xg_in{u % 2}"], 16)
                    if not isinstance(t, int) or t >= 2:
                        sp.wait_ge(s["y_kept"], t - 1)
                        sp.dma_start(rows_of(ys_d, t - 2), yg[u % 2][:]).then_inc(s[f"yg_out{u % 2}"], 16)

            expert_pair(0)
            with sp.Fori(1, X // 2) as i:
                expert_pair(i)
            for t in (X * GPX - 2, X * GPX - 1):
                sp.wait_ge(s["y_kept"], t + 1)
                sp.dma_start(rows_of(ys_d, t), yg[t % 2][:]).then_inc(s[f"yg_out{t % 2}"], 16)

            sp.wait_ge(s["x2_saved"], 16 * NG)

            def tokens_of(dram, t):
                part = dram[t * GB * T:(t + 1) * GB * T] if isinstance(t, int) else dram[bass.ds(t * (GB * T), GB * T)]
                return part.rearrange("(b t) d -> t b d", t=T)

            out_rows = out.rearrange("b t d -> (b t) d")

            def token_pair(i):
                for u in range(2):
                    t = 2 * i + u
                    if not isinstance(t, int) or t >= 2:
                        sp.wait_ge(s["out_ready"], t - 1)
                        sp.dma_start(tokens_of(out_rows, t - 2), final[u]).then_inc(s[f"out_saved{u}"], 16)
                    sp.dma_start(x2b[u], tokens_of(x2_d, t)).then_inc(s[f"x2_back{u}"], 16)

            token_pair(0)
            with sp.Fori(1, NG // 2) as i:
                token_pair(i)
            for t in (NG - 2, NG - 1):
                sp.wait_ge(s["out_ready"], t + 1)
                sp.dma_start(tokens_of(out_rows, t), final[t % 2]).then_inc(s[f"out_saved{t % 2}"], 16)
            for u in range(2):
                sp.wait_ge(s[f"out_saved{u}"], 16 * NG // 2)
                sp.wait_ge(s[f"yg_out{u}"], 16 * X * GPX // 2)

        @block.gpsimd
        def _(pool):
            chain = Chain(pool, s["pool_chain"])
            chain.link(pool.memset(wk_aug[C:CA, :], 0.0))
            chain.link(pool.memset(wv_aug[C:CA, :], 0.0))
            chain.link(pool.memset(ctx_rows[:], 0.0))
            null_mark = ctx_rows[:, :, NULL_ROW:NULL_ROW + 1]
            chain.link(pool.affine_select(out=null_mark, in_=null_mark, pattern=[[0, GB], [0, 1]], compare_op=ALU.not_equal,
                                          fill=1.0, base=-S2, channel_multiplier=1))
            chain.link(pool.memset(zeros[:], 0.0))
            chain.link(pool.memset(neg_half[:], -0.5))
            pool.memset(taken[:], 0.0).then_inc(s["zero_set"], 1)
            for t in (ident, causal, row_bias):
                chain.link(pool.memset(t[:], 0.0))
            for t in (before, ones_b):
                chain.link(pool.memset(t[:], 1.0))
            chain.link(pool.affine_select(out=ident[:], in_=ident[:], pattern=[[-1, 128]], compare_op=ALU.not_equal,
                                          fill=1.0, base=0, channel_multiplier=1))
            chain.link(pool.affine_select(out=causal[:], in_=causal[:], pattern=[[-1, T]], compare_op=ALU.is_ge,
                                          fill=MASKED, base=0, channel_multiplier=1))
            chain.link(pool.affine_select(out=before[:], in_=before[:], pattern=[[1, 128]], compare_op=ALU.is_gt,
                                          fill=0.0, base=0, channel_multiplier=-1))
            chain.link(pool.affine_select(out=row_bias[:], in_=row_bias[:], pattern=[[0, 1]], compare_op=ALU.not_equal,
                                          fill=1.0, base=-MASK_ROW, channel_multiplier=1))
            for v in V:
                chain.link(pool.memset(v[:, :, E:E + 1], 1.0))
            for e in range(X):
                chain.link(pool.memset(rev[:, e:e + 1], float(X - e)))
            pool.memset(top[:], 0.0).then_inc(s["consts"], 1)

            def rsqrt(dst, var, plus):
                alone(pool)
                chain.link(pool.tensor_scalar(plus, var, EPS, None, ALU.add))
                return pool.tensor_tensor(dst, plus, neg_half[:, 0:dst.shape[1]], ALU.pow)

            def self_norm(g):
                pool.wait_ge(s["r1_var"], g + 1)
                var = mv1[:, :, 1]
                chain.link(rsqrt(rs1[:], var, lnt[:, 0, :]))
                chain.link(pool.tensor_tensor(lnt[:, 1, :], rs1[:], rs1[:], ALU.mult))
                chain.link(pool.tensor_tensor(lnt[:, 2, :], lnt[:, 1, :], var, ALU.mult))
                rsqrt(rn1[:, 1, :], lnt[:, 2, :], lnt[:, 0, :]).then_inc(s["x1_rstd"], 1)

            def split(hi, lo, whole, done):
                alone(pool)
                chain.link(pool.tensor_copy(hi, whole))
                alone(pool)
                pool.tensor_tensor(lo, whole, hi.bitcast(F32), ALU.subtract).then_inc(done, 1)

            def split_x1T(g):
                pool.wait_ge(s["x1T_kept"], g + 1)
                split(x1T_hi[:], x1T_lo[:], x1T[:], s["x1T_split"])

            def split_ctxT(g):
                pool.wait_ge(s["ctxT_kept"], g + 1)
                split(ctxT_hi[:], ctxT_lo[:], ctxT[:], s["ctxT_split"])

            split_ctxT(0)
            self_norm(0)
            split_x1T(0)
            pool.wait_ge(s["xs_zeroed"], 16 * (SLOTS // 2048))

            def group(g):
                for k in range(GB):
                    c, p, q, n = live(g, k)
                    if q:
                        pool.wait_ge(s["out_var"], GB * g + (k - 1))
                        rsqrt(rs_o[:], mv_o[:, 1:2], lne_o[:]).then_inc(s["out_rstd"], 1)
                    if k == 0 and (not isinstance(g, int) or g >= 2):
                        pool.wait_ge(s["slots_done"], g - 1)
                        alone(pool)
                        for b in range(GB):
                            for j in range(2):
                                pool.indirect_dma_start(
                                    out=xs_d, out_offset=bass.IndirectOffsetOnAxis(ap=slot[:, j, b:b + 1], axis=0),
                                    in_=x2[:, b, :], in_offset=None, bounds_check=SLOTS - 1,
                                    oob_is_err=False).then_inc(s["scattered"], 16)
                    if k == 1 and routes(g):
                        pool.wait_ge(s["r2_var"], g)
                        rsqrt(rs2[:], mv2[:, :, 1], lne2[:]).then_inc(s["x2_rstd"], 1)
                    if k == 1 and (not isinstance(g, int) or g < NG):
                        pool.wait_ge(s["r2_done"], GB * g) if routes(g) else None
                        alone(pool)
                        pool.tensor_copy(x1_late[:], x1[:, 1:GB, :]).then_inc(s["x1_saved"], 1)
                    if k == 2 and more(g):
                        self_norm(g + 1)
                    if k == 2 and more(g):
                        split_x1T(g + 1)
                    if k == 3 and more(g):
                        split_ctxT(g + 1)

            all_groups(pool, group, chain, POOL_LINKS)
            pool.wait_ge(s["slots_done"], NG)
            for b in range(GB):
                for j in range(2):
                    pool.indirect_dma_start(
                        out=xs_d, out_offset=bass.IndirectOffsetOnAxis(ap=slot[:, j, b:b + 1], axis=0),
                        in_=x2[:, b, :], in_offset=None, bounds_check=SLOTS - 1,
                        oob_is_err=False).then_inc(s["scattered"], 16)

            def expert_pair(i):
                for u in range(2):
                    e = 2 * i + u
                    if not isinstance(e, int) or e >= 2:
                        pool.wait_ge(s["y_done"], GPX * e - GPX)
                    one = (lambda t: t[:, e]) if isinstance(e, int) else (lambda t: t[:, bass.ds(e, 1)])
                    whole = one(w1_all) if isinstance(e, int) else one(w1_all).rearrange("p o f -> p (o f)")
                    down = one(w2_all) if isinstance(e, int) else one(w2_all).rearrange("p o i d -> p (o i) d")
                    alone(pool)
                    chain.link(pool.tensor_copy(w2_e[u][:], down))
                    split(w1_hi[u][:], w1_lo[u][:], whole, s["w_split"])

            expert_pair(0)
            with pool.Fori(1, X // 2) as i:
                chain.enter(i, 1, 4)
                expert_pair(i)
            chain.leave(X // 2 - 1)

            for u in range(2):
                pool.wait_ge(s[f"yg_out{u}"], 16 * X * GPX // 2)

            def token_pair(i):
                for u in range(2):
                    t = 2 * i + u
                    pool.wait_ge(s["idx_set"], t + 1)
                    alone(pool)
                    for b in range(GB):
                        for j in range(2):
                            pool.indirect_dma_start(
                                out=yb[u][:, j, b, :], out_offset=None, in_=ys_d,
                                in_offset=bass.IndirectOffsetOnAxis(ap=idx[u][:, j * GB + b:j * GB + b + 1], axis=0),
                                ).then_inc(s[f"y_back{u}"], 16)
                    pool.wait_ge(s["r3_var"], t + 1)
                    rsqrt(rs3[:], mv3[:, :, 1], lne3[:]).then_inc(s["r3_rstd"], 1)

            token_pair(0)
            with pool.Fori(1, NG // 2) as i:
                chain.enter(i, 1, 2)
                token_pair(i)
            chain.leave(NG // 2 - 1)

        @block.scalar
        def _(act):
            def copy(dst, src, **kw):
                return nc.scalar.activation(dst, src, ACT.Copy, **kw)

            act.wait_ge(s["setup_T"], 1)
            copy(wqT_a[:], ps_s[:, 0, 0:128])
            copy(wkT_a[:], ps_s[:, 0, 128:256])
            copy(wgT[:], ps_s[:, 0, 256:256 + X]).then_inc(s["setup_Ts"], 1)
            act.wait_ge(s["setup_T"], 2)
            copy(wqT[:].rearrange("p j d -> p (j d)"), ps_0[:].rearrange("p b n -> p (b n)")).then_inc(s["setup_Ts"], 1)
            act.wait_ge(s["setup_T"], 3)
            copy(wkT[:].rearrange("p (b j) c -> p b j c", b=2), heads4(ps_1, 128, CA)).then_inc(s["setup_Ts"], 1)

            def self_xT(g):
                act.wait_ge(s["xT_done"], g + 1)
                copy(xT[:].rearrange("p b t -> p (b t)"), ps_t[:, 0, :]).then_inc(s["xT_kept"], 1)

            def self_AV(g):
                act.wait_ge(s["sA_done"], g + 1)
                copy(sA[:].rearrange("p b t -> p (b t)"), ps_t[:, 0, :]).then_inc(s["sA_kept"], 1)
                act.wait_ge(s["sV_done"], g + 1)
                copy(sV[:].rearrange("p b t -> p (b t)"), ps_t[:, 1, :]).then_inc(s["sV_kept"], 1)

            def self_exp(g):
                act.wait_ge(s["sS_masked"], g + 1)
                for b in range(GB):
                    last = nc.scalar.activation(sP[:, b, :], sS[:, b, :], ACT.Exp, bias=s_nmax[:, b:b + 1],
                                                accum_out=s_sum[:, b:b + 1])
                last.then_inc(s["sP_done"], 1)

            def self_PT(g):
                act.wait_ge(s["sPT_done"], g + 1)
                copy(sPT[:].rearrange("p b t -> p (b t)"), ps_t[:, 1, :]).then_inc(s["sPT_kept"], 1)

            def turn_x1(g):
                act.wait_ge(s["x1T_done"], g + 1)
                copy(x1T[:].rearrange("p b t -> p (b t)"), ps_t[:, 0, :]).then_inc(s["x1T_kept"], 1)

            def turn_ctx(g):
                act.wait_ge(s["ctxT_done"], g + 1)
                copy(ctxT[:].rearrange("p b j -> p (b j)"), ps_t[:CA, 0, 0:GB * KEYS]).then_inc(s["ctxT_kept"], 1)

            def keep_A(n, par, half):
                act.wait_ge(s["a_done"], n * 2 + (half + 1))
                nc.scalar.activation(A[par][:, HH * half:HH * (half + 1), :].rearrange("p h t -> p (h t)"),
                                     ps_0[:CA].rearrange("p b n -> p (b n)"), ACT.Identity,
                                     bias=row_bias[:, 0:1]).then_inc(s["a_kept"], 1)

            self_xT(0)
            self_AV(0)
            turn_ctx(0)
            self_exp(0)
            self_PT(0)
            turn_x1(0)
            keep_A(0, 0, 0)
            keep_A(0, 0, 1)

            def exp_half(cnt, k, half):
                act.wait_ge(s["shifted_done"], cnt + (half + 1))
                nc.scalar.activation(P[k % 2][:, HH * half:HH * (half + 1), :].rearrange("p h j -> p (h j)"),
                                     shifted[half][:].rearrange("p b h j -> p (b h j)"), ACT.Exp,
                                     scale=(rn1[:, 0, k:k + 1])).then_inc(s["probs_done"], 1)

            def keep_PT(cnt, half):
                act.wait_ge(s["PT_done"], cnt + (half - 1))
                copy(PT[:].rearrange("p h t -> p (h t)"), ps_t[:KEYS].rearrange("p b n -> p (b n)")).then_inc(s["PT_kept"], 1)

            def group(g):
                for k in range(GB):
                    c, p, q, n = live(g, k)
                    cnt = 2 * GB * g + 2 * k
                    if k == 0 and c:
                        act.wait_ge(s["x1_rstd"], g + 1)
                        if p:
                            act.wait_ge(s["probs_done"], cnt)
                        copy(rn1[:, 0, :], rn1[:, 1, :]).then_inc(s["act_chain"], 1)
                        act.wait_ge(s["act_chain"], g + 1)
                    if c:
                        act.wait_ge(s["v_done"], GB * g + (k + 1))
                        copy(V[k % 2][:, :, 0:E], ps_1[:KEYS].rearrange("p b (h e) -> p (b h) e", e=E)).then_inc(s["v_kept"], 1)
                    if p:
                        keep_PT(cnt, 0)
                    if c:
                        exp_half(cnt, k, 0)
                    if n:
                        keep_A(GB * g + (k + 1), (k + 1) % 2, 0)
                    if k == 0 and more(g):
                        self_xT(g + 1)
                    if k == 1 and more(g):
                        self_exp(g + 1)
                    if k == 2 and routes(g):
                        act.wait_ge(s["x2T_done"], g)
                        copy(x2T[:].rearrange("p b t -> p (b t)"), ps_t[:, 1, :]).then_inc(s["x2T_kept"], 1)
                    if k == 3 and routes(g):
                        act.wait_ge(s["dlt_done"], g)
                        nc.scalar.activation(ex[:], dlt[:], ACT.Exp).then_inc(s["ex_done"], 1)
                    if p:
                        keep_PT(cnt, 1)
                    if n:
                        keep_A(GB * g + (k + 1), (k + 1) % 2, 1)
                    if k == 0 and more(g):
                        self_AV(g + 1)
                    if k == 1 and more(g):
                        self_PT(g + 1)
                    if k == 2 and more(g):
                        turn_x1(g + 1)
                    if k == 3 and more(g):
                        turn_ctx(g + 1)
                    if p:
                        act.wait_ge(s["OT_done"], GB * g + k)
                        copy(OT[:].rearrange("p j t -> p (j t)"), ps_1[:].rearrange("p b n -> p (b n)")).then_inc(s["OT_kept"], 1)
                    if c:
                        exp_half(cnt, k, 1)

            all_groups(act, group)

            def rows_hi(t):
                act.wait_ge(s["xgT_done"], t + 1)
                copy(xgT_hi[:], ps_t[:, 0, :]).then_inc(s["xg_hi_kept"], 1)

            def expert_pair(i):
                for u in range(2 * GPX):
                    t = 2 * GPX * i + u
                    rows_hi(t)
                    act.wait_ge(s["inp_done"], t + 1)
                    if not isinstance(t, int) or t >= 1:
                        act.wait_ge(s["hid_done"], t)
                    nc.scalar.activation(act_u[:], ps_0[:], ACT.Gelu).then_inc(s["gelu_done"], 1)
                    if not isinstance(t, int) or t >= 1:
                        keep_y(t - 1, (u - 1) % 2)

            def keep_y(t, par):
                act.wait_ge(s["y_done"], t + 1)
                if not isinstance(t, int) or t >= 2:
                    act.wait_ge(s[f"yg_out{par}"], store_count(t - 2, par))
                copy(yg[par][:].rearrange("p r d -> p (r d)"), ps_s[:, 0, :]).then_inc(s["y_kept"], 1)

            def store_count(t, par):
                return t * 8 + (16 - 8 * par)

            expert_pair(0)
            with act.Fori(1, X // 2) as i:
                expert_pair(i)
            keep_y(X * GPX - 1, 1)

        @block.vector
        def _(dve):
            chain = Chain(dve, s["dve_chain"])
            v = nc.vector

            dve.wait_ge(s["mask_in"], 16)
            chain.link(v.tensor_copy(mask_f[:], mask_u8[:]))
            v.tensor_scalar(mask_f[:], mask_f[:], 1.0, -MASKED, ALU.subtract, ALU.mult).then_inc(s["setup_mask"], 1)
            dve.wait_ge(s["setup_qk"], 1)
            v.tensor_scalar(wqk[:], ps_s[:, 1, 0:D], float(D) ** -0.5, None, ALU.mult).then_inc(s["setup_done"], 1)
            dve.wait_ge(s["setup_T"], 4)
            chain.link(v.tensor_copy(maskT[:], ps_s[:S2, 1, 128:128 + B]))

            def mask_col(g):
                src = maskT[:, GB * g:GB * (g + 1)] if isinstance(g, int) else maskT[:, bass.ds(g * GB, GB)]
                v.tensor_scalar(ctx_rows[0:S2, :, MASK_ROW], src, 1.0, None, ALU.mult).then_inc(s["mask_col"], 1)

            dve.wait_ge(s["zero_set"], 1)
            mask_col(0)
            dve.wait_ge(s["small_in"], 16 * 5)
            dve.wait_ge(s["weights_in"], 16 * 9)
            for half in range(2):
                dve.wait_ge(s["setup_G"], half + 1)
                ps = ps_0 if half == 0 else ps_1
                whole = zeros[:, 0:HH * CA].rearrange("p (i b c) -> p b i c", b=2, c=CA)
                if half == 0:
                    dve.wait_ge(s["xs_zeroed"], 16 * (SLOTS // 2048))
                chain.link(v.tensor_scalar(whole, heads4(ps, D, CA), g_col[:, 0:1], float(E) ** -0.5, ALU.mult, ALU.mult))
                flat = zeros[:, 0:HH * CA]
                hi = G_hi[:, HH * half:HH * (half + 1), :].rearrange("p h c -> p (h c)")
                lo = G_lo[:, HH * half:HH * (half + 1), :].rearrange("p h c -> p (h c)")
                chain.link(v.tensor_copy(hi, flat))
                chain.link(v.tensor_tensor(lo, flat, hi.bitcast(F32), ALU.subtract))
            chain.link(v.tensor_copy(wv_hi[:], wv_aug[:]))
            v.tensor_tensor(wv_lo[:], wv_aug[:], wv_hi[:].bitcast(F32), ALU.subtract).then_inc(s["setup_Gs"], 1)

            def self_mask(g):
                dve.wait_ge(s["sS_done"], g + 1)
                chain.link(v.tensor_tensor(sS[:], ps_t[:, 0, :].rearrange("p (b t) -> p b t", b=GB),
                                           causal[:].unsqueeze(1).broadcast_to([T, GB, T]), ALU.add))
                v.tensor_reduce(s_nmax[:], sS[:], AX_X, ALU.max, negate=True).then_inc(s["sS_masked"], 1)

            def self_residual(g):
                dve.wait_ge(s["sPV_done"], g + 1)
                dve.wait_ge(s["x_in"], g * 16 + 16)
                chain.link(v.reciprocal(s_rec[:], s_sum[:]))
                for b in range(GB):
                    last = v.scalar_tensor_tensor(r1[:, b, :], ps_t[:, 0, T * b:T * (b + 1)], s_rec[:, b:b + 1],
                                                  x_raw[:, b, :], ALU.mult, ALU.add)
                last.then_inc(s["r1_done"], 1)
                dve.wait_ge(s["r1_done"], g + 1)
                for b in range(GB):
                    last = v.bn_stats(st6[:, b, :], r1[:, b, :])
                chain.link(last)
                alone(dve)
                for b in range(GB):
                    last = v.bn_aggr(mv1[:, b, :], st6[:, b, :])
                last.then_inc(s["r1_var"], 1)

            def self_apply(g):
                dve.wait_ge(s["x1_rstd"], g + 1)
                for b in range(GB):
                    last = v.tensor_scalar(x1[:, b, :], r1[:, b, :], mv1[:, b, 0:1], rs1[:, b:b + 1],
                                           ALU.subtract, ALU.mult)
                last.then_inc(s["x1_done"], 1)

            self_mask(0)
            self_residual(0)
            self_apply(0)

            def shift(c, cnt, half, p):
                dve.wait_ge(s["scores_done"], cnt + (half + 1))
                scores = heads4(ps_s, T, KEYS)
                chain.link(v.tensor_reduce(top[:], scores, AX_X, ALU.max))
                if p:
                    dve.wait_ge(s["probs_done"], cnt + (half - 1))
                v.tensor_tensor(shifted[half][:], scores, top[:].unsqueeze(3).broadcast_to([T, 2, HB, KEYS]),
                                ALU.subtract).then_inc(s["shifted_done"], 1)

            def scale_heads(cnt, half):
                dve.wait_ge(s["pv_done"], cnt + (half - 1))
                heads = heads4(ps_1, T, E + 1)
                chain.link(v.reciprocal(rec[:], heads[:, :, :, E]))
                dst = O[:, HH * half:HH * (half + 1), :].rearrange("p (b h) e -> p b h e", b=2)
                v.tensor_tensor(dst, heads[:, :, :, 0:E], rec[:].unsqueeze(3).broadcast_to([T, 2, HB, E]),
                                ALU.mult).then_inc(s["heads_scaled"], 1)

            def route_top2(g):
                dve.wait_ge(s["logits_done"], g)
                L = ps_t[:, 1, 0:GB * X].rearrange("p (b e) -> p b e", b=GB)
                revs = rev[:].unsqueeze(1).broadcast_to([T, GB, X])
                for j in range(2):
                    src = L if j == 0 else L2[:]
                    chain.link(v.tensor_reduce(m12[:, j, :], src, AX_X, ALU.max))
                    chain.link(v.tensor_tensor(eq[:], src, m12[:, j, :].unsqueeze(2).broadcast_to([T, GB, X]), ALU.is_equal))
                    chain.link(v.tensor_tensor(eq[:], eq[:], revs, ALU.mult))
                    chain.link(v.tensor_reduce(r12[:, j, :], eq[:], AX_X, ALU.max))
                    chain.link(v.tensor_tensor(oh[:, j], r12[:, j, :].unsqueeze(2).broadcast_to([T, GB, X]), revs, ALU.is_equal))
                    if j == 0:
                        v.scalar_tensor_tensor(L2[:], oh[:, 0], MASKED, L, ALU.mult, ALU.add).then_inc(s["logits_read"], 1)
                        dve.wait_ge(s["logits_read"], g)
                v.tensor_tensor(picked[:], oh[:, 0], oh[:, 1], ALU.add).then_inc(s["picked_done"], 1)
                v.tensor_tensor(dlt[:], m12[:, 1, :], m12[:, 0, :], ALU.subtract).then_inc(s["dlt_done"], 1)

            def route_ranks(g):
                dve.wait_ge(s["rank_done"], g)
                ranks = ps_t[:, 1, 0:(GB + 1) * X].rearrange("p (b e) -> p b e", e=X)
                chain.link(v.tensor_tensor(pos[:], ranks[:, 0:GB, :], taken[:].unsqueeze(1).broadcast_to([T, GB, X]), ALU.add))
                v.tensor_tensor(taken[:], taken[:], ranks[:, GB, :], ALU.add).then_inc(s["rank_read"], 1)

            def route_slots(g):
                dve.wait_ge(s["ex_done"], g)
                dve.wait_ge(s["rank_read"], g)
                chain.link(v.tensor_scalar(gate[:, 0, :], ex[:], 1.0, None, ALU.add))
                chain.link(v.tensor_tensor(at[:], oh[:], pos[:].unsqueeze(1).broadcast_to([T, 2, GB, X]), ALU.mult))
                chain.link(v.reciprocal(gate[:, 0, :], gate[:, 0, :]))
                chain.link(v.tensor_reduce(place[:], at[:], AX_X, ALU.add))
                chain.link(v.tensor_tensor(gate[:, 1, :], ex[:], gate[:, 0, :], ALU.mult))
                v.tensor_scalar(first[:], r12[:], -float(CAP), float(X * CAP), ALU.mult, ALU.add)
                chain.link(v.tensor_scalar(over[:], place[:], float(CAP), None, ALU.is_ge))
                chain.link(v.tensor_tensor(slot_f[:], first[:], place[:], ALU.add))
                v.scalar_tensor_tensor(slot[:], over[:], SKIP, slot_f[:], ALU.mult, ALU.add).then_inc(s["slots_done"], 1)
                dst = (lambda t: t[:, g - 1, :].rearrange("p (j b) -> p j b", j=2)) if isinstance(g, int) else \
                    (lambda t: t[:, bass.ds(g - 1, 1), :].rearrange("p o (j b) -> p (o j) b", j=2))
                chain.link(v.scalar_tensor_tensor(dst(back_all), place[:], float(CAP - 1), first[:], ALU.min, ALU.add))
                chain.link(v.tensor_scalar(over[:], over[:], -1.0, 1.0, ALU.mult, ALU.add))
                chain.link(v.tensor_tensor(dst(gate_all), over[:], gate[:], ALU.mult))

            def group(g):
                for k in range(GB):
                    c, p, q, n = live(g, k)
                    cnt = 2 * GB * g + 2 * k
                    if c:
                        shift(c, cnt, 0, p)
                    if k == 3 and routes(g):
                        route_top2(g)
                    if q:
                        dve.wait_ge(s["wout_done"], GB * g + (k - 1))
                        chain.link(v.bn_stats(st_o[:], ps_0[:, 0, 0:D]))
                        alone(dve)
                        v.bn_aggr(mv_o[:], st_o[:]).then_inc(s["out_var"], 1)
                        dve.wait_ge(s["out_var"], GB * g + (k - 1))
                        v.scalar_tensor_tensor(centred[:], ps_0[:, 0, 0:D], mv_o[:, 0:1], g_out_bc[:], ALU.subtract,
                                               ALU.mult).then_inc(s["out_centred"], 1)
                    if p:
                        scale_heads(cnt, 0)
                    if q:
                        dve.wait_ge(s["out_rstd"], GB * g + (k - 1))
                        dve.wait_ge(s["out_centred"], GB * g + (k - 1))
                        if k == 3:
                            dve.wait_ge(s["x1_saved"], g + 1)
                        res = x1[:, 0, :] if k == 2 else x1_of(g, k)
                        j = (k + 2) % GB
                        v.scalar_tensor_tensor(r2[:, j, :], centred[:], rs_o[:, 0:1], res, ALU.mult,
                                               ALU.add).then_inc(s["r2_done"], 1)
                        dve.wait_ge(s["r2_done"], GB * g + (k - 1))
                        chain.link(v.bn_stats(st_o[:], r2[:, j, :]))
                        alone(dve)
                        last = v.bn_aggr(mv2[:, j, :], st_o[:])
                        if k == 1:
                            last.then_inc(s["r2_var"], 1)
                        else:
                            chain.link(last)
                    if k == 1 and more(g):
                        self_mask(g + 1)
                    if k == 2 and more(g):
                        self_residual(g + 1)
                    if k == 3 and routes(g):
                        route_ranks(g)
                    if c:
                        shift(c, cnt, 1, p)
                    if p:
                        scale_heads(cnt, 1)
                    if k == 0 and more(g):
                        dve.wait_ge(s["ctxT_done"], g + 1)
                        mask_col(g + 1)
                    if k == 1 and routes(g):
                        dve.wait_ge(s["x2_rstd"], g)
                        if not isinstance(g, int) or g >= 2:
                            dve.wait_ge(s["scattered"], g * (32 * GB) - 32 * GB)
                            dve.wait_ge(s["x2_saved"], g * 16 - 16)
                        for b in range(GB):
                            last = v.tensor_scalar(x2[:, b, :], r2[:, b, :], mv2[:, b, 0:1], rs2[:, b:b + 1],
                                                   ALU.subtract, ALU.mult)
                        last.then_inc(s["x2_done"], 1)
                    if k == 2 and more(g):
                        dve.wait_ge(s["x1_saved"], g + 1)
                        self_apply(g + 1)
                    if k == 3 and routes(g):
                        route_slots(g)

            def x1_of(g, k):
                return x1_late[:, {3: 0, 0: 1, 1: 2}[k], :]

            all_groups(dve, group, chain, DVE_LINKS)

            def rows_lo(t):
                dve.wait_ge(s["xg_hi_kept"], t + 1)
                v.tensor_tensor(xgT_lo[:], ps_t[:, 0, :], xgT_hi[:].bitcast(F32), ALU.subtract).then_inc(s["xg_lo_kept"], 1)

            def expert_pair(i):
                for u in range(2 * GPX):
                    t = 2 * GPX * i + u
                    rows_lo(t)
                    dve.wait_ge(s["gates_done"], t + 1)
                    dve.wait_ge(s["gelu_done"], t + 1)
                    v.tensor_tensor(hid[u % 2][:], act_u[:], ps_1[:], ALU.mult).then_inc(s["hid_done"], 1)

            expert_pair(0)
            with dve.Fori(1, X // 2) as i:
                expert_pair(i)

            def set_idx(t, u):
                src = (lambda a: a[:, t, :]) if isinstance(t, int) else (lambda a: a[:, bass.ds(t, 1), :].rearrange("p o n -> p (o n)"))
                if not isinstance(t, int) or t >= 2:
                    dve.wait_ge(s[f"y_back{u}"], back_count(t - 2, u))
                v.tensor_scalar(idx[u][:], src(back_all), 1.0, None, ALU.mult).then_inc(s["idx_set"], 1)

            def back_count(t, u):
                return t * (8 * GB * 2) + (16 * 2 * GB - 8 * GB * 2 * u)

            set_idx(0, 0)

            def token_pair(i):
                for u in range(2):
                    t = 2 * i + u
                    if not (isinstance(t, int) and t + 1 >= NG):
                        set_idx(t + 1, (u + 1) % 2)
                    gates = gate_all[:, t, :] if isinstance(t, int) else gate_all[:, bass.ds(t, 1), :].rearrange("p o n -> p (o n)")
                    chain.link(v.tensor_scalar(gate_t[:], gates, 1.0, None, ALU.mult))
                    dve.wait_ge(s[f"y_back{u}"], back_count(t, u))
                    dve.wait_ge(s[f"x2_back{u}"], t * 8 + (16 - 8 * u))
                    for j in range(2):
                        for b in range(GB):
                            last = v.scalar_tensor_tensor(r3[:, b, :], yb[u][:, j, b, :], gate_t[:, j * GB + b:j * GB + b + 1],
                                                          (x2b[u] if j == 0 else r3)[:, b, :], ALU.mult, ALU.add)
                        chain.link(last)
                    for b in range(GB):
                        last = v.bn_stats(st6[:, b, :], r3[:, b, :])
                    chain.link(last)
                    alone(dve)
                    for b in range(GB):
                        last = v.bn_aggr(mv3[:, b, :], st6[:, b, :])
                    last.then_inc(s["r3_var"], 1)
                    dve.wait_ge(s["r3_rstd"], t + 1)
                    if not isinstance(t, int) or t >= 2:
                        dve.wait_ge(s[f"out_saved{u}"], (t - 2) * 8 + (16 - 8 * u))
                    for b in range(GB):
                        last = v.tensor_scalar(final[u][:, b, :], r3[:, b, :], mv3[:, b, 0:1], rs3[:, b:b + 1],
                                               ALU.subtract, ALU.mult)
                    last.then_inc(s["out_ready"], 1)

            token_pair(0)
            with dve.Fori(1, NG // 2 - 1) as i:
                chain.enter(i, 1, 8)
                token_pair(i)
            chain.leave(NG // 2 - 2)
            token_pair(NG // 2 - 1)

        @block.tensor
        def _(pe):
            mm = nc.tensor.matmul

            def turn(dst, src):
                rows = src.shape[0]
                return nc.tensor.transpose(dst, src, ident[:rows, :rows])

            def mm3(dst, a, b):
                mm(dst, a[0], b[0], start=True, stop=False)
                mm(dst, a[1], b[0], start=False, stop=False)
                return mm(dst, a[0], b[1], start=False, stop=True)

            pe.wait_ge(s["consts"], 1)
            pe.wait_ge(s["weights_in"], 16 * 9)
            pe.wait_ge(s["small_in"], 16 * 5)
            turn(ps_s[:, 0, 0:128], wq_a[:])
            turn(ps_s[:, 0, 128:256], wk_a[:])
            turn(ps_s[:, 0, 256:256 + X], wg_sb[:]).then_inc(s["setup_T"], 1)
            for j in range(8):
                last = turn(ps_0[:, j // 4, 128 * (j % 4):128 * (j % 4 + 1)], wq_sb[:, 128 * j:128 * (j + 1)])
            last.then_inc(s["setup_T"], 1)
            for j in range(8):
                last = turn(ps_1[:, j // 4, CA * (j % 4):CA * (j % 4 + 1)], wk_aug[:, 128 * j:128 * (j + 1)])
            last.then_inc(s["setup_T"], 1)
            pe.wait_ge(s["setup_Ts"], 1)
            mm(ps_s[:, 1, 0:D], wqT_a[:], wkT_a[:], start=True, stop=True).then_inc(s["setup_qk"], 1)
            pe.wait_ge(s["setup_done"], 1)
            pe.wait_ge(s["setup_mask"], 1)
            turn(ps_s[:S2, 1, 128:128 + B], mask_f[:]).then_inc(s["setup_T"], 1)
            pe.wait_ge(s["setup_Ts"], 3)
            for half in range(2):
                ps = ps_0 if half == 0 else ps_1
                for i in range(HB):
                    for b in range(2):
                        h = HH * half + 2 * i + b
                        last = mm(ps[:, b, CA * i:CA * (i + 1)], wqT[E * b:E * (b + 1), h // 2, :],
                                  wkT[E * b:E * (b + 1), h // 2, :], start=True, stop=True)
                last.then_inc(s["setup_G"], 1)

            def self_xT(g):
                pe.wait_ge(s["x_in"], g * 16 + 16)
                for b in range(GB):
                    last = turn(ps_t[:, 0, T * b:T * (b + 1)], x_raw[:, b, :])
                last.then_inc(s["xT_done"], 1)

            def self_AV(g):
                pe.wait_ge(s["xT_kept"], g + 1)
                mm(ps_t[:, 0, :], wqk[:], xT[:].rearrange("p b t -> p (b t)"), start=True, stop=True).then_inc(s["sA_done"], 1)
                for b in range(GB):
                    last = mm(ps_t[:, 1, T * b:T * (b + 1)], xT[:, b, :], wv_self[:], start=True, stop=True)
                last.then_inc(s["sV_done"], 1)

            def self_S(g):
                pe.wait_ge(s["sA_kept"], g + 1)
                for b in range(GB):
                    last = mm(ps_t[:, 0, T * b:T * (b + 1)], sA[:, b, :], xT[:, b, :], start=True, stop=True)
                last.then_inc(s["sS_done"], 1)

            def self_PT(g):
                pe.wait_ge(s["sP_done"], g + 1)
                for b in range(GB):
                    last = turn(ps_t[:, 1, T * b:T * (b + 1)], sP[:, b, :])
                last.then_inc(s["sPT_done"], 1)

            def self_PV(g):
                pe.wait_ge(s["sPT_kept"], g + 1)
                pe.wait_ge(s["sV_kept"], g + 1)
                for b in range(GB):
                    last = mm(ps_t[:, 0, T * b:T * (b + 1)], sPT[:, b, :], sV[:, b, :], start=True, stop=True)
                last.then_inc(s["sPV_done"], 1)

            def turn_x1(g):
                pe.wait_ge(s["x1_done"], g + 1)
                for b in range(GB):
                    last = turn(ps_t[:, 0, T * b:T * (b + 1)], x1[:, b, :])
                last.then_inc(s["x1T_done"], 1)

            def turn_ctx(g):
                pe.wait_ge(s["ctx_in"], g * 16 + 16)
                pe.wait_ge(s["mask_col"], g + 1)
                for b in range(GB):
                    last = turn(ps_t[:CA, 0, KEYS * b:KEYS * (b + 1)], ctx_rows[:, b, :])
                last.then_inc(s["ctxT_done"], 1)

            def project(n, k, half):
                for i in range(HH):
                    h = HH * half + i
                    last = mm3(ps_0[:CA, i // HB, T * (i % HB):T * (i % HB + 1)], (G_hi[:, h, :], G_lo[:, h, :]),
                               (x1T_hi[:, k, :], x1T_lo[:, k, :]))
                last.then_inc(s["a_done"], 1)

            self_xT(0)
            self_AV(0)
            pe.wait_ge(s["sA_kept"], 1)
            pe.wait_ge(s["sV_kept"], 1)
            turn_ctx(0)
            pe.wait_ge(s["ctxT_kept"], 1)
            self_S(0)
            self_PT(0)
            pe.wait_ge(s["sS_masked"], 1)
            self_PV(0)
            pe.wait_ge(s["r1_done"], 1)
            turn_x1(0)
            pe.wait_ge(s["x1T_split"], 1)
            pe.wait_ge(s["setup_Gs"], 1)
            project(0, 0, 0)
            pe.wait_ge(s["a_kept"], 1)
            project(0, 0, 1)

            def scores(k, half):
                for i in range(HH):
                    h = HH * half + i
                    last = mm(ps_s[:, i // HB, KEYS * (i % HB):KEYS * (i % HB + 1)], A[k % 2][:, h, :], ctxT[:, k, :],
                              start=True, stop=True)
                last.then_inc(s["scores_done"], 1)

            def turn_probs(k, half):
                for i in range(HH):
                    last = turn(ps_t[:KEYS, i // HB, T * (i % HB):T * (i % HB + 1)], P[k % 2][:, HH * half + i, :])
                last.then_inc(s["PT_done"], 1)

            def weigh(k, half):
                for i in range(HH):
                    last = mm(ps_1[:, i // HB, (E + 1) * (i % HB):(E + 1) * (i % HB + 1)], PT[:, i, :],
                              V[k % 2][:, HH * half + i, :], start=True, stop=True)
                last.then_inc(s["pv_done"], 1)

            def group(g):
                for k in range(GB):
                    c, p, q, n = live(g, k)
                    cnt = 2 * GB * g + 2 * k
                    done = GB * g + k
                    if c:
                        pe.wait_ge(s["a_kept"], cnt + 2)
                        if k == 0:
                            pe.wait_ge(s["ctxT_split"], g + 1)
                        wait(pe, s["shifted_done"], cnt)
                        scores(k, 0)
                    if q:
                        pe.wait_ge(s["OT_kept"], done - 1)
                        for j in range(8):
                            last = mm(ps_0[:, 0, 0:D], OT[:, j, :], wout_sb[:, j, :], start=(j == 0), stop=(j == 7))
                        last.then_inc(s["wout_done"], 1)
                    if c:
                        if p:
                            wait(pe, s["OT_kept"], done - 1)
                        for j in range(2):
                            last = mm3(ps_1[:KEYS, j, :], (ctxT_hi[:, k, :], ctxT_lo[:, k, :]),
                                       (wv_hi[:, BANK * j:BANK * (j + 1)], wv_lo[:, BANK * j:BANK * (j + 1)]))
                        last.then_inc(s["v_done"], 1)
                    if k == 0:
                        pe.wait_ge(s["ctxT_kept"], g + 1) if more(g - 1) else None
                        if routes(g - 1):
                            pe.wait_ge(s["rank_read"], g - 1)
                    if k == 1 and more(g):
                        pe.wait_ge(s["sA_kept"], g + 2)
                        pe.wait_ge(s["sV_kept"], g + 2)
                    if k == 2 and more(g):
                        pe.wait_ge(s["sPT_kept"], g + 2)
                    if k == 3:
                        if more(g):
                            pe.wait_ge(s["x1T_kept"], g + 2)
                        if routes(g):
                            pe.wait_ge(s["logits_read"], g)
                    if p:
                        pe.wait_ge(s["probs_done"], cnt - 1)
                        turn_probs(k + 1, 0)
                    if n:
                        if q:
                            pe.wait_ge(s["out_centred"], done - 1)
                        pe.wait_ge(s["a_kept"], cnt + 2)
                        if k == 3:
                            pe.wait_ge(s["x1T_split"], g + 2)
                        project(done + 1, (k + 1) % GB, 0)
                    if p:
                        if c:
                            pe.wait_ge(s["v_kept"], done + 1)
                        pe.wait_ge(s["PT_kept"], cnt - 1)
                        if not c:
                            pe.wait_ge(s["OT_kept"], done - 1)
                        weigh(k + 1, 0)
                    if k == 0 and more(g):
                        self_xT(g + 1)
                    if k == 1 and more(g):
                        self_S(g + 1)
                    if k == 2:
                        if more(g):
                            self_PV(g + 1)
                        if routes(g):
                            pe.wait_ge(s["x2_done"], g)
                            for b in range(GB):
                                last = turn(ps_t[:, 1, T * b:T * (b + 1)], x2[:, b, :])
                            last.then_inc(s["x2T_done"], 1)
                    if k == 3 and routes(g):
                        pe.wait_ge(s["picked_done"], g)
                        ranks = ps_t[:, 1, 0:(GB + 1) * X]
                        for b in range(GB + 1):
                            for a in range(min(b + 1, GB)):
                                last = mm(ranks[:, X * b:X * (b + 1)], (before if a == b else ones_b)[:], picked[:, a, :],
                                          start=(a == 0), stop=(a == min(b, GB - 1)))
                        last.then_inc(s["rank_done"], 1)
                    if c:
                        pe.wait_ge(s["shifted_done"], cnt + 1)
                        scores(k, 1)
                    if k == 0 and more(g):
                        pe.wait_ge(s["xT_kept"], g + 2)
                    if k == 1 and more(g):
                        pe.wait_ge(s["sS_masked"], g + 2)
                    if k == 2:
                        if more(g):
                            pe.wait_ge(s["r1_done"], g + 2)
                        if routes(g):
                            pe.wait_ge(s["x2T_kept"], g)
                    if k == 3 and routes(g):
                        pe.wait_ge(s["rank_read"], g)
                    if p:
                        pe.wait_ge(s["probs_done"], cnt)
                        turn_probs(k + 1, 1)
                    if n:
                        pe.wait_ge(s["a_kept"], cnt + 3)
                        project(done + 1, (k + 1) % GB, 1)
                    if p:
                        pe.wait_ge(s["PT_kept"], cnt)
                        pe.wait_ge(s["heads_scaled"], cnt - 1)
                        weigh(k + 1, 1)
                    if k == 0 and more(g):
                        self_AV(g + 1)
                    if k == 1 and more(g):
                        self_PT(g + 1)
                    if k == 2:
                        if more(g):
                            turn_x1(g + 1)
                        if routes(g):
                            for b in range(GB):
                                last = mm(ps_t[:, 1, X * b:X * (b + 1)], x2T[:, b, :], wgT[:], start=True, stop=True)
                            last.then_inc(s["logits_done"], 1)
                    if k == 3 and more(g):
                        turn_ctx(g + 1)
                    if p:
                        pe.wait_ge(s["heads_scaled"], cnt)
                        for j in range(8):
                            last = turn(ps_1[:, j // 4, 128 * (j % 4):128 * (j % 4 + 1)],
                                        O[:, 2 * j:2 * j + 2, :].rearrange("p h e -> p (h e)"))
                        last.then_inc(s["OT_done"], 1)

            all_groups(pe, group)

            def turn_rows(t, u):
                pe.wait_ge(s[f"xg_in{u % 2}"], t * 8 + (16 - 8 * (u % 2)))
                if not isinstance(t, int) or t >= 1:
                    pe.wait_ge(s["xg_lo_kept"], t)
                for r in range(4):
                    last = turn(ps_t[:, 0, 128 * r:128 * (r + 1)], xg[u % 2][:, r, :])
                last.then_inc(s["xgT_done"], 1)

            def up(t, u):
                e = u // GPX
                pe.wait_ge(s["xg_lo_kept"], t + 1)
                if not isinstance(t, int) or t >= 1:
                    pe.wait_ge(s["hid_done"], t)
                for b in range(4):
                    ps = ps_0 if b < 2 else ps_1
                    last = mm3(ps[:, b % 2, :], (w1_hi[e][:, 128 * b:128 * (b + 1)], w1_lo[e][:, 128 * b:128 * (b + 1)]),
                               (xgT_hi[:], xgT_lo[:]))
                    if b == 1:
                        last.then_inc(s["inp_done"], 1)
                last.then_inc(s["gates_done"], 1)

            def down(t, u):
                e = u // GPX
                pe.wait_ge(s["hid_done"], t + 1)
                if not isinstance(t, int) or t >= 1:
                    pe.wait_ge(s["y_kept"], t)
                for r in range(4):
                    for j in range(2):
                        last = mm(ps_s[:, 0, D * r:D * (r + 1)], hid[u % 2][:, j, 128 * r:128 * (r + 1)], w2_e[e][:, j, :],
                                  start=(j == 0), stop=(j == 1))
                last.then_inc(s["y_done"], 1)

            def expert_pair(i):
                for u in range(2 * GPX):
                    t = 2 * GPX * i + u
                    turn_rows(t, u)
                    if u % GPX == 0:
                        pe.wait_ge(s["w_split"], 2 * i + (u // GPX + 1))
                    up(t, u)
                    if not isinstance(t, int) or t >= 1:
                        down(t - 1, (u - 1) % (2 * GPX))

            expert_pair(0)
            with pe.Fori(1, X // 2) as i:
                expert_pair(i)
            down(X * GPX - 1, 2 * GPX - 1)


POOL_LINKS = 12
DVE_LINKS = 51

_INS = ["x", "ctx_768", "mask_BxS2_bf1", "L0_attn_Wq", "L0_attn_Wk", "L0_attn_Wv", "L0_xattn_g_norm",
        "L0_xattn_null_kv", "L0_xattn_Wq", "L0_xattn_Wkv", "L0_xattn_Wout", "L0_xattn_g_out",
        "L0_ffn_Wg", "L0_ffn_W1", "L0_ffn_W2"]


def kernel(**inputs):
    import numpy as _np
    import concourse.bacc as _bacc
    from concourse import mybir as _mybir
    from concourse.bass_utils import run_bass_kernel_spmd as _run

    nc = _bacc.Bacc("TRN2", target_bir_lowering=False, num_devices=1)
    arrays, args = {}, []
    for name in _INS:
        a = _np.ascontiguousarray(inputs[name])
        arrays[f"in_{name}_dram"] = a
        args.append(nc.dram_tensor(f"in_{name}_dram", a.shape, _mybir.dt.from_np(a.dtype), kind="ExternalInput").ap())
    args.append(nc.dram_tensor("out_0_dram", (B, T, D), F32, kind="ExternalOutput").ap())
    decoder(nc, *args)
    r = _run(nc, [arrays], core_ids=[0])
    return r.results[0]["out_0_dram"]
```

```python
from contextlib import ExitStack

import concourse.bass as bass
from concourse import mybir

F32 = mybir.dt.float32
F32R = mybir.dt.float32r
BF16 = mybir.dt.bfloat16
I32 = mybir.dt.int32
U8 = mybir.dt.uint8
ALU = mybir.AluOpType
ACT = mybir.ActivationFunctionType
AX_X = mybir.AxisListType.X

B, T, D = 64, 128, 128
S2, C = 120, 96
H, E = 16, 64
KEYS = S2 + 1
CA = C + 2
NULL_ROW, MASK_ROW = C, C + 1
GB = 4
NG = B // GB
HH = H // 2
HB = HH // 2
X, K2, FI = 8, 2, 256
TOKENS = B * T
CAP = int(TOKENS * K2 * 1.25 / X)
SLOTS = X * CAP
SG = 512
GPX = CAP // SG
MASKED = -float(2 ** 100)
SKIP = float(2 * SLOTS)
EPS = 1e-5
BANK = 512
assert CAP % SG == 0 and GPX % 2 == 1


class Chain:

    def __init__(self, eng, sem):
        self.eng, self.sem, self.n, self.loop = eng, sem, 0, None

    def enter(self, i, start, per):
        self.loop = (i, start, per, self.n)

    def leave(self, turns):
        i, start, per, n0 = self.loop
        assert self.n - n0 == per, (self.n - n0, per)
        self.n, self.loop = n0 + per * turns, None

    def link(self, ins):
        ins.then_inc(self.sem, 1)
        self.n += 1
        if self.loop is None:
            self.eng.wait_ge(self.sem, self.n)
        else:
            i, start, per, _ = self.loop
            self.eng.wait_ge(self.sem, i * per + (self.n - start * per))


def wait(eng, sem, value):
    if not isinstance(value, int) or value > 0:
        eng.wait_ge(sem, value)


def decoder(nc, x, ctx_in, mask, wq_s, wk_s, wv_s, g_norm, null_kv, wq_c, wkv, wout, g_out, wg, w1, w2, out):
    with ExitStack() as stack:
        def sb(name, shape, dt=F32):
            return stack.enter_context(nc.sbuf_tensor(name, shape, dt))

        def pair(name):
            return stack.enter_context(nc.psum_tensor(name, [128, 2, BANK], F32))

        def sem(name):
            return stack.enter_context(nc.semaphore(name))

        xs_d = nc.dram_tensor("routed_rows", [SLOTS, D], F32, kind="Internal").ap()
        ys_d = nc.dram_tensor("expert_rows", [SLOTS, D], F32, kind="Internal").ap()
        x2_d = nc.dram_tensor("tokens_x2", [TOKENS, D], F32, kind="Internal").ap()

        ps_s, ps_t, ps_v, ps_w = pair("ps_scores"), pair("ps_turned"), pair("ps_values"), pair("ps_work")
        W, F = 0, 1

        ident = sb("ident", [128, 128])
        causal = sb("causal", [T, T])
        before = sb("before", [128, 128], BF16)
        ones_b = sb("ones_b", [128, 128], BF16)
        rev = sb("rev", [128, X])
        neg_half = sb("neg_half", [128, GB])
        zeros = sb("zeros", [128, 2048])
        row_bias = sb("row_bias", [CA, 1])
        wqk = sb("wqk", [D, D])
        wv_self = sb("wv_self", [D, D])
        G_hi, G_lo = sb("G_hi", [D, H, CA], F32R), sb("G_lo", [D, H, CA], F32R)
        wv_aug = sb("wv_aug", [CA, H * E])
        wv_hi, wv_lo = sb("wv_hi", [CA, H * E], F32R), sb("wv_lo", [CA, H * E], F32R)
        wout_sb = sb("wout_sb", [128, H * E // 128, D])
        g_col = sb("g_col", [D, 1])
        g_out_bc = sb("g_out_bc", [T, D])
        wgT = sb("wgT", [D, X])
        mask_u8 = sb("mask_u8", [B, S2], U8)
        mask_f = sb("mask_f", [B, S2])
        maskT = sb("maskT", [S2, B])
        w1_all = sb("w1_all", [D, X, 2 * FI])
        w2_all = sb("w2_all", [128, X, FI // 128, D])
        x_raw = sb("x_raw", [T, GB, D])
        xT = sb("xT", [D, GB, T])
        sA = sb("sA", [D, GB, T])
        sV = sb("sV", [T, GB, D])
        sS = sb("sS", [T, GB, T])
        sP = sb("sP", [T, GB, T])
        sPT = sb("sPT", [T, GB, T])
        s_nmax, s_sum, s_rec = sb("s_nmax", [T, GB]), sb("s_sum", [T, GB]), sb("s_rec", [T, GB])
        r1 = sb("r1", [T, GB, D])
        st6 = sb("st6", [T, GB, 6])
        mv1 = sb("mv1", [T, GB, 2])
        rs1, rn1 = sb("rs1", [T, GB]), sb("rn1", [T, 2, GB])
        lnt = sb("lnt", [T, 3, GB])
        x1, x1_late = sb("x1", [T, GB, D]), sb("x1_late", [T, 3, D])
        x1T_hi, x1T_lo = sb("x1T_hi", [D, GB, T], F32R), sb("x1T_lo", [D, GB, T], F32R)
        rn_late = sb("rn_late", [T, 1])

        ctx_rows = sb("ctx_rows", [KEYS, GB, CA])
        ctxT = sb("ctxT", [CA, GB, KEYS])
        ctxT_hi, ctxT_lo = sb("ctxT_hi", [CA, GB, KEYS], F32R), sb("ctxT_lo", [CA, GB, KEYS], F32R)
        A = sb("A", [128, H, GB, T])
        V = [sb(f"V{i}", [KEYS, H, E]) for i in range(2)]
        top = sb("top", [T, 2, HB])
        shifted = [sb(f"shifted{i}", [T, 2, HB, KEYS]) for i in range(2)]
        P = [sb(f"P{i}", [T, H, KEYS]) for i in range(2)]
        PT = sb("PT", [KEYS, HH, T])
        total = [sb(f"total{i}", [T, HH]) for i in range(2)]
        rec = [sb(f"rec{i}", [T, HH]) for i in range(2)]
        OT = sb("OT", [128, 8, T])
        st_o, mv_o, rs_o, lne_o = sb("st_o", [T, 6]), sb("mv_o", [T, 2]), sb("rs_o", [T, 1]), sb("lne_o", [T, 1])
        centred = sb("centred", [T, D])
        r2, mv2, rs2, lne2 = sb("r2", [T, GB, D]), sb("mv2", [T, GB, 2]), sb("rs2", [T, GB]), sb("lne2", [T, GB])

        x2 = sb("x2", [T, GB, D])
        x2T = sb("x2T", [D, GB, T])
        logits = sb("logits", [T, GB, X])
        m12 = sb("m12", [T, 2, GB])
        eq, L2 = sb("eq", [T, GB, X]), sb("L2", [T, GB, X])
        r12 = sb("r12", [T, 2, GB])
        oh = sb("oh", [T, 2, GB, X])
        picked = sb("picked", [T, GB, X], BF16)
        dlt, ex, gate = sb("dlt", [T, GB]), sb("ex", [T, GB]), sb("gate", [T, 2, GB])
        pos, taken = sb("pos", [T, GB, X]), sb("taken", [T, X])
        at = sb("at", [T, 2, GB, X])
        place, first, over = sb("place", [T, 2, GB]), sb("first", [T, 2, GB]), sb("over", [T, 2, GB])
        slot_f = sb("slot_f", [T, 2, GB])
        slot = sb("slot", [T, 2, GB], I32)
        back_all = sb("back_all", [T, NG, 2 * GB])
        gate_all = sb("gate_all", [T, NG, 2 * GB])

        s = {}
        for name in """self_in cross_in small_in wout_in ffn_in mask_in ident_set zero_set consts setup_T setup_Ts setup_qk setup_G setup_Gs setup_mask setup_done
                       x_in ctx_in xs_zeroed x2_saved scattered
                       scores_done v_done PT_done a_done pv_done wout_done
                       xT_done sA_done sV_done sS_done sPT_done sPV_done x1T_done ctxT_done x2T_done logits_done rank_done
                       shifted_done totals_done out_centred out_var r2_done
                       sS_masked r1_done r1_var x1_done x2_done mask_col picked_done rank_read slots_done dlt_done r2_var
                       probs_done probs_normed v_kept PT_kept a_kept OT_kept
                       xT_kept sA_kept sV_kept sP_done sPT_kept x1T_kept ctxT_kept x2T_kept logits_kept ex_done
                       out_rstd x1_rstd x2_rstd x1_saved x1T_split ctxT_split scatters_sent
                       dve_chain pool_chain act_chain waited""".split():
            s[name] = sem(name)

        with ExitStack() as early:
            def eb(name, shape, dt=F32):
                return early.enter_context(nc.sbuf_tensor(name, shape, dt))

            wq_a, wk_a = eb("wq_a", [D, D]), eb("wk_a", [D, D])
            wqT_a, wkT_a = eb("wqT_a", [D, D]), eb("wkT_a", [D, D])
            wq_sb = eb("wq_sb", [D, H * E])
            wk_aug = eb("wk_aug", [CA, H * E])
            wg_sb = eb("wg_sb", [X, D])
            wqT, wkT = eb("wqT", [128, 8, D]), eb("wkT", [128, 8, CA])

        xgT_hi, xgT_lo = sb("xgT_hi", [D, SG], F32R), sb("xgT_lo", [D, SG], F32R)
        w1_hi = [sb(f"w1_hi{i}", [D, 2 * FI], F32R) for i in range(2)]
        w1_lo = [sb(f"w1_lo{i}", [D, 2 * FI], F32R) for i in range(2)]
        w2_e = [sb(f"w2_e{i}", [128, 2, D]) for i in range(2)]
        act_u = A[:, 0:2].rearrange("p h b t -> p h (b t)")
        hid = [A[:, 2 + 2 * i:4 + 2 * i].rearrange("p h b t -> p h (b t)") for i in range(2)]
        yg = [A[:, 6 + i] for i in range(2)]
        xg = [A[:, 8 + i] for i in range(2)]
        for name in """xg_in0 xg_in1 xgT_done xg_hi_kept xg_lo_kept inp_done gates_done gelu_done hid_done y_done y_kept yg_out0 yg_out1 w_split
                       x2_back0 x2_back1 y_back0 y_back1 idx_set r3_summed r3_var r3_rstd out_ready out_saved0 out_saved1 gathers_sent""".split():
            s[name] = sem(name)
        idx = [sb(f"idx{i}", [T, 2 * GB], I32) for i in range(2)]
        flat_P = [P[i][:].rearrange("p h j -> p (h j)") for i in range(2)]
        yb = [flat_P[i][:, 0:2 * GB * D].rearrange("p (j b d) -> p j b d", j=2, b=GB) for i in range(2)]
        final = [flat_P[i][:, 2 * GB * D:3 * GB * D].rearrange("p (b d) -> p b d", b=GB) for i in range(2)]
        x2b = [shifted[i][:].rearrange("p b h j -> p (b h j)")[:, 0:GB * D].rearrange("p (b d) -> p b d", b=GB) for i in range(2)]
        r3 = sb("r3", [T, GB, D])
        gate_t = sb("gate_t", [T, 2 * GB])
        mv3, rs3, lne3 = sb("mv3", [T, GB, 2]), sb("rs3", [T, GB]), sb("lne3", [T, GB])

        block = stack.enter_context(nc.Block())

        def live(g, k):
            if not isinstance(g, int):
                return True, True, True
            c = GB * g + k
            return c < B, 1 <= c <= B, 2 <= c < B + 2

        def more(g):
            return not isinstance(g, int) or g + 1 < NG

        def routes(g):
            return not isinstance(g, int) or 1 <= g <= NG

        def places(g):
            return not isinstance(g, int) or g >= 2

        def bank_of(h):
            return W if (h % 2 == 0) == (h < 6) else F

        def all_groups(eng, group, chain=None, links=0):
            group(0)
            group(1)
            with eng.Fori(2, NG - 1) as g:
                if chain:
                    chain.enter(g, 2, links)
                group(g)
            if chain:
                chain.leave(NG - 3)
            group(NG - 1)
            group(NG)

        def alone(eng):
            eng.sem_inc(s["waited"], 1)

        def heads4(ps, rows, width):
            return ps[:rows, :, 0:HB * width].rearrange("p b (h e) -> p b h e", h=HB)

        @block.sync
        def _(sp):
            sp.dma_start(x_raw[:], x[0:GB].rearrange("b t d -> t b d")).then_inc(s["x_in"], 16)
            for dst, src in ((wq_a[:], wq_s), (wk_a[:], wk_s), (wv_self[:], wv_s)):
                sp.dma_start(dst, src).then_inc(s["self_in"], 16)
            sp.dma_start(wg_sb[:], wg).then_inc(s["self_in"], 16)
            for dst, src in ((wq_sb[:], wq_c), (wk_aug[0:C, :], wkv[:, 0:H * E])):
                sp.dma_start(dst, src).then_inc(s["cross_in"], 16)
            sp.dma_start(mask_u8[:], mask).then_inc(s["mask_in"], 16)
            sp.wait_ge(s["zero_set"], 1)
            sp.dma_start(ctx_rows[0:S2, :, 0:C], ctx_in[0:GB].rearrange("b j c -> j b c")).then_inc(s["ctx_in"], 16)
            for dst, kv in ((wk_aug, 0), (wv_aug, 1)):
                sp.dma_start(dst[NULL_ROW:NULL_ROW + 1, :].rearrange("o (h e) -> o h e", h=H),
                             null_kv[kv:kv + 1, :].unsqueeze(1).broadcast_to([1, H, E])).then_inc(s["small_in"], 16)
            sp.dma_start(g_col[:], g_norm.rearrange("(d o) -> d o", o=1)).then_inc(s["small_in"], 16)
            sp.dma_start(g_out_bc[:], g_out.rearrange("(o d) -> o d", o=1).broadcast_to([T, D])).then_inc(s["small_in"], 16)
            sp.dma_start(wv_aug[0:C, :], wkv[:, H * E:2 * H * E]).then_inc(s["small_in"], 16)
            sp.dma_start(wout_sb[:], wout.rearrange("(j p) d -> p j d", p=128)).then_inc(s["wout_in"], 16)
            rows = 2048 * 128 // D
            for z in range(SLOTS // rows):
                sp.dma_start(xs_d[z * rows:(z + 1) * rows].rearrange("(p r) d -> p (r d)", p=128), zeros[:]).then_inc(s["xs_zeroed"], 16)
            sp.dma_start(w1_all[:], w1.rearrange("e d f -> d e f")).then_inc(s["ffn_in"], 16)
            sp.dma_start(w2_all[:], w2.rearrange("e (i p) d -> p e i d", p=128)).then_inc(s["ffn_in"], 16)
            sp.wait_ge(s["r1_done"], 1)
            sp.dma_start(x_raw[:], x[GB:2 * GB].rearrange("b t d -> t b d")).then_inc(s["x_in"], 16)

            def group(g):
                def batches(dram, i):
                    part = dram[i * GB:(i + 1) * GB] if isinstance(i, int) else dram[bass.ds(i * GB, GB)]
                    return part.rearrange("b j c -> j b c")

                if more(g):
                    sp.wait_ge(s["ctxT_done"], g + 1)
                    sp.dma_start(ctx_rows[0:S2, :, 0:C], batches(ctx_in, g + 1)).then_inc(s["ctx_in"], 16)
                if routes(g):
                    sp.wait_ge(s["x2_done"], g)
                    at_row = (g - 1) * (GB * T)
                    rows2 = x2_d[at_row:at_row + GB * T] if isinstance(g, int) else x2_d[bass.ds(at_row, GB * T)]
                    sp.dma_start(rows2.rearrange("(b t) d -> t b d", t=T), x2[:]).then_inc(s["x2_saved"], 16)
                if not isinstance(g, int) or g + 2 < NG:
                    sp.wait_ge(s["r1_done"], g + 2)
                    sp.dma_start(x_raw[:], batches(x, g + 2)).then_inc(s["x_in"], 16)

            group(0)
            group(1)
            with sp.Fori(2, NG - 2) as g:
                group(g)
            group(NG - 2)
            group(NG - 1)
            group(NG)

            sp.wait_ge(s["scattered"], 16 * 2 * GB * NG)

            def rows_of(dram, t):
                part = dram[t * SG:(t + 1) * SG] if isinstance(t, int) else dram[bass.ds(t * SG, SG)]
                return part.rearrange("(p r) d -> p r d", p=128)

            def expert_pair(i):
                for u in range(2 * GPX):
                    t = 2 * GPX * i + u
                    if not isinstance(t, int) or t >= 2:
                        sp.wait_ge(s["xgT_done"], t - 1)
                    sp.dma_start(xg[u % 2], rows_of(xs_d, t)).then_inc(s[f"xg_in{u % 2}"], 16)
                    if not isinstance(t, int) or t >= 2:
                        sp.wait_ge(s["y_kept"], t - 1)
                        sp.dma_start(rows_of(ys_d, t - 2), yg[u % 2]).then_inc(s[f"yg_out{u % 2}"], 16)

            expert_pair(0)
            with sp.Fori(1, X // 2) as i:
                expert_pair(i)
            for t in (X * GPX - 2, X * GPX - 1):
                sp.wait_ge(s["y_kept"], t + 1)
                sp.dma_start(rows_of(ys_d, t), yg[t % 2]).then_inc(s[f"yg_out{t % 2}"], 16)

            sp.wait_ge(s["x2_saved"], 16 * NG)

            def tokens_of(dram, t):
                part = dram[t * GB * T:(t + 1) * GB * T] if isinstance(t, int) else dram[bass.ds(t * (GB * T), GB * T)]
                return part.rearrange("(b t) d -> t b d", t=T)

            out_rows = out.rearrange("b t d -> (b t) d")

            def token_pair(i):
                for u in range(2):
                    t = 2 * i + u
                    if not isinstance(t, int) or t >= 2:
                        sp.wait_ge(s["out_ready"], t - 1)
                        sp.dma_start(tokens_of(out_rows, t - 2), final[u]).then_inc(s[f"out_saved{u}"], 16)
                    sp.dma_start(x2b[u], tokens_of(x2_d, t)).then_inc(s[f"x2_back{u}"], 16)

            token_pair(0)
            with sp.Fori(1, NG // 2) as i:
                token_pair(i)
            for t in (NG - 2, NG - 1):
                sp.wait_ge(s["out_ready"], t + 1)
                sp.dma_start(tokens_of(out_rows, t), final[t % 2]).then_inc(s[f"out_saved{t % 2}"], 16)
            for u in range(2):
                sp.wait_ge(s[f"out_saved{u}"], 16 * NG // 2)
                sp.wait_ge(s[f"yg_out{u}"], 16 * X * GPX // 2)

        @block.gpsimd
        def _(pool):
            chain = Chain(pool, s["pool_chain"])
            chain.link(pool.memset(ident[:], 0.0))
            pool.affine_select(out=ident[:], in_=ident[:], pattern=[[-1, 128]], compare_op=ALU.not_equal,
                               fill=1.0, base=0, channel_multiplier=1).then_inc(s["ident_set"], 1)
            pool.wait_ge(s["ident_set"], 1)
            chain.link(pool.memset(wk_aug[C:CA, :], 0.0))
            chain.link(pool.memset(wv_aug[C:CA, :], 0.0))
            chain.link(pool.memset(ctx_rows[:], 0.0))
            null_mark = ctx_rows[:, :, NULL_ROW:NULL_ROW + 1]
            chain.link(pool.affine_select(out=null_mark, in_=null_mark, pattern=[[0, GB], [0, 1]], compare_op=ALU.not_equal,
                                          fill=1.0, base=-S2, channel_multiplier=1))
            chain.link(pool.memset(zeros[:], 0.0))
            chain.link(pool.memset(neg_half[:], -0.5))
            pool.memset(taken[:], 0.0).then_inc(s["zero_set"], 1)
            for t in (causal, row_bias):
                chain.link(pool.memset(t[:], 0.0))
            for t in (before, ones_b):
                chain.link(pool.memset(t[:], 1.0))
            chain.link(pool.affine_select(out=causal[:], in_=causal[:], pattern=[[-1, T]], compare_op=ALU.is_ge,
                                          fill=MASKED, base=0, channel_multiplier=1))
            chain.link(pool.affine_select(out=before[:], in_=before[:], pattern=[[1, 128]], compare_op=ALU.is_gt,
                                          fill=0.0, base=0, channel_multiplier=-1))
            chain.link(pool.affine_select(out=row_bias[:], in_=row_bias[:], pattern=[[0, 1]], compare_op=ALU.not_equal,
                                          fill=1.0, base=-MASK_ROW, channel_multiplier=1))
            for e in range(X):
                chain.link(pool.memset(rev[:, e:e + 1], float(X - e)))
            pool.memset(top[:], 0.0).then_inc(s["consts"], 1)

            def rsqrt(dst, var, plus):
                alone(pool)
                chain.link(pool.tensor_scalar(plus, var, EPS, None, ALU.add))
                return pool.tensor_tensor(dst, plus, neg_half[:, 0:dst.shape[1]], ALU.pow)

            def self_norm(g):
                pool.wait_ge(s["r1_var"], g + 1)
                var = mv1[:, :, 1]
                chain.link(rsqrt(rs1[:], var, lnt[:, 0, :]))
                chain.link(pool.tensor_tensor(lnt[:, 1, :], rs1[:], rs1[:], ALU.mult))
                chain.link(pool.tensor_tensor(lnt[:, 2, :], lnt[:, 1, :], var, ALU.mult))
                rsqrt(rn1[:, 1, :], lnt[:, 2, :], lnt[:, 0, :]).then_inc(s["x1_rstd"], 1)

            def split(hi, lo, whole, done):
                alone(pool)
                chain.link(pool.tensor_copy(hi, whole))
                alone(pool)
                pool.tensor_tensor(lo, whole, hi.bitcast(F32), ALU.subtract).then_inc(done, 1)

            self_norm(0)
            pool.wait_ge(s["xs_zeroed"], 16 * (SLOTS // 2048))

            def norm_probs(m, par, half):
                pool.wait_ge(s["totals_done"], m)
                alone(pool)
                part = P[par][:, HH * half:HH * (half + 1), :]
                pool.tensor_tensor(part, part, rec[half][:].unsqueeze(2).broadcast_to([T, HH, KEYS]),
                                   ALU.mult).then_inc(s["probs_normed"], 1)

            def scatter(b):
                for j in range(2):
                    pool.indirect_dma_start(
                        out=xs_d, out_offset=bass.IndirectOffsetOnAxis(ap=slot[:, j, b:b + 1], axis=0),
                        in_=x2[:, b, :], in_offset=None, bounds_check=SLOTS - 1,
                        oob_is_err=False).then_inc(s["scattered"], 16)

            def group(g):
                for k in range(GB):
                    c, p, q = live(g, k)
                    cnt = 2 * GB * g + 2 * k
                    if p:
                        norm_probs(cnt, (k + 1) % 2, 1)
                    if q:
                        pool.wait_ge(s["out_var"], GB * g + (k - 1))
                        rsqrt(rs_o[:], mv_o[:, 1:2], lne_o[:]).then_inc(s["out_rstd"], 1)
                    if c:
                        norm_probs(cnt + 1, k % 2, 0)
                    if k == 0 and places(g):
                        pool.wait_ge(s["slots_done"], g - 1)
                        alone(pool)
                        for b in range(GB):
                            scatter(b)
                    if k == 1 and routes(g):
                        pool.wait_ge(s["r2_var"], g)
                        rsqrt(rs2[:], mv2[:, :, 1], lne2[:]).then_inc(s["x2_rstd"], 1)
                    if k == 1 and (not isinstance(g, int) or g < NG):
                        if routes(g):
                            pool.wait_ge(s["r2_done"], GB * g)
                        alone(pool)
                        pool.tensor_copy(x1_late[:], x1[:, 1:GB, :]).then_inc(s["x1_saved"], 1)
                    if k == 2 and more(g):
                        self_norm(g + 1)

            all_groups(pool, group, chain, POOL_LINKS)
            pool.wait_ge(s["slots_done"], NG)
            for b in range(GB):
                scatter(b)

            def expert_pair(i):
                for u in range(2):
                    e = 2 * i + u
                    if isinstance(e, int) and e == 0:
                        pool.wait_ge(s["ffn_in"], 16 * 2)
                    if not isinstance(e, int) or e >= 2:
                        pool.wait_ge(s["y_done"], GPX * e - GPX)
                    one = (lambda t: t[:, e]) if isinstance(e, int) else (lambda t: t[:, bass.ds(e, 1)])
                    whole = one(w1_all) if isinstance(e, int) else one(w1_all).rearrange("p o f -> p (o f)")
                    down = one(w2_all) if isinstance(e, int) else one(w2_all).rearrange("p o i d -> p (o i) d")
                    alone(pool)
                    chain.link(pool.tensor_copy(w2_e[u][:], down))
                    split(w1_hi[u][:], w1_lo[u][:], whole, s["w_split"])

            expert_pair(0)
            with pool.Fori(1, X // 2) as i:
                chain.enter(i, 1, 4)
                expert_pair(i)
            chain.leave(X // 2 - 1)

            for u in range(2):
                pool.wait_ge(s[f"yg_out{u}"], 16 * X * GPX // 2)

            def gather(t, u):
                pool.wait_ge(s["idx_set"], t + 1)
                if not isinstance(t, int) or t >= 2:
                    pool.wait_ge(s["r3_summed"], t - 1)
                alone(pool)
                for b in range(GB):
                    for j in range(2):
                        pool.indirect_dma_start(
                            out=yb[u][:, j, b, :], out_offset=None, in_=ys_d,
                            in_offset=bass.IndirectOffsetOnAxis(ap=idx[u][:, j * GB + b:j * GB + b + 1], axis=0),
                            ).then_inc(s[f"y_back{u}"], 16)

            def token_pair(i):
                for u in range(2):
                    t = 2 * i + u
                    if not (isinstance(t, int) and t + 1 == NG):
                        gather(t + 1, (u + 1) % 2)
                    pool.wait_ge(s["r3_var"], t + 1)
                    rsqrt(rs3[:], mv3[:, :, 1], lne3[:]).then_inc(s["r3_rstd"], 1)

            gather(0, 0)
            token_pair(0)
            with pool.Fori(1, NG // 2 - 1) as i:
                chain.enter(i, 1, 2)
                token_pair(i)
            chain.leave(NG // 2 - 2)
            token_pair(NG // 2 - 1)

        @block.scalar
        def _(act):
            def copy(dst, src, **kw):
                return nc.scalar.activation(dst, src, ACT.Copy, **kw)

            def self_xT(g):
                act.wait_ge(s["xT_done"], g + 1)
                copy(xT[:].rearrange("p b t -> p (b t)"), ps_w[:, F, :]).then_inc(s["xT_kept"], 1)

            def self_AV(g):
                act.wait_ge(s["sA_done"], g + 1)
                copy(sA[:].rearrange("p b t -> p (b t)"), ps_w[:, F, :]).then_inc(s["sA_kept"], 1)
                act.wait_ge(s["sV_done"], g + 1)
                copy(sV[:].rearrange("p b t -> p (b t)"), ps_w[:, W, :]).then_inc(s["sV_kept"], 1)

            def self_exp(g):
                act.wait_ge(s["sS_masked"], g + 1)
                for b in range(GB):
                    last = nc.scalar.activation(sP[:, b, :], sS[:, b, :], ACT.Exp, bias=s_nmax[:, b:b + 1],
                                                accum_out=s_sum[:, b:b + 1])
                last.then_inc(s["sP_done"], 1)

            def self_PT(g):
                act.wait_ge(s["sPT_done"], g + 1)
                copy(sPT[:].rearrange("p b t -> p (b t)"), ps_w[:, F, :]).then_inc(s["sPT_kept"], 1)

            def turn_x1(g):
                act.wait_ge(s["x1T_done"], g + 1)
                copy(x1T_hi[:].rearrange("p b t -> p (b t)"), ps_w[:, F, :]).then_inc(s["x1T_kept"], 1)

            def turn_ctx(g):
                act.wait_ge(s["ctxT_done"], g + 1)
                copy(ctxT[:].rearrange("p b j -> p (b j)"), ps_w[:CA, W, 0:GB * KEYS]).then_inc(s["ctxT_kept"], 1)

            def keep_A(g, heads):
                for h in heads:
                    act.wait_ge(s["a_done"], g * H + (h + 1))
                    nc.scalar.activation(A[:CA, h].rearrange("p b t -> p (b t)"), ps_w[:CA, bank_of(h), :], ACT.Identity,
                                         bias=row_bias[:, 0:1]).then_inc(s["a_kept"], 1)

            act.wait_ge(s["setup_T"], 1)
            copy(wqT_a[:], ps_s[:, 0, 0:128])
            copy(wkT_a[:], ps_s[:, 0, 128:256])
            copy(wgT[:], ps_s[:, 0, 256:256 + X]).then_inc(s["setup_Ts"], 1)
            self_xT(0)
            self_AV(0)
            act.wait_ge(s["setup_T"], 2)
            copy(wqT[:].rearrange("p j d -> p (j d)"), ps_v[:].rearrange("p b n -> p (b n)")).then_inc(s["setup_Ts"], 1)
            act.wait_ge(s["setup_T"], 3)
            copy(wkT[:].rearrange("p (b j) c -> p b j c", b=2), heads4(ps_t, 128, CA)).then_inc(s["setup_Ts"], 1)
            self_exp(0)
            turn_ctx(0)
            self_PT(0)
            turn_x1(0)
            act.wait_ge(s["consts"], 1)
            keep_A(0, range(H))

            def exp_half(cnt, k, half):
                act.wait_ge(s["shifted_done"], cnt + (half + 1))
                nc.scalar.activation(P[k % 2][:, HH * half:HH * (half + 1), :].rearrange("p h j -> p (h j)"),
                                     shifted[half][:].rearrange("p b h j -> p (b h j)"), ACT.Exp,
                                     scale=(rn1[:, 0, k:k + 1])).then_inc(s["probs_done"], 1)

            def keep_PT(cnt, half):
                act.wait_ge(s["PT_done"], cnt + (half - 1))
                copy(PT[:].rearrange("p h t -> p (h t)"), ps_t[:KEYS].rearrange("p b n -> p (b n)")).then_inc(s["PT_kept"], 1)

            def keep_OT(cnt, half):
                act.wait_ge(s["pv_done"], cnt + (half - 1))
                copy(OT[:, HB * half:HB * (half + 1), :].rearrange("p j t -> p (j t)"), ps_v[:, half, :]).then_inc(s["OT_kept"], 1)

            def group(g):
                for k in range(GB):
                    c, p, q = live(g, k)
                    cnt = 2 * GB * g + 2 * k
                    if k == 0 and c:
                        act.wait_ge(s["x1_rstd"], g + 1)
                        if p:
                            act.wait_ge(s["probs_done"], cnt)
                        copy(rn1[:, 0, :], rn1[:, 1, :]).then_inc(s["act_chain"], 1)
                        act.wait_ge(s["act_chain"], g + 1)
                    if k == 3 and routes(g):
                        act.wait_ge(s["logits_done"], g)
                        copy(logits[:].rearrange("p b e -> p (b e)"), ps_w[:, F, 0:GB * X]).then_inc(s["logits_kept"], 1)
                    if p:
                        keep_PT(cnt, 0)
                    if c:
                        act.wait_ge(s["v_done"], GB * g + (k + 1))
                        copy(V[k % 2][:], ps_v[:KEYS].rearrange("p b (h e) -> p (b h) e", e=E)).then_inc(s["v_kept"], 1)
                        exp_half(cnt, k, 0)
                    if k == 0 and more(g):
                        self_xT(g + 1)
                    if k == 3 and more(g):
                        turn_x1(g + 1)
                    if p:
                        keep_OT(cnt, 0)
                    if k == 1 and more(g):
                        self_exp(g + 1)
                    if p:
                        keep_PT(cnt, 1)
                    if k == 0 and more(g):
                        self_AV(g + 1)
                    if k == 1 and more(g):
                        self_PT(g + 1)
                    if k == 2 and routes(g):
                        act.wait_ge(s["x2T_done"], g)
                        copy(x2T[:].rearrange("p b t -> p (b t)"), ps_w[:, W, :]).then_inc(s["x2T_kept"], 1)
                    if k == 3 and more(g):
                        keep_A(g + 1, range(0, 6))
                        turn_ctx(g + 1)
                        keep_A(g + 1, (6, 7))
                    if c:
                        exp_half(cnt, k, 1)
                    if k == 3 and more(g):
                        keep_A(g + 1, (8, 9))
                    if p:
                        keep_OT(cnt, 1)
                    if k == 3 and more(g):
                        keep_A(g + 1, range(10, H))
                    if k == 3 and routes(g):
                        act.wait_ge(s["dlt_done"], g)
                        nc.scalar.activation(ex[:], dlt[:], ACT.Exp).then_inc(s["ex_done"], 1)

            all_groups(act, group)

            def rows_hi(t):
                act.wait_ge(s["xgT_done"], t + 1)
                copy(xgT_hi[:], ps_t[:, 0, :]).then_inc(s["xg_hi_kept"], 1)

            def expert_pair(i):
                for u in range(2 * GPX):
                    t = 2 * GPX * i + u
                    act.wait_ge(s["inp_done"], t + 1)
                    if not isinstance(t, int) or t >= 1:
                        act.wait_ge(s["hid_done"], t)
                    nc.scalar.activation(act_u, ps_v[:], ACT.Gelu).then_inc(s["gelu_done"], 1)
                    if not (isinstance(t, int) and t + 1 == X * GPX):
                        rows_hi(t + 1)
                    if not isinstance(t, int) or t >= 1:
                        keep_y(t - 1, (u - 1) % 2)

            def keep_y(t, par):
                act.wait_ge(s["y_done"], t + 1)
                if not isinstance(t, int) or t >= 2:
                    act.wait_ge(s[f"yg_out{par}"], store_count(t - 2, par))
                copy(yg[par].rearrange("p r d -> p (r d)"), ps_s[:, 0, :]).then_inc(s["y_kept"], 1)

            def store_count(t, par):
                return t * 8 + (16 - 8 * par)

            rows_hi(0)
            expert_pair(0)
            with act.Fori(1, X // 2 - 1) as i:
                expert_pair(i)
            expert_pair(X // 2 - 1)
            keep_y(X * GPX - 1, 1)

        @block.vector
        def _(dve):
            chain = Chain(dve, s["dve_chain"])
            v = nc.vector

            dve.wait_ge(s["setup_qk"], 1)
            v.tensor_scalar(wqk[:], ps_s[:, 1, 0:D], float(D) ** -0.5, None, ALU.mult).then_inc(s["setup_done"], 1)
            dve.wait_ge(s["mask_in"], 16)
            chain.link(v.tensor_copy(mask_f[:], mask_u8[:]))
            v.tensor_scalar(mask_f[:], mask_f[:], 1.0, -MASKED, ALU.subtract, ALU.mult).then_inc(s["setup_mask"], 1)
            dve.wait_ge(s["setup_T"], 4)
            chain.link(v.tensor_copy(maskT[:], ps_s[:S2, 1, 128:128 + B]))

            def mask_col(g):
                src = maskT[:, GB * g:GB * (g + 1)] if isinstance(g, int) else maskT[:, bass.ds(g * GB, GB)]
                v.tensor_scalar(ctx_rows[0:S2, :, MASK_ROW], src, 1.0, None, ALU.mult).then_inc(s["mask_col"], 1)

            dve.wait_ge(s["zero_set"], 1)
            mask_col(0)

            def self_mask(g):
                dve.wait_ge(s["sS_done"], g + 1)
                chain.link(v.tensor_tensor(sS[:], ps_w[:, F, :].rearrange("p (b t) -> p b t", b=GB),
                                           causal[:].unsqueeze(1).broadcast_to([T, GB, T]), ALU.add))
                v.tensor_reduce(s_nmax[:], sS[:], AX_X, ALU.max, negate=True).then_inc(s["sS_masked"], 1)

            def self_residual(g):
                dve.wait_ge(s["sPV_done"], g + 1)
                dve.wait_ge(s["x_in"], g * 16 + 16)
                chain.link(v.reciprocal(s_rec[:], s_sum[:]))
                for b in range(GB):
                    last = v.scalar_tensor_tensor(r1[:, b, :], ps_w[:, F, T * b:T * (b + 1)], s_rec[:, b:b + 1],
                                                  x_raw[:, b, :], ALU.mult, ALU.add)
                last.then_inc(s["r1_done"], 1)

            def self_stats(g):
                dve.wait_ge(s["r1_done"], g + 1)
                for b in range(GB):
                    last = v.bn_stats(st6[:, b, :], r1[:, b, :])
                chain.link(last)
                alone(dve)
                for b in range(GB):
                    last = v.bn_aggr(mv1[:, b, :], st6[:, b, :])
                last.then_inc(s["r1_var"], 1)

            def x1T_rest(g):
                dve.wait_ge(s["x1T_kept"], g + 1)
                v.tensor_tensor(x1T_lo[:].rearrange("p b t -> p (b t)"), ps_w[:, F, :],
                                x1T_hi[:].rearrange("p b t -> p (b t)").bitcast(F32), ALU.subtract).then_inc(s["x1T_split"], 1)

            def split_ctxT(g):
                dve.wait_ge(s["ctxT_kept"], g + 1)
                chain.link(v.tensor_copy(ctxT_hi[:], ctxT[:]))
                v.tensor_tensor(ctxT_lo[:], ctxT[:], ctxT_hi[:].bitcast(F32), ALU.subtract).then_inc(s["ctxT_split"], 1)

            def self_apply(g):
                dve.wait_ge(s["x1_rstd"], g + 1)
                for b in range(GB):
                    last = v.tensor_scalar(x1[:, b, :], r1[:, b, :], mv1[:, b, 0:1], rs1[:, b:b + 1],
                                           ALU.subtract, ALU.mult)
                last.then_inc(s["x1_done"], 1)

            dve.wait_ge(s["consts"], 1)
            self_mask(0)
            dve.wait_ge(s["small_in"], 16 * 5)
            for half in range(2):
                dve.wait_ge(s["setup_G"], half + 1)
                ps = ps_v if half == 0 else ps_t
                flat = shifted[0][:].rearrange("p b h j -> p (b h j)")[:, 0:HH * CA]
                whole = flat.rearrange("p (i b c) -> p b i c", b=2, c=CA)
                chain.link(v.tensor_scalar(whole, heads4(ps, D, CA), g_col[:, 0:1], float(E) ** -0.5, ALU.mult, ALU.mult))
                hi = G_hi[:, HH * half:HH * (half + 1), :].rearrange("p h c -> p (h c)")
                lo = G_lo[:, HH * half:HH * (half + 1), :].rearrange("p h c -> p (h c)")
                chain.link(v.tensor_copy(hi, flat))
                chain.link(v.tensor_tensor(lo, flat, hi.bitcast(F32), ALU.subtract))
                if half == 0:
                    self_residual(0)
                    self_stats(0)
                    self_apply(0)
                    x1T_rest(0)
            split_ctxT(0)
            chain.link(v.tensor_copy(wv_hi[:], wv_aug[:]))
            v.tensor_tensor(wv_lo[:], wv_aug[:], wv_hi[:].bitcast(F32), ALU.subtract).then_inc(s["setup_Gs"], 1)

            def shift(c, cnt, half, p):
                dve.wait_ge(s["scores_done"], cnt + (half + 1))
                scores = heads4(ps_s, T, KEYS)
                chain.link(v.tensor_reduce(top[:], scores, AX_X, ALU.max))
                if p:
                    dve.wait_ge(s["probs_done"], cnt + (half - 1))
                v.tensor_tensor(shifted[half][:], scores, top[:].unsqueeze(3).broadcast_to([T, 2, HB, KEYS]),
                                ALU.subtract).then_inc(s["shifted_done"], 1)

            def sum_probs(m, par, half):
                dve.wait_ge(s["probs_done"], m)
                part = P[par][:, HH * half:HH * (half + 1), :]
                chain.link(v.tensor_reduce(total[half][:], part, AX_X, ALU.add))
                wait(dve, s["probs_normed"], m - 2)
                v.reciprocal(rec[half][:], total[half][:]).then_inc(s["totals_done"], 1)

            def route_top2(g):
                dve.wait_ge(s["logits_kept"], g)
                revs = rev[:].unsqueeze(1).broadcast_to([T, GB, X])
                for j in range(2):
                    src = logits[:] if j == 0 else L2[:]
                    chain.link(v.tensor_reduce(m12[:, j, :], src, AX_X, ALU.max))
                    chain.link(v.tensor_tensor(eq[:], src, m12[:, j, :].unsqueeze(2).broadcast_to([T, GB, X]), ALU.is_equal))
                    chain.link(v.tensor_tensor(eq[:], eq[:], revs, ALU.mult))
                    chain.link(v.tensor_reduce(r12[:, j, :], eq[:], AX_X, ALU.max))
                    chain.link(v.tensor_tensor(oh[:, j], r12[:, j, :].unsqueeze(2).broadcast_to([T, GB, X]), revs, ALU.is_equal))
                    if j == 0:
                        chain.link(v.scalar_tensor_tensor(L2[:], oh[:, 0], MASKED, logits[:], ALU.mult, ALU.add))
                v.tensor_tensor(picked[:], oh[:, 0], oh[:, 1], ALU.add).then_inc(s["picked_done"], 1)
                v.tensor_tensor(dlt[:], m12[:, 1, :], m12[:, 0, :], ALU.subtract).then_inc(s["dlt_done"], 1)

            def route_ranks(g):
                dve.wait_ge(s["rank_done"], g)
                ranks = ps_w[:, F, 0:(GB + 1) * X].rearrange("p (b e) -> p b e", e=X)
                chain.link(v.tensor_tensor(pos[:], ranks[:, 0:GB, :], taken[:].unsqueeze(1).broadcast_to([T, GB, X]), ALU.add))
                v.tensor_tensor(taken[:], taken[:], ranks[:, GB, :], ALU.add).then_inc(s["rank_read"], 1)

            def route_slots(g):
                dve.wait_ge(s["ex_done"], g)
                dve.wait_ge(s["rank_read"], g)
                chain.link(v.tensor_scalar(gate[:, 0, :], ex[:], 1.0, None, ALU.add))
                chain.link(v.tensor_tensor(at[:], oh[:], pos[:].unsqueeze(1).broadcast_to([T, 2, GB, X]), ALU.mult))
                chain.link(v.reciprocal(gate[:, 0, :], gate[:, 0, :]))
                chain.link(v.tensor_reduce(place[:], at[:], AX_X, ALU.add))
                chain.link(v.tensor_tensor(gate[:, 1, :], ex[:], gate[:, 0, :], ALU.mult))
                v.tensor_scalar(first[:], r12[:], -float(CAP), float(X * CAP), ALU.mult, ALU.add)
                chain.link(v.tensor_scalar(over[:], place[:], float(CAP), None, ALU.is_ge))
                chain.link(v.tensor_tensor(slot_f[:], first[:], place[:], ALU.add))
                v.scalar_tensor_tensor(slot[:], over[:], SKIP, slot_f[:], ALU.mult, ALU.add).then_inc(s["slots_done"], 1)
                dst = (lambda t: t[:, g - 1, :].rearrange("p (j b) -> p j b", j=2)) if isinstance(g, int) else \
                    (lambda t: t[:, bass.ds(g - 1, 1), :].rearrange("p o (j b) -> p (o j) b", j=2))
                chain.link(v.scalar_tensor_tensor(dst(back_all), place[:], float(CAP - 1), first[:], ALU.min, ALU.add))
                chain.link(v.tensor_scalar(over[:], over[:], -1.0, 1.0, ALU.mult, ALU.add))
                chain.link(v.tensor_tensor(dst(gate_all), over[:], gate[:], ALU.mult))

            def group(g):
                for k in range(GB):
                    c, p, q = live(g, k)
                    cnt = 2 * GB * g + 2 * k
                    if p:
                        sum_probs(cnt, (k + 1) % 2, 1)
                    if c:
                        shift(c, cnt, 0, p)
                    if k == 3 and more(g):
                        dve.wait_ge(s["x1_saved"], g + 1)
                        self_apply(g + 1)
                    if k == 2 and routes(g):
                        dve.wait_ge(s["x2_rstd"], g)
                        if not isinstance(g, int) or g >= 2:
                            dve.wait_ge(s["scattered"], g * (32 * GB) - 32 * GB)
                            dve.wait_ge(s["x2_saved"], g * 16 - 16)
                        for b in range(GB):
                            last = v.tensor_scalar(x2[:, b, :], r2[:, b, :], mv2[:, b, 0:1], rs2[:, b:b + 1],
                                                   ALU.subtract, ALU.mult)
                        last.then_inc(s["x2_done"], 1)
                    if k == 0 and places(g):
                        route_ranks(g - 1)
                    if q:
                        dve.wait_ge(s["wout_done"], GB * g + (k - 1))
                        chain.link(v.bn_stats(st_o[:], ps_w[:, W, 0:D]))
                        alone(dve)
                        v.bn_aggr(mv_o[:], st_o[:]).then_inc(s["out_var"], 1)
                        dve.wait_ge(s["out_var"], GB * g + (k - 1))
                        v.scalar_tensor_tensor(centred[:], ps_w[:, W, 0:D], mv_o[:, 0:1], g_out_bc[:], ALU.subtract,
                                               ALU.mult).then_inc(s["out_centred"], 1)
                    if k == 1 and more(g):
                        self_mask(g + 1)
                    if k == 3 and more(g):
                        x1T_rest(g + 1)
                    if c:
                        sum_probs(cnt + 1, k % 2, 0)
                    if k == 0 and places(g):
                        route_slots(g - 1)
                    if k == 3 and routes(g):
                        route_top2(g)
                    if q:
                        dve.wait_ge(s["out_rstd"], GB * g + (k - 1))
                        dve.wait_ge(s["out_centred"], GB * g + (k - 1))
                        if k == 3:
                            dve.wait_ge(s["x1_saved"], g + 1)
                        res = x1[:, 0, :] if k == 2 else x1_of(g, k)
                        j = (k + 2) % GB
                        v.scalar_tensor_tensor(r2[:, j, :], centred[:], rs_o[:, 0:1], res, ALU.mult,
                                               ALU.add).then_inc(s["r2_done"], 1)
                        dve.wait_ge(s["r2_done"], GB * g + (k - 1))
                        chain.link(v.bn_stats(st_o[:], r2[:, j, :]))
                        alone(dve)
                        last = v.bn_aggr(mv2[:, j, :], st_o[:])
                        if k == 1:
                            last.then_inc(s["r2_var"], 1)
                        else:
                            chain.link(last)
                    if k == 2 and more(g):
                        self_residual(g + 1)
                    if c:
                        shift(c, cnt, 1, p)
                    if k == 0 and more(g):
                        dve.wait_ge(s["ctxT_done"], g + 1)
                        mask_col(g + 1)
                    if k == 2 and more(g):
                        self_stats(g + 1)
                    if k == 3 and more(g):
                        split_ctxT(g + 1)

            def x1_of(g, k):
                return x1_late[:, {3: 0, 0: 1, 1: 2}[k], :]

            all_groups(dve, group, chain, DVE_LINKS)
            route_ranks(NG)
            route_slots(NG)

            def rows_lo(t):
                dve.wait_ge(s["xg_hi_kept"], t + 1)
                v.tensor_tensor(xgT_lo[:], ps_t[:, 0, :], xgT_hi[:].bitcast(F32), ALU.subtract).then_inc(s["xg_lo_kept"], 1)

            def expert_pair(i):
                for u in range(2 * GPX):
                    t = 2 * GPX * i + u
                    dve.wait_ge(s["gates_done"], t + 1)
                    dve.wait_ge(s["gelu_done"], t + 1)
                    v.tensor_tensor(hid[u % 2], act_u, ps_w[:], ALU.mult).then_inc(s["hid_done"], 1)
                    if not (isinstance(t, int) and t + 1 == X * GPX):
                        rows_lo(t + 1)

            rows_lo(0)
            expert_pair(0)
            with dve.Fori(1, X // 2 - 1) as i:
                expert_pair(i)
            expert_pair(X // 2 - 1)

            def set_idx(t, u):
                src = (lambda a: a[:, t, :]) if isinstance(t, int) else (lambda a: a[:, bass.ds(t, 1), :].rearrange("p o n -> p (o n)"))
                if not isinstance(t, int) or t >= 2:
                    dve.wait_ge(s[f"y_back{u}"], back_count(t - 2, u))
                v.tensor_scalar(idx[u][:], src(back_all), 1.0, None, ALU.mult).then_inc(s["idx_set"], 1)

            def back_count(t, u):
                return t * (8 * GB * 2) + (16 * 2 * GB - 8 * GB * 2 * u)

            set_idx(0, 0)

            def token_pair(i):
                for u in range(2):
                    t = 2 * i + u
                    if not (isinstance(t, int) and t + 1 >= NG):
                        set_idx(t + 1, (u + 1) % 2)
                    gates = gate_all[:, t, :] if isinstance(t, int) else gate_all[:, bass.ds(t, 1), :].rearrange("p o n -> p (o n)")
                    chain.link(v.tensor_scalar(gate_t[:], gates, 1.0, None, ALU.mult))
                    dve.wait_ge(s[f"y_back{u}"], back_count(t, u))
                    dve.wait_ge(s[f"x2_back{u}"], t * 8 + (16 - 8 * u))
                    for j in range(2):
                        for b in range(GB):
                            last = v.scalar_tensor_tensor(r3[:, b, :], yb[u][:, j, b, :], gate_t[:, j * GB + b:j * GB + b + 1],
                                                          (x2b[u] if j == 0 else r3)[:, b, :], ALU.mult, ALU.add)
                        if j == 0:
                            chain.link(last)
                    last.then_inc(s["r3_summed"], 1)
                    dve.wait_ge(s["r3_summed"], t + 1)
                    for b in range(GB):
                        last = v.bn_stats(st6[:, b, :], r3[:, b, :])
                    chain.link(last)
                    alone(dve)
                    for b in range(GB):
                        last = v.bn_aggr(mv3[:, b, :], st6[:, b, :])
                    last.then_inc(s["r3_var"], 1)
                    dve.wait_ge(s["r3_rstd"], t + 1)
                    if not isinstance(t, int) or t >= 2:
                        dve.wait_ge(s[f"out_saved{u}"], (t - 2) * 8 + (16 - 8 * u))
                    for b in range(GB):
                        last = v.tensor_scalar(final[u][:, b, :], r3[:, b, :], mv3[:, b, 0:1], rs3[:, b:b + 1],
                                               ALU.subtract, ALU.mult)
                    last.then_inc(s["out_ready"], 1)

            token_pair(0)
            with dve.Fori(1, NG // 2 - 1) as i:
                chain.enter(i, 1, 6)
                token_pair(i)
            chain.leave(NG // 2 - 2)
            token_pair(NG // 2 - 1)

        @block.tensor
        def _(pe):
            mm = nc.tensor.matmul

            def turn(dst, src):
                rows = src.shape[0]
                return nc.tensor.transpose(dst, src, ident[:rows, :rows])

            def mm3(dst, a, b):
                mm(dst, a[0], b[0], start=True, stop=False)
                mm(dst, a[1], b[0], start=False, stop=False)
                return mm(dst, a[0], b[1], start=False, stop=True)

            def self_xT(g):
                pe.wait_ge(s["x_in"], g * 16 + 16)
                for b in range(GB):
                    last = turn(ps_w[:, F, T * b:T * (b + 1)], x_raw[:, b, :])
                last.then_inc(s["xT_done"], 1)

            def self_AV(g):
                pe.wait_ge(s["xT_kept"], g + 1)
                mm(ps_w[:, F, :], wqk[:], xT[:].rearrange("p b t -> p (b t)"), start=True, stop=True).then_inc(s["sA_done"], 1)
                for b in range(GB):
                    last = mm(ps_w[:, W, T * b:T * (b + 1)], xT[:, b, :], wv_self[:], start=True, stop=True)
                last.then_inc(s["sV_done"], 1)

            def self_S(g):
                pe.wait_ge(s["sA_kept"], g + 1)
                for b in range(GB):
                    last = mm(ps_w[:, F, T * b:T * (b + 1)], sA[:, b, :], xT[:, b, :], start=True, stop=True)
                last.then_inc(s["sS_done"], 1)

            def self_PT(g):
                pe.wait_ge(s["sS_masked"], g + 1)
                pe.wait_ge(s["sP_done"], g + 1)
                for b in range(GB):
                    last = turn(ps_w[:, F, T * b:T * (b + 1)], sP[:, b, :])
                last.then_inc(s["sPT_done"], 1)

            def self_PV(g):
                pe.wait_ge(s["sPT_kept"], g + 1)
                pe.wait_ge(s["sV_kept"], g + 1)
                for b in range(GB):
                    last = mm(ps_w[:, F, T * b:T * (b + 1)], sPT[:, b, :], sV[:, b, :], start=True, stop=True)
                last.then_inc(s["sPV_done"], 1)

            def turn_x1(g):
                pe.wait_ge(s["x1_done"], g + 1)
                for b in range(GB):
                    last = turn(ps_w[:, F, T * b:T * (b + 1)], x1[:, b, :])
                last.then_inc(s["x1T_done"], 1)

            def turn_ctx(g):
                pe.wait_ge(s["ctx_in"], g * 16 + 16)
                pe.wait_ge(s["mask_col"], g + 1)
                for b in range(GB):
                    last = turn(ps_w[:CA, W, KEYS * b:KEYS * (b + 1)], ctx_rows[:, b, :])
                last.then_inc(s["ctxT_done"], 1)

            def project(g, heads):
                for h in heads:
                    if h == 7:
                        pe.wait_ge(s["ctxT_kept"], g + 1)
                    if h >= 2:
                        pe.wait_ge(s["a_kept"], g * H + (h if h == 6 else h - 1))
                    mm3(ps_w[:CA, bank_of(h), :], (G_hi[:, h, :], G_lo[:, h, :]),
                        (x1T_hi[:].rearrange("p b t -> p (b t)"),
                         x1T_lo[:].rearrange("p b t -> p (b t)"))).then_inc(s["a_done"], 1)

            pe.wait_ge(s["ident_set"], 1)
            pe.wait_ge(s["self_in"], 16 * 4)
            turn(ps_s[:, 0, 0:128], wq_a[:])
            turn(ps_s[:, 0, 128:256], wk_a[:])
            turn(ps_s[:, 0, 256:256 + X], wg_sb[:]).then_inc(s["setup_T"], 1)
            self_xT(0)
            pe.wait_ge(s["setup_Ts"], 1)
            mm(ps_s[:, 1, 0:D], wqT_a[:], wkT_a[:], start=True, stop=True).then_inc(s["setup_qk"], 1)
            pe.wait_ge(s["setup_done"], 1)
            self_AV(0)
            pe.wait_ge(s["cross_in"], 16 * 2)
            for j in range(8):
                last = turn(ps_v[:, j // 4, 128 * (j % 4):128 * (j % 4 + 1)], wq_sb[:, 128 * j:128 * (j + 1)])
            last.then_inc(s["setup_T"], 1)
            pe.wait_ge(s["small_in"], 16 * 5)
            for j in range(8):
                last = turn(ps_t[:, j // 4, CA * (j % 4):CA * (j % 4 + 1)], wk_aug[:, 128 * j:128 * (j + 1)])
            last.then_inc(s["setup_T"], 1)
            self_S(0)
            pe.wait_ge(s["setup_mask"], 1)
            turn(ps_s[:S2, 1, 128:128 + B], mask_f[:]).then_inc(s["setup_T"], 1)
            pe.wait_ge(s["setup_Ts"], 3)
            for half in range(2):
                ps = ps_v if half == 0 else ps_t
                for i in range(HB):
                    for b in range(2):
                        h = HH * half + 2 * i + b
                        last = mm(ps[:, b, CA * i:CA * (i + 1)], wqT[E * b:E * (b + 1), h // 2, :],
                                  wkT[E * b:E * (b + 1), h // 2, :], start=True, stop=True)
                last.then_inc(s["setup_G"], 1)
            pe.wait_ge(s["sV_kept"], 1)
            turn_ctx(0)
            self_PT(0)
            self_PV(0)
            turn_x1(0)
            pe.wait_ge(s["x1T_split"], 1)
            pe.wait_ge(s["setup_Gs"], 1)
            project(0, range(H))

            def score(k, half, i):
                last = mm(ps_s[:, i // HB, KEYS * (i % HB):KEYS * (i % HB + 1)], A[:CA, HH * half + i, k, :], ctxT[:, k, :],
                          start=True, stop=True)
                if i == HH - 1:
                    last.then_inc(s["scores_done"], 1)

            def turn_probs(par, half):
                for i in range(HH):
                    last = turn(ps_t[:KEYS, i // HB, T * (i % HB):T * (i % HB + 1)], P[par][:, HH * half + i, :])
                last.then_inc(s["PT_done"], 1)

            def weigh(par, half, first, end):
                for i in range(first, end):
                    last = mm(ps_v[E * (i % 2):E * (i % 2 + 1), half, T * (i // 2):T * (i // 2 + 1)],
                              V[par][:, HH * half + i, :], PT[:, i, :], start=True, stop=True)
                if end == HH:
                    last.then_inc(s["pv_done"], 1)

            def group(g):
                for k in range(GB):
                    c, p, q = live(g, k)
                    cnt = 2 * GB * g + 2 * k
                    done = GB * g + k
                    if p:
                        pe.wait_ge(s["probs_normed"], cnt - 1)
                        wait(pe, s["PT_kept"], cnt - 2)
                        turn_probs((k + 1) % 2, 0)
                    if c:
                        if k == 0:
                            pe.wait_ge(s["a_kept"], g * H + H)
                            pe.wait_ge(s["ctxT_kept"], g + 1)
                        wait(pe, s["shifted_done"], cnt)
                        for i in range(HH):
                            score(k, 0, i)
                        if k == 0:
                            pe.wait_ge(s["ctxT_split"], g + 1)
                    if k == 3 and routes(g):
                        pe.wait_ge(s["x2T_kept"], g)
                        if more(g):
                            pe.wait_ge(s["r1_done"], g + 2)
                        elif places(g):
                            pe.wait_ge(s["rank_read"], g - 1)
                        for b in range(GB):
                            last = mm(ps_w[:, F, X * b:X * (b + 1)], x2T[:, b, :], wgT[:], start=True, stop=True)
                        last.then_inc(s["logits_done"], 1)
                    if p or q:
                        wait(pe, s["OT_kept"], cnt - 2)
                    if c:
                        for j in range(2):
                            last = mm3(ps_v[:KEYS, j, :], (ctxT_hi[:, k, :], ctxT_lo[:, k, :]),
                                       (wv_hi[:, BANK * j:BANK * (j + 1)], wv_lo[:, BANK * j:BANK * (j + 1)]))
                        last.then_inc(s["v_done"], 1)
                    if k == 1 and more(g):
                        pe.wait_ge(s["sV_kept"], g + 2)
                    if q:
                        wait(pe, s["out_centred"], done - 2)
                        for j in range(8):
                            last = mm(ps_w[:, W, 0:D], OT[:, j, :], wout_sb[:, j, :], start=(j == 0), stop=(j == 7))
                        last.then_inc(s["wout_done"], 1)
                    if k == 0 and more(g):
                        if places(g):
                            pe.wait_ge(s["rank_read"], g - 1)
                        self_xT(g + 1)
                    if k == 1 and more(g):
                        self_S(g + 1)
                    if k == 2 and more(g):
                        self_PV(g + 1)
                    if k == 3 and more(g):
                        if routes(g):
                            pe.wait_ge(s["logits_kept"], g)
                        turn_x1(g + 1)
                    if p:
                        if c:
                            pe.wait_ge(s["v_kept"], done + 1)
                        pe.wait_ge(s["PT_kept"], cnt - 1)
                        weigh((k + 1) % 2, 0, 0, HH)
                        pe.wait_ge(s["probs_normed"], cnt)
                        turn_probs((k + 1) % 2, 1)
                    if k == 3 and more(g):
                        pe.wait_ge(s["x1T_split"], g + 2)
                        if q:
                            pe.wait_ge(s["out_centred"], done - 1)
                        project(g + 1, (0, 1))
                    if c:
                        pe.wait_ge(s["shifted_done"], cnt + 1)
                        for i in range(HH):
                            score(k, 1, i)
                            if k == 3 and more(g) and i == HB - 1:
                                project(g + 1, (2, 3))
                    if k == 0 and more(g):
                        if q:
                            pe.wait_ge(s["out_centred"], done - 1)
                        self_AV(g + 1)
                    if k == 1 and more(g):
                        self_PT(g + 1)
                    if k == 2 and routes(g):
                        if q:
                            pe.wait_ge(s["out_centred"], done - 1)
                        pe.wait_ge(s["x2_done"], g)
                        for b in range(GB):
                            last = turn(ps_w[:, W, T * b:T * (b + 1)], x2[:, b, :])
                        last.then_inc(s["x2T_done"], 1)
                    if k == 3 and more(g):
                        project(g + 1, (4, 5))
                        pe.wait_ge(s["a_kept"], g * H + (H + 5))
                        turn_ctx(g + 1)
                        project(g + 1, (6, 7))
                    if p:
                        pe.wait_ge(s["PT_kept"], cnt)
                        weigh((k + 1) % 2, 1, 0, HB)
                        if k == 3 and more(g):
                            project(g + 1, (8, 9))
                        weigh((k + 1) % 2, 1, HB, HH)
                    if k == 3 and more(g):
                        project(g + 1, range(10, H))
                        pe.wait_ge(s["a_kept"], g * H + (H + 15))
                    if k == 3 and routes(g):
                        pe.wait_ge(s["picked_done"], g)
                        if not more(g):
                            pe.wait_ge(s["logits_kept"], g)
                        ranks = ps_w[:, F, 0:(GB + 1) * X]
                        for b in range(GB + 1):
                            for a in range(min(b + 1, GB)):
                                last = mm(ranks[:, X * b:X * (b + 1)], (before if a == b else ones_b)[:], picked[:, a, :],
                                          start=(a == 0), stop=(a == min(b, GB - 1)))
                        last.then_inc(s["rank_done"], 1)

            pe.wait_ge(s["consts"], 1)
            pe.wait_ge(s["wout_in"], 16)
            all_groups(pe, group)

            def turn_rows(t, u):
                pe.wait_ge(s[f"xg_in{u % 2}"], t * 8 + (16 - 8 * (u % 2)))
                if not isinstance(t, int) or t >= 1:
                    pe.wait_ge(s["xg_lo_kept"], t)
                for r in range(4):
                    last = turn(ps_t[:, 0, 128 * r:128 * (r + 1)], xg[u % 2][:, r, :])
                last.then_inc(s["xgT_done"], 1)

            def up(t, u):
                e = u // GPX
                pe.wait_ge(s["xg_lo_kept"], t + 1)
                if not isinstance(t, int) or t >= 1:
                    pe.wait_ge(s["hid_done"], t)
                for b in range(4):
                    ps = ps_v if b < 2 else ps_w
                    last = mm3(ps[:, b % 2, :], (w1_hi[e][:, 128 * b:128 * (b + 1)], w1_lo[e][:, 128 * b:128 * (b + 1)]),
                               (xgT_hi[:], xgT_lo[:]))
                    if b == 1:
                        last.then_inc(s["inp_done"], 1)
                last.then_inc(s["gates_done"], 1)

            def down(t, u):
                e = u // GPX
                pe.wait_ge(s["hid_done"], t + 1)
                if not isinstance(t, int) or t >= 1:
                    pe.wait_ge(s["y_kept"], t)
                for r in range(4):
                    for j in range(2):
                        last = mm(ps_s[:, 0, D * r:D * (r + 1)], hid[u % 2][:, j, 128 * r:128 * (r + 1)], w2_e[e][:, j, :],
                                  start=(j == 0), stop=(j == 1))
                last.then_inc(s["y_done"], 1)

            def expert_pair(i):
                for u in range(2 * GPX):
                    t = 2 * GPX * i + u
                    if u % GPX == 0:
                        pe.wait_ge(s["w_split"], 2 * i + (u // GPX + 1))
                    up(t, u)
                    if not (isinstance(t, int) and t + 1 == X * GPX):
                        turn_rows(t + 1, (u + 1) % (2 * GPX))
                    if not isinstance(t, int) or t >= 1:
                        down(t - 1, (u - 1) % (2 * GPX))

            turn_rows(0, 0)
            expert_pair(0)
            with pe.Fori(1, X // 2 - 1) as i:
                expert_pair(i)
            expert_pair(X // 2 - 1)
            down(X * GPX - 1, 2 * GPX - 1)


POOL_LINKS = 10
DVE_LINKS = 53

_INS = ["x", "ctx_768", "mask_BxS2_bf1", "L0_attn_Wq", "L0_attn_Wk", "L0_attn_Wv", "L0_xattn_g_norm",
        "L0_xattn_null_kv", "L0_xattn_Wq", "L0_xattn_Wkv", "L0_xattn_Wout", "L0_xattn_g_out",
        "L0_ffn_Wg", "L0_ffn_W1", "L0_ffn_W2"]


def kernel(**inputs):
    import numpy as _np
    import concourse.bacc as _bacc
    from concourse import mybir as _mybir
    from concourse.bass_utils import run_bass_kernel_spmd as _run

    nc = _bacc.Bacc("TRN2", target_bir_lowering=False, num_devices=1)
    arrays, args = {}, []
    for name in _INS:
        a = _np.ascontiguousarray(inputs[name])
        arrays[f"in_{name}_dram"] = a
        args.append(nc.dram_tensor(f"in_{name}_dram", a.shape, _mybir.dt.from_np(a.dtype), kind="ExternalInput").ap())
    args.append(nc.dram_tensor("out_0_dram", (B, T, D), F32, kind="ExternalOutput").ap())
    decoder(nc, *args)
    r = _run(nc, [arrays], core_ids=[0])
    return r.results[0]["out_0_dram"]
```

```python
from contextlib import ExitStack

import concourse.bass as bass
from concourse import mybir

F32 = mybir.dt.float32
F32R = mybir.dt.float32r
BF16 = mybir.dt.bfloat16
I32 = mybir.dt.int32
U8 = mybir.dt.uint8
ALU = mybir.AluOpType
ACT = mybir.ActivationFunctionType
AX_X = mybir.AxisListType.X

B, T, D = 64, 128, 128
S2, C = 120, 96
H, E = 16, 64
KEYS = S2 + 1
CA = C + 2
NULL_ROW, MASK_ROW = C, C + 1
GB = 4
NG = B // GB
HH = H // 2
HB = HH // 2
X, K2, FI = 8, 2, 256
TOKENS = B * T
CAP = int(TOKENS * K2 * 1.25 / X)
SLOTS = X * CAP
SG = 512
GPX = CAP // SG
MASKED = -float(2 ** 100)
SKIP = 2 * SLOTS
EPS = 1e-5
BANK = 512
DW = D + 2
FILL_ROWS = 1024
RING = GPX
TRING = 4
assert CAP % SG == 0 and GPX % 2 == 1 and SKIP > TOKENS * K2


class Chain:

    def __init__(self, eng, sem):
        self.eng, self.sem, self.n, self.loop = eng, sem, 0, None

    def enter(self, i, start, per):
        self.loop = (i, start, per, self.n)

    def leave(self, turns):
        i, start, per, n0 = self.loop
        assert self.n - n0 == per, (self.n - n0, per)
        self.n, self.loop = n0 + per * turns, None

    def link(self, ins):
        ins.then_inc(self.sem, 1)
        self.n += 1
        if self.loop is None:
            self.eng.wait_ge(self.sem, self.n)
        else:
            i, start, per, _ = self.loop
            self.eng.wait_ge(self.sem, i * per + (self.n - start * per))


def wait(eng, sem, value):
    if not isinstance(value, int) or value > 0:
        eng.wait_ge(sem, value)


def decoder(nc, x, ctx_in, mask, wq_s, wk_s, wv_s, g_norm, null_kv, wq_c, wkv, wout, g_out, wg, w1, w2, out):
    with ExitStack() as stack:
        def sb(name, shape, dt=F32):
            return stack.enter_context(nc.sbuf_tensor(name, shape, dt))

        def pair(name):
            return stack.enter_context(nc.psum_tensor(name, [128, 2, BANK], F32))

        def sem(name):
            return stack.enter_context(nc.semaphore(name))

        xs_d = nc.dram_tensor("routed_rows", [SLOTS, DW], F32, kind="Internal").ap()
        ys_d = nc.dram_tensor("result_rows", [TOKENS * K2, D], F32, kind="Internal").ap()
        x2_d = nc.dram_tensor("tokens_x2", [TOKENS, D], F32, kind="Internal").ap()

        ps_s, ps_t, ps_v, ps_w = pair("ps_scores"), pair("ps_turned"), pair("ps_values"), pair("ps_work")
        W, F = 0, 1

        ident = sb("ident", [128, 128])
        causal = sb("causal", [T, T])
        before = sb("before", [128, 128], BF16)
        ones_b = sb("ones_b", [128, 128], BF16)
        rev = sb("rev", [128, X])
        neg_half = sb("neg_half", [128, GB])
        zeros = sb("zeros", [128, FILL_ROWS * D // 128])
        unused = sb("unused", [128, FILL_ROWS // 128, DW])
        row_bias = sb("row_bias", [CA, 1])
        wqk = sb("wqk", [D, D])
        wv_self = sb("wv_self", [D, D])
        G_hi, G_lo = sb("G_hi", [D, H, CA], F32R), sb("G_lo", [D, H, CA], F32R)
        wv_aug = sb("wv_aug", [CA, H * E])
        wv_hi, wv_lo = sb("wv_hi", [CA, H * E], F32R), sb("wv_lo", [CA, H * E], F32R)
        wout_sb = sb("wout_sb", [128, H * E // 128, D])
        g_col = sb("g_col", [D, 1])
        g_out_bc = sb("g_out_bc", [T, D])
        wgT = sb("wgT", [D, X])
        mask_u8 = sb("mask_u8", [B, S2], U8)
        mask_f = sb("mask_f", [B, S2])
        maskT = sb("maskT", [S2, B])
        w1_all = sb("w1_all", [D, X, 2 * FI])
        w2_all = sb("w2_all", [128, X, FI // 128, D])
        x_raw = sb("x_raw", [T, GB, D])
        xT = sb("xT", [D, GB, T])
        sA = sb("sA", [D, GB, T])
        sV = sb("sV", [T, GB, D])
        sS = sb("sS", [T, GB, T])
        sP = sb("sP", [T, GB, T])
        sPT = sb("sPT", [T, GB, T])
        s_nmax, s_sum, s_rec = sb("s_nmax", [T, GB]), sb("s_sum", [T, GB]), sb("s_rec", [T, GB])
        r1 = sb("r1", [T, GB, D])
        st6 = sb("st6", [T, GB, 6])
        mv1 = sb("mv1", [T, GB, 2])
        rs1, rn1 = sb("rs1", [T, GB]), sb("rn1", [T, 2, GB])
        lnt = sb("lnt", [T, 3, GB])
        x1, x1_late = sb("x1", [T, GB, D]), sb("x1_late", [T, 3, D])
        x1T_hi, x1T_lo = sb("x1T_hi", [D, GB, T], F32R), sb("x1T_lo", [D, GB, T], F32R)

        ctx_rows = sb("ctx_rows", [KEYS, GB, CA])
        ctxT = sb("ctxT", [CA, GB, KEYS])
        ctxT_hi, ctxT_lo = sb("ctxT_hi", [CA, GB, KEYS], F32R), sb("ctxT_lo", [CA, GB, KEYS], F32R)
        A = sb("A", [128, H, GB, T])
        V = [sb(f"V{i}", [KEYS, H, E]) for i in range(2)]
        top = sb("top", [T, 2, HB])
        shifted = [sb(f"shifted{i}", [T, 2, HB, KEYS]) for i in range(2)]
        P = [sb(f"P{i}", [T, H, KEYS]) for i in range(2)]
        PT = sb("PT", [KEYS, HH, T])
        total = [sb(f"total{i}", [T, HH]) for i in range(2)]
        rec = [sb(f"rec{i}", [T, HH]) for i in range(2)]
        OT = sb("OT", [128, 8, T])
        st_o, mv_o, rs_o, lne_o = sb("st_o", [T, 6]), sb("mv_o", [T, 2]), sb("rs_o", [T, 1]), sb("lne_o", [T, 1])
        centred = sb("centred", [T, D])
        r2, mv2, rs2, lne2 = sb("r2", [T, GB, D]), sb("mv2", [T, GB, 2]), sb("rs2", [T, GB]), sb("lne2", [T, GB])

        routed = sb("routed", [T, 2, GB, DW])
        x2 = routed[:, 0, :, 0:D]
        x2T = sb("x2T", [D, GB, T])
        logits = sb("logits", [T, GB, X])
        m12 = sb("m12", [T, 2, GB])
        eq, L2 = sb("eq", [T, GB, X]), sb("L2", [T, GB, X])
        r12 = sb("r12", [T, 2, GB])
        oh = sb("oh", [T, 2, GB, X])
        picked = sb("picked", [T, GB, X], BF16)
        dlt, ex, gate = sb("dlt", [T, GB]), sb("ex", [T, GB]), sb("gate", [T, 2, GB])
        pos, taken = sb("pos", [T, GB, X]), sb("taken", [T, X])
        at = sb("at", [T, 2, GB, X])
        place, first, over = sb("place", [T, 2, GB]), sb("first", [T, 2, GB]), sb("over", [T, 2, GB])
        slot_f = sb("slot_f", [T, 2, GB])
        slot = sb("slot", [T, 2, GB], I32)
        result_row = sb("result_row", [T, 2, GB])

        s = {}
        for name in """self_in cross_in small_in wout_in ffn_in mask_in ident_set unused_set rows_set token_no zero_set consts setup_T setup_Ts setup_qk setup_G setup_Gs setup_mask setup_done wv_split
                       x_in ctx_in xs_filled ys_filled x2_saved scattered
                       scores_done v_done PT_done a_done pv_done wout_done
                       xT_done sA_done sV_done sS_done sPT_done sPV_done x1T_done ctxT_done x2T_done logits_done rank_done
                       shifted_done totals_done out_centred out_var r2_done
                       sS_masked r1_done r1_var x1_done x2_done mask_col picked_done rank_read slots_done dlt_done r2_var
                       probs_done probs_normed v_kept PT_kept a_kept OT_kept
                       xT_kept sA_kept sV_kept sP_done sPT_kept x1T_kept ctxT_kept x2T_kept logits_kept ex_done
                       out_rstd x1_rstd x1_norm x2_rstd x1_saved x1T_split ctxT_split
                       dve_chain pool_chain act_chain waited""".split():
            s[name] = sem(name)

        with ExitStack() as early:
            def eb(name, shape, dt=F32):
                return early.enter_context(nc.sbuf_tensor(name, shape, dt))

            wq_a, wk_a = eb("wq_a", [D, D]), eb("wk_a", [D, D])
            wqT_a, wkT_a = eb("wqT_a", [D, D]), eb("wkT_a", [D, D])
            wq_sb = eb("wq_sb", [D, H * E])
            wk_aug = eb("wk_aug", [CA, H * E])
            wg_sb = eb("wg_sb", [X, D])
            wqT, wkT = eb("wqT", [128, 8, D]), eb("wkT", [128, 8, CA])

        xgT_hi, xgT_lo = sb("xgT_hi", [D, SG], F32R), sb("xgT_lo", [D, SG], F32R)
        w1_hi = [sb(f"w1_hi{i}", [D, 2 * FI], F32R) for i in range(2)]
        w1_lo = [sb(f"w1_lo{i}", [D, 2 * FI], F32R) for i in range(2)]
        w2_e = [sb(f"w2_e{i}", [128, 2, D]) for i in range(2)]
        flat_A = A[:].rearrange("p h b t -> p (h b t)")
        place_A = [0]

        def in_A(*shape):
            at, size = place_A[0], shape[0] * shape[1]
            place_A[0] = at + size
            assert place_A[0] <= H * GB * T
            return flat_A[:, at:at + size].rearrange("p (r n) -> p r n", n=shape[1])

        act_u = in_A(2, SG)
        hid = [in_A(2, SG) for _ in range(2)]
        yg = [in_A(4, D) for _ in range(2)]
        xg = [in_A(4, DW) for _ in range(RING)]
        for name in """xg_in0 xg_in1 xg_in2 xg_in3 xg_in4 w1_hi_kept w_split
                       xgT_done xg_hi_kept xg_lo_kept inp_done gates_done gelu_done hid_done y_done y_kept yg_out0 yg_out1
                       x2_back0 x2_back1 x2_back2 x2_back3 y_back0 y_back1 y_back2 y_back3 r3_summed r3_var r3_rstd out_ready out_saved0 out_saved1""".split():
            s[name] = sem(name)
        flat_P = [P[i][:].rearrange("p h j -> p (h j)") for i in range(2)]
        x2b = [flat_P[i // 2][:, (i % 2) * GB * D:(i % 2 + 1) * GB * D].rearrange("p (b d) -> p b d", b=GB) for i in range(TRING)]
        final = [flat_P[i][:, 2 * GB * D:3 * GB * D].rearrange("p (b d) -> p b d", b=GB) for i in range(2)]
        yb = [flat_A[:, i * 2 * GB * D:(i + 1) * 2 * GB * D].rearrange("p (b j d) -> p b j d", j=2, b=GB) for i in range(TRING)]
        r3 = [r1, r2, x1, x_raw]
        mv3 = [sb(f"mv3_{i}", [T, GB, 2]) for i in range(TRING)]
        rs3, nb3 = [sb(f"rs3_{i}", [T, GB]) for i in range(TRING)], [sb(f"nb3_{i}", [T, GB]) for i in range(TRING)]
        lne3 = lnt[:, 0, :]

        block = stack.enter_context(nc.Block())

        def live(g, k):
            if not isinstance(g, int):
                return True, True, True
            c = GB * g + k
            return c < B, 1 <= c <= B, 2 <= c < B + 2

        def more(g):
            return not isinstance(g, int) or g + 1 < NG

        def routes(g):
            return not isinstance(g, int) or 1 <= g <= NG

        def places(g):
            return not isinstance(g, int) or g >= 2

        CTX_SLOT = 6

        def slot_of(h):
            return h if h < CTX_SLOT else h + 1

        def bank(slot):
            pair = ps_w if slot % 4 < 2 else ps_t
            return pair[:CA, slot % 2, :]

        def all_groups(eng, group, chain=None, links=0):
            group(0)
            group(1)
            with eng.Fori(2, NG - 1) as g:
                if chain:
                    chain.enter(g, 2, links)
                group(g)
            if chain:
                chain.leave(NG - 3)
            group(NG - 1)
            group(NG)

        def alone(eng):
            eng.sem_inc(s["waited"], 1)

        def scatter_count(t, par):
            return t * 32 + (64 - 32 * par)

        def heads4(ps, rows, width):
            return ps[:rows, :, 0:HB * width].rearrange("p b (h e) -> p b h e", h=HB)

        @block.sync
        def _(sp):
            sp.dma_start(x_raw[:], x[0:GB].rearrange("b t d -> t b d")).then_inc(s["x_in"], 16)
            for dst, src in ((wq_a[:], wq_s), (wk_a[:], wk_s), (wv_self[:], wv_s)):
                sp.dma_start(dst, src).then_inc(s["self_in"], 16)
            sp.dma_start(wg_sb[:], wg).then_inc(s["self_in"], 16)
            for dst, src in ((wq_sb[:], wq_c), (wk_aug[0:C, :], wkv[:, 0:H * E])):
                sp.dma_start(dst, src).then_inc(s["cross_in"], 16)
            sp.dma_start(mask_u8[:], mask).then_inc(s["mask_in"], 16)
            sp.wait_ge(s["zero_set"], 1)
            sp.dma_start(ctx_rows[0:S2, :, 0:C], ctx_in[0:GB].rearrange("b j c -> j b c")).then_inc(s["ctx_in"], 16)
            for dst, kv in ((wk_aug, 0), (wv_aug, 1)):
                sp.dma_start(dst[NULL_ROW:NULL_ROW + 1, :].rearrange("o (h e) -> o h e", h=H),
                             null_kv[kv:kv + 1, :].unsqueeze(1).broadcast_to([1, H, E])).then_inc(s["small_in"], 16)
            sp.dma_start(g_col[:], g_norm.rearrange("(d o) -> d o", o=1)).then_inc(s["small_in"], 16)
            sp.dma_start(g_out_bc[:], g_out.rearrange("(o d) -> o d", o=1).broadcast_to([T, D])).then_inc(s["small_in"], 16)
            sp.dma_start(wv_aug[0:C, :], wkv[:, H * E:2 * H * E]).then_inc(s["small_in"], 16)
            sp.dma_start(wout_sb[:], wout.rearrange("(j p) d -> p j d", p=128)).then_inc(s["wout_in"], 16)
            def preset_slots():
                sp.wait_ge(s["unused_set"], 1)
                for z in range(0, SLOTS, FILL_ROWS):
                    sp.dma_start(xs_d[z:z + FILL_ROWS].rearrange("(p r) d -> p (r d)", p=128),
                                 unused[:].rearrange("p r d -> p (r d)")).then_inc(s["xs_filled"], 16)

            def preset_results(half):
                rows = TOKENS * K2
                for z in range(half * rows // 2, (half + 1) * rows // 2, FILL_ROWS):
                    sp.dma_start(ys_d[z:z + FILL_ROWS].rearrange("(p r) d -> p (r d)", p=128), zeros[:]).then_inc(s["ys_filled"], 16)

            sp.wait_ge(s["r1_done"], 1)
            sp.dma_start(x_raw[:], x[GB:2 * GB].rearrange("b t d -> t b d")).then_inc(s["x_in"], 16)

            def group(g):
                def batches(dram, i):
                    part = dram[i * GB:(i + 1) * GB] if isinstance(i, int) else dram[bass.ds(i * GB, GB)]
                    return part.rearrange("b j c -> j b c")

                if more(g):
                    sp.wait_ge(s["ctxT_done"], g + 1)
                    sp.dma_start(ctx_rows[0:S2, :, 0:C], batches(ctx_in, g + 1)).then_inc(s["ctx_in"], 16)
                if isinstance(g, int) and g == 0:
                    preset_slots()
                if routes(g):
                    sp.wait_ge(s["x2_done"], g)
                    at_row = (g - 1) * (GB * T)
                    rows2 = x2_d[at_row:at_row + GB * T] if isinstance(g, int) else x2_d[bass.ds(at_row, GB * T)]
                    sp.dma_start(rows2.rearrange("(b t) d -> t b d", t=T), x2).then_inc(s["x2_saved"], 16)
                if not isinstance(g, int) or g + 2 < NG:
                    sp.wait_ge(s["r1_done"], g + 2)
                    sp.dma_start(x_raw[:], batches(x, g + 2)).then_inc(s["x_in"], 16)

            group(0)
            preset_results(0)
            sp.dma_start(w1_all[:], w1.rearrange("e d f -> d e f")).then_inc(s["ffn_in"], 16)
            sp.dma_start(w2_all[:], w2.rearrange("e (i p) d -> p e i d", p=128)).then_inc(s["ffn_in"], 16)
            group(1)
            preset_results(1)
            with sp.Fori(2, NG - 2) as g:
                group(g)
            group(NG - 2)
            group(NG - 1)
            group(NG)

            sp.wait_ge(s["scattered"], 16 * 2 * GB * NG)
            sp.wait_ge(s["xs_filled"], 16 * SLOTS // FILL_ROWS)

            def rows_of(dram, t):
                part = dram[t * SG:(t + 1) * SG] if isinstance(t, int) else dram[bass.ds(t * SG, SG)]
                return part.rearrange("(p r) d -> p r d", p=128)

            def expert_pair(i):
                for u in range(2 * GPX):
                    t = 2 * GPX * i + u
                    if not isinstance(t, int) or t >= RING:
                        sp.wait_ge(s[f"yg_out{(u + 1) % 2}"], scatter_count(t - RING, (u + 1) % 2))
                    sp.dma_start(xg[u % RING], rows_of(xs_d, t)).then_inc(s[f"xg_in{u % RING}"], 16)

            expert_pair(0)
            with sp.Fori(1, X // 2) as i:
                expert_pair(i)

            sp.wait_ge(s["x2_saved"], 16 * NG)

            def results_of(t):
                rows = K2 * GB * T
                part = ys_d[t * rows:(t + 1) * rows] if isinstance(t, int) else ys_d[bass.ds(t * rows, rows)]
                return part.rearrange("(b t j) d -> t b j d", t=T, j=K2)

            def tokens_of(dram, t):
                part = dram[t * GB * T:(t + 1) * GB * T] if isinstance(t, int) else dram[bass.ds(t * (GB * T), GB * T)]
                return part.rearrange("(b t) d -> t b d", t=T)

            out_rows = out.rearrange("b t d -> (b t) d")

            def load_x2(t, u):
                sp.dma_start(x2b[u], tokens_of(x2_d, t)).then_inc(s[f"x2_back{u}"], 16)

            def load_y(t, u):
                sp.dma_start(yb[u], results_of(t)).then_inc(s[f"y_back{u}"], 16)

            def store(t, par):
                sp.wait_ge(s["out_ready"], t + 1)
                sp.dma_start(tokens_of(out_rows, t), final[par]).then_inc(s[f"out_saved{par}"], 16)

            def token_groups(i, more=True):
                for u in range(TRING):
                    t = TRING * i + u
                    if more:
                        sp.wait_ge(s["r3_summed"], t + 1)
                        load_x2(t + TRING, u)
                        load_y(t + TRING, u)
                    if not (isinstance(t, int) and t == 0):
                        store(t - 1, (u + 1) % 2)

            for u in range(TRING):
                load_x2(u, u)
            for u in range(2):
                sp.wait_ge(s[f"yg_out{u}"], 64 * X * GPX // 2)
            for u in range(TRING):
                load_y(u, u)
            token_groups(0)
            with sp.Fori(1, NG // TRING - 1) as i:
                token_groups(i)
            token_groups(NG // TRING - 1, more=False)
            store(NG - 1, 1)
            for u in range(2):
                sp.wait_ge(s[f"out_saved{u}"], 16 * NG // 2)

        @block.gpsimd
        def _(pool):
            chain = Chain(pool, s["pool_chain"])
            chain.link(pool.memset(ident[:], 0.0))
            pool.affine_select(out=ident[:], in_=ident[:], pattern=[[-1, 128]], compare_op=ALU.not_equal,
                               fill=1.0, base=0, channel_multiplier=1).then_inc(s["ident_set"], 1)
            pool.wait_ge(s["ident_set"], 1)
            chain.link(pool.memset(wk_aug[C:CA, :], 0.0))
            chain.link(pool.memset(wv_aug[C:CA, :], 0.0))
            chain.link(pool.memset(ctx_rows[:], 0.0))
            null_mark = ctx_rows[:, :, NULL_ROW:NULL_ROW + 1]
            chain.link(pool.affine_select(out=null_mark, in_=null_mark, pattern=[[0, GB], [0, 1]], compare_op=ALU.not_equal,
                                          fill=1.0, base=-S2, channel_multiplier=1))
            chain.link(pool.memset(zeros[:], 0.0))
            chain.link(pool.memset(neg_half[:], -0.5))
            chain.link(pool.memset(unused[:], 0.0))
            pool.memset(taken[:], 0.0).then_inc(s["zero_set"], 1)
            for t in (causal, row_bias):
                chain.link(pool.memset(t[:], 0.0))
            for t in (before, ones_b):
                chain.link(pool.memset(t[:], 1.0))
            chain.link(pool.affine_select(out=causal[:], in_=causal[:], pattern=[[-1, T]], compare_op=ALU.is_ge,
                                          fill=MASKED, base=0, channel_multiplier=1))
            chain.link(pool.affine_select(out=before[:], in_=before[:], pattern=[[1, 128]], compare_op=ALU.is_gt,
                                          fill=0.0, base=0, channel_multiplier=-1))
            chain.link(pool.affine_select(out=row_bias[:], in_=row_bias[:], pattern=[[0, 1]], compare_op=ALU.not_equal,
                                          fill=1.0, base=-MASK_ROW, channel_multiplier=1))
            for e in range(X):
                chain.link(pool.memset(rev[:, e:e + 1], float(X - e)))
            pool.memset(top[:], 0.0).then_inc(s["consts"], 1)

            def rsqrt(dst, var, plus):
                alone(pool)
                chain.link(pool.tensor_scalar(plus, var, EPS, None, ALU.add))
                return pool.tensor_tensor(dst, plus, neg_half[:, 0:dst.shape[1]], ALU.pow)

            def self_norm(g):
                pool.wait_ge(s["r1_var"], g + 1)
                var = mv1[:, :, 1]
                rsqrt(rs1[:], var, lnt[:, 0, :]).then_inc(s["x1_rstd"], 1)
                pool.wait_ge(s["x1_rstd"], g + 1)
                chain.link(pool.tensor_tensor(lnt[:, 1, :], rs1[:], rs1[:], ALU.mult))
                chain.link(pool.tensor_tensor(lnt[:, 2, :], lnt[:, 1, :], var, ALU.mult))
                rsqrt(rn1[:, 1, :], lnt[:, 2, :], lnt[:, 0, :]).then_inc(s["x1_norm"], 1)

            def split(hi, lo, whole, done):
                alone(pool)
                chain.link(pool.tensor_copy(hi, whole))
                alone(pool)
                pool.tensor_tensor(lo, whole, hi.bitcast(F32), ALU.subtract).then_inc(done, 1)

            self_norm(0)
            pool.wait_ge(s["small_in"], 16 * 5)
            split(wv_hi[:], wv_lo[:], wv_aug[:], s["wv_split"])

            def norm_probs(m, par, half):
                pool.wait_ge(s["totals_done"], m)
                alone(pool)
                part = P[par][:, HH * half:HH * (half + 1), :]
                pool.tensor_tensor(part, part, rec[half][:].unsqueeze(2).broadcast_to([T, HH, KEYS]),
                                   ALU.mult).then_inc(s["probs_normed"], 1)

            def scatter(b):
                for j in range(2):
                    pool.indirect_dma_start(
                        out=xs_d, out_offset=bass.IndirectOffsetOnAxis(ap=slot[:, j, b:b + 1], axis=0),
                        in_=routed[:, j, b, :], in_offset=None, bounds_check=SLOTS - 1,
                        oob_is_err=False).then_inc(s["scattered"], 16)

            def group(g):
                for k in range(GB):
                    c, p, q = live(g, k)
                    cnt = 2 * GB * g + 2 * k
                    if p:
                        norm_probs(cnt, (k + 1) % 2, 1)
                    if k == 3 and more(g):
                        self_norm(g + 1)
                    if q:
                        pool.wait_ge(s["out_var"], GB * g + (k - 1))
                        rsqrt(rs_o[:], mv_o[:, 1:2], lne_o[:]).then_inc(s["out_rstd"], 1)
                    if c:
                        norm_probs(cnt + 1, k % 2, 0)
                    if k == 0 and places(g):
                        pool.wait_ge(s["slots_done"], g - 1)
                        pool.wait_ge(s["xs_filled"], 16 * SLOTS // FILL_ROWS)
                        alone(pool)
                        for b in range(GB // 2):
                            scatter(b)
                    if k == 1 and places(g):
                        for b in range(GB // 2, GB):
                            scatter(b)
                    if k == 1 and routes(g):
                        pool.wait_ge(s["r2_var"], g)
                        rsqrt(rs2[:], mv2[:, :, 1], lne2[:]).then_inc(s["x2_rstd"], 1)
                    if k == 1 and (not isinstance(g, int) or g < NG):
                        if routes(g):
                            pool.wait_ge(s["r2_done"], GB * g)
                        alone(pool)
                        pool.tensor_copy(x1_late[:], x1[:, 1:GB, :]).then_inc(s["x1_saved"], 1)
                    if k == 3 and routes(g):
                        pool.wait_ge(s["x2_done"], g)
                        alone(pool)
                        chain.link(pool.tensor_copy(routed[:, 1, :, 0:D], x2))

            all_groups(pool, group, chain, POOL_LINKS)
            pool.wait_ge(s["slots_done"], NG)
            for b in range(GB):
                scatter(b)

            pool.wait_ge(s["ys_filled"], 16 * TOKENS * K2 // FILL_ROWS)

            def expert_pair(i):
                for u in range(2 * GPX):
                    t = 2 * GPX * i + u
                    pool.wait_ge(s["y_kept"], t + 1)
                    alone(pool)
                    for r in range(4):
                        pool.indirect_dma_start(
                            out=ys_d, out_offset=bass.IndirectOffsetOnAxis(ap=xg[u % RING][:, r, D:D + 1].bitcast(I32), axis=0),
                            in_=yg[u % 2][:, r, :], in_offset=None, bounds_check=TOKENS * K2 - 1,
                            oob_is_err=False).then_inc(s[f"yg_out{u % 2}"], 16)

            expert_pair(0)
            with pool.Fori(1, X // 2) as i:
                expert_pair(i)

            def token_groups(i):
                for u in range(TRING):
                    t = TRING * i + u
                    pool.wait_ge(s["r3_var"], t + 1)
                    if not isinstance(t, int) or t >= TRING:
                        pool.wait_ge(s["out_ready"], t - (TRING - 1))
                    chain.link(rsqrt(rs3[u][:], mv3[u][:, :, 1], lne3))
                    chain.link(pool.tensor_tensor(nb3[u][:], mv3[u][:, :, 0], rs3[u][:], ALU.mult))
                    alone(pool)
                    pool.tensor_scalar(nb3[u][:], nb3[u][:], -1.0, None, ALU.mult).then_inc(s["r3_rstd"], 1)

            token_groups(0)
            with pool.Fori(1, NG // TRING) as i:
                chain.enter(i, 1, 3 * TRING)
                token_groups(i)
            chain.leave(NG // TRING - 1)

        @block.scalar
        def _(act):
            def copy(dst, src, **kw):
                return nc.scalar.activation(dst, src, ACT.Copy, **kw)

            def self_xT(g):
                act.wait_ge(s["xT_done"], g + 1)
                copy(xT[:].rearrange("p b t -> p (b t)"), ps_w[:, F, :]).then_inc(s["xT_kept"], 1)

            def self_AV(g):
                act.wait_ge(s["sA_done"], g + 1)
                copy(sA[:].rearrange("p b t -> p (b t)"), ps_w[:, F, :]).then_inc(s["sA_kept"], 1)
                act.wait_ge(s["sV_done"], g + 1)
                copy(sV[:].rearrange("p b t -> p (b t)"), ps_w[:, W, :]).then_inc(s["sV_kept"], 1)

            def self_exp(g):
                act.wait_ge(s["sS_masked"], g + 1)
                for b in range(GB):
                    last = nc.scalar.activation(sP[:, b, :], sS[:, b, :], ACT.Exp, bias=s_nmax[:, b:b + 1],
                                                accum_out=s_sum[:, b:b + 1])
                last.then_inc(s["sP_done"], 1)

            def self_PT(g):
                act.wait_ge(s["sPT_done"], g + 1)
                copy(sPT[:].rearrange("p b t -> p (b t)"), ps_w[:, F, :]).then_inc(s["sPT_kept"], 1)

            def turn_x1(g):
                act.wait_ge(s["x1T_done"], g + 1)
                copy(x1T_hi[:].rearrange("p b t -> p (b t)"), ps_w[:, F, :]).then_inc(s["x1T_kept"], 1)

            def keep_A(g, heads):
                for h in heads:
                    act.wait_ge(s["a_done"], g * H + (h + 1))
                    nc.scalar.activation(A[:CA, h].rearrange("p b t -> p (b t)"), bank(slot_of(h)), ACT.Identity,
                                         bias=row_bias[:, 0:1]).then_inc(s["a_kept"], 1)

            act.wait_ge(s["setup_T"], 1)
            copy(wqT_a[:], ps_s[:, 0, 0:128])
            copy(wkT_a[:], ps_s[:, 0, 128:256])
            copy(wgT[:], ps_s[:, 0, 256:256 + X]).then_inc(s["setup_Ts"], 1)
            self_xT(0)
            self_AV(0)
            act.wait_ge(s["setup_T"], 2)
            copy(wqT[:].rearrange("p j d -> p (j d)"), ps_v[:].rearrange("p b n -> p (b n)")).then_inc(s["setup_Ts"], 1)
            act.wait_ge(s["setup_T"], 3)
            copy(wkT[:].rearrange("p (b j) c -> p b j c", b=2), heads4(ps_t, 128, CA)).then_inc(s["setup_Ts"], 1)
            self_exp(0)
            self_PT(0)
            turn_x1(0)
            act.wait_ge(s["consts"], 1)
            keep_A(0, range(H))

            def exp_half(cnt, k, half):
                act.wait_ge(s["shifted_done"], cnt + (half + 1))
                nc.scalar.activation(P[k % 2][:, HH * half:HH * (half + 1), :].rearrange("p h j -> p (h j)"),
                                     shifted[half][:].rearrange("p b h j -> p (b h j)"), ACT.Exp,
                                     scale=(rn1[:, 0, k:k + 1])).then_inc(s["probs_done"], 1)

            def keep_PT(cnt, half):
                act.wait_ge(s["PT_done"], cnt + (half - 1))
                copy(PT[:].rearrange("p h t -> p (h t)"), ps_t[:KEYS].rearrange("p b n -> p (b n)")).then_inc(s["PT_kept"], 1)

            def keep_OT(cnt, half):
                act.wait_ge(s["pv_done"], cnt + (half - 1))
                copy(OT[:, HB * half:HB * (half + 1), :].rearrange("p j t -> p (j t)"), ps_v[:, half, :]).then_inc(s["OT_kept"], 1)

            def group(g):
                for k in range(GB):
                    c, p, q = live(g, k)
                    cnt = 2 * GB * g + 2 * k
                    if k == 0 and c:
                        act.wait_ge(s["x1_norm"], g + 1)
                        if p:
                            act.wait_ge(s["probs_done"], cnt)
                        copy(rn1[:, 0, :], rn1[:, 1, :]).then_inc(s["act_chain"], 1)
                        act.wait_ge(s["act_chain"], g + 1)
                    if k == 3 and routes(g):
                        act.wait_ge(s["logits_done"], g)
                        copy(logits[:].rearrange("p b e -> p (b e)"), ps_w[:, F, 0:GB * X]).then_inc(s["logits_kept"], 1)
                    if p:
                        keep_PT(cnt, 0)
                    if c:
                        act.wait_ge(s["v_done"], GB * g + (k + 1))
                        copy(V[k % 2][:], ps_v[:KEYS].rearrange("p b (h e) -> p (b h) e", e=E)).then_inc(s["v_kept"], 1)
                        exp_half(cnt, k, 0)
                    if k == 0 and more(g):
                        self_xT(g + 1)
                    if p:
                        keep_OT(cnt, 0)
                    if k == 1 and more(g):
                        self_exp(g + 1)
                    if p:
                        keep_PT(cnt, 1)
                    if k == 0 and more(g):
                        self_AV(g + 1)
                    if k == 1 and more(g):
                        self_PT(g + 1)
                    if k == 2 and routes(g):
                        act.wait_ge(s["x2T_done"], g)
                        copy(x2T[:].rearrange("p b t -> p (b t)"), ps_w[:, W, :]).then_inc(s["x2T_kept"], 1)
                    if k == 3 and more(g):
                        turn_x1(g + 1)
                    if k == 3 and more(g):
                        keep_A(g + 1, range(0, 4))
                    if c and not (k == 3 and more(g)):
                        exp_half(cnt, k, 1)
                    if p:
                        keep_OT(cnt, 1)
                    if k == 3 and more(g):
                        keep_A(g + 1, range(4, 7))
                        exp_half(cnt, k, 1)
                    if k == 3 and more(g):
                        keep_A(g + 1, range(7, H))
                    if k == 3 and routes(g):
                        act.wait_ge(s["dlt_done"], g)
                        nc.scalar.activation(ex[:], dlt[:], ACT.Exp).then_inc(s["ex_done"], 1)

            all_groups(act, group)

            def rows_hi(t):
                act.wait_ge(s["xgT_done"], t + 1)
                copy(xgT_hi[:], ps_t[:, 0, :]).then_inc(s["xg_hi_kept"], 1)

            def weights_hi(e, par):
                one = slice(e, e + 1) if isinstance(e, int) else bass.ds(e, 1)
                copy(w2_e[par][:], w2_all[:, one].rearrange("p o i d -> p (o i) d"))
                copy(w1_hi[par][:], w1_all[:, one].rearrange("p o f -> p (o f)")).then_inc(s["w1_hi_kept"], 1)

            def expert_pair(i):
                for u in range(2 * GPX):
                    t = 2 * GPX * i + u
                    act.wait_ge(s["inp_done"], t + 1)
                    if not isinstance(t, int) or t >= 1:
                        act.wait_ge(s["hid_done"], t)
                    nc.scalar.activation(act_u, ps_v[:], ACT.Gelu).then_inc(s["gelu_done"], 1)
                    if not (isinstance(t, int) and t + 1 == X * GPX):
                        rows_hi(t + 1)
                    e = 2 * i + (u // GPX + 1)
                    if u % GPX == 1 and not (isinstance(e, int) and e == X):
                        weights_hi(e, (u // GPX + 1) % 2)

            act.wait_ge(s["ffn_in"], 16 * 2)
            weights_hi(0, 0)
            rows_hi(0)
            expert_pair(0)
            with act.Fori(1, X // 2 - 1) as i:
                expert_pair(i)
            expert_pair(X // 2 - 1)

            def token_groups(i):
                for u in range(TRING):
                    t, par = TRING * i + u, u % 2
                    act.wait_ge(s["r3_rstd"], t + 1)
                    if not isinstance(t, int) or t >= 2:
                        act.wait_ge(s[f"out_saved{par}"], (t - 2) * 8 + (16 - 8 * par))
                    for b in range(GB):
                        last = nc.scalar.activation(final[par][:, b, :], r3[u][:, b, :], ACT.Identity,
                                                    scale=rs3[u][:, b:b + 1], bias=nb3[u][:, b:b + 1])
                    last.then_inc(s["out_ready"], 1)

            token_groups(0)
            with act.Fori(1, NG // TRING) as i:
                token_groups(i)

        @block.vector
        def _(dve):
            chain = Chain(dve, s["dve_chain"])
            v = nc.vector

            dve.wait_ge(s["zero_set"], 1)
            v.tensor_scalar(unused[:, :, D:D + 1].bitcast(I32), unused[:, :, D:D + 1], 1.0, float(SKIP), ALU.mult,
                            ALU.add).then_inc(s["unused_set"], 1)
            dve.wait_ge(s["setup_qk"], 1)
            v.tensor_scalar(wqk[:], ps_s[:, 1, 0:D], float(D) ** -0.5, None, ALU.mult).then_inc(s["setup_done"], 1)
            dve.wait_ge(s["mask_in"], 16)
            chain.link(v.tensor_copy(mask_f[:], mask_u8[:]))
            v.tensor_scalar(mask_f[:], mask_f[:], 1.0, -MASKED, ALU.subtract, ALU.mult).then_inc(s["setup_mask"], 1)
            dve.wait_ge(s["setup_T"], 4)
            chain.link(v.tensor_copy(maskT[:], ps_s[:S2, 1, 128:128 + B]))

            def mask_col(g):
                src = maskT[:, GB * g:GB * (g + 1)] if isinstance(g, int) else maskT[:, bass.ds(g * GB, GB)]
                v.tensor_scalar(ctx_rows[0:S2, :, MASK_ROW], src, 1.0, None, ALU.mult).then_inc(s["mask_col"], 1)

            mask_col(0)

            def self_mask(g):
                dve.wait_ge(s["sS_done"], g + 1)
                chain.link(v.tensor_tensor(sS[:], ps_w[:, F, :].rearrange("p (b t) -> p b t", b=GB),
                                           causal[:].unsqueeze(1).broadcast_to([T, GB, T]), ALU.add))
                v.tensor_reduce(s_nmax[:], sS[:], AX_X, ALU.max, negate=True).then_inc(s["sS_masked"], 1)

            def self_residual(g):
                dve.wait_ge(s["sPV_done"], g + 1)
                dve.wait_ge(s["x_in"], g * 16 + 16)
                chain.link(v.reciprocal(s_rec[:], s_sum[:]))
                for b in range(GB):
                    last = v.scalar_tensor_tensor(r1[:, b, :], ps_w[:, F, T * b:T * (b + 1)], s_rec[:, b:b + 1],
                                                  x_raw[:, b, :], ALU.mult, ALU.add)
                last.then_inc(s["r1_done"], 1)

            def self_stats(g):
                dve.wait_ge(s["r1_done"], g + 1)
                for b in range(GB):
                    last = v.bn_stats(st6[:, b, :], r1[:, b, :])
                chain.link(last)
                alone(dve)
                for b in range(GB):
                    last = v.bn_aggr(mv1[:, b, :], st6[:, b, :])
                last.then_inc(s["r1_var"], 1)

            def x1T_rest(g):
                dve.wait_ge(s["x1T_kept"], g + 1)
                v.tensor_tensor(x1T_lo[:].rearrange("p b t -> p (b t)"), ps_w[:, F, :],
                                x1T_hi[:].rearrange("p b t -> p (b t)").bitcast(F32), ALU.subtract).then_inc(s["x1T_split"], 1)

            def keep_ctxT(g):
                dve.wait_ge(s["ctxT_done"], g + 1)
                v.tensor_copy(ctxT[:].rearrange("p b j -> p (b j)"), bank(CTX_SLOT)[:, 0:GB * KEYS]).then_inc(s["ctxT_kept"], 1)
                dve.wait_ge(s["ctxT_kept"], g + 1)
                alone(dve)
                chain.link(v.tensor_copy(ctxT_hi[:], ctxT[:]))
                v.tensor_tensor(ctxT_lo[:], ctxT[:], ctxT_hi[:].bitcast(F32), ALU.subtract).then_inc(s["ctxT_split"], 1)

            def self_apply(g):
                dve.wait_ge(s["x1_rstd"], g + 1)
                for b in range(GB):
                    last = v.tensor_scalar(x1[:, b, :], r1[:, b, :], mv1[:, b, 0:1], rs1[:, b:b + 1],
                                           ALU.subtract, ALU.mult)
                last.then_inc(s["x1_done"], 1)

            dve.wait_ge(s["consts"], 1)
            self_mask(0)
            dve.wait_ge(s["small_in"], 16 * 5)
            for half in range(2):
                dve.wait_ge(s["setup_G"], half + 1)
                ps = ps_v if half == 0 else ps_t
                flat = shifted[0][:].rearrange("p b h j -> p (b h j)")[:, 0:HH * CA]
                whole = flat.rearrange("p (i b c) -> p b i c", b=2, c=CA)
                chain.link(v.tensor_scalar(whole, heads4(ps, D, CA), g_col[:, 0:1], float(E) ** -0.5, ALU.mult, ALU.mult))
                hi = G_hi[:, HH * half:HH * (half + 1), :].rearrange("p h c -> p (h c)")
                lo = G_lo[:, HH * half:HH * (half + 1), :].rearrange("p h c -> p (h c)")
                chain.link(v.tensor_copy(hi, flat))
                v.tensor_tensor(lo, flat, hi.bitcast(F32), ALU.subtract).then_inc(s["setup_Gs"], 1)
                dve.wait_ge(s["setup_Gs"], half + 1)
                if half == 0:
                    self_residual(0)
                    self_stats(0)
            self_apply(0)
            x1T_rest(0)
            keep_ctxT(0)
            dve.wait_ge(s["token_no"], 1)
            for b in range(GB):
                for j in range(2):
                    last = v.tensor_scalar(result_row[:, j, b:b + 1], ps_s[:, 0, 0:1], float(K2), float(K2 * T * b + j),
                                           ALU.mult, ALU.add)
            last.then_inc(s["rows_set"], 1)
            dve.wait_ge(s["rows_set"], 1)

            def shift(c, cnt, half, p):
                dve.wait_ge(s["scores_done"], cnt + (half + 1))
                scores = heads4(ps_s, T, KEYS)
                chain.link(v.tensor_reduce(top[:], scores, AX_X, ALU.max))
                if p:
                    dve.wait_ge(s["probs_done"], cnt + (half - 1))
                v.tensor_tensor(shifted[half][:], scores, top[:].unsqueeze(3).broadcast_to([T, 2, HB, KEYS]),
                                ALU.subtract).then_inc(s["shifted_done"], 1)

            def sum_probs(m, par, half):
                dve.wait_ge(s["probs_done"], m)
                part = P[par][:, HH * half:HH * (half + 1), :]
                chain.link(v.tensor_reduce(total[half][:], part, AX_X, ALU.add))
                wait(dve, s["probs_normed"], m - 2)
                v.reciprocal(rec[half][:], total[half][:]).then_inc(s["totals_done"], 1)

            def route_top2(g):
                dve.wait_ge(s["logits_kept"], g)
                revs = rev[:].unsqueeze(1).broadcast_to([T, GB, X])
                for j in range(2):
                    src = logits[:] if j == 0 else L2[:]
                    chain.link(v.tensor_reduce(m12[:, j, :], src, AX_X, ALU.max))
                    chain.link(v.tensor_tensor(eq[:], src, m12[:, j, :].unsqueeze(2).broadcast_to([T, GB, X]), ALU.is_equal))
                    chain.link(v.tensor_tensor(eq[:], eq[:], revs, ALU.mult))
                    chain.link(v.tensor_reduce(r12[:, j, :], eq[:], AX_X, ALU.max))
                    chain.link(v.tensor_tensor(oh[:, j], r12[:, j, :].unsqueeze(2).broadcast_to([T, GB, X]), revs, ALU.is_equal))
                    if j == 0:
                        chain.link(v.scalar_tensor_tensor(L2[:], oh[:, 0], MASKED, logits[:], ALU.mult, ALU.add))
                v.tensor_tensor(picked[:], oh[:, 0], oh[:, 1], ALU.add).then_inc(s["picked_done"], 1)
                v.tensor_tensor(dlt[:], m12[:, 1, :], m12[:, 0, :], ALU.subtract).then_inc(s["dlt_done"], 1)

            def route_ranks(g):
                dve.wait_ge(s["rank_done"], g)
                ranks = ps_w[:, F, 0:(GB + 1) * X].rearrange("p (b e) -> p b e", e=X)
                chain.link(v.tensor_tensor(pos[:], ranks[:, 0:GB, :], taken[:].unsqueeze(1).broadcast_to([T, GB, X]), ALU.add))
                v.tensor_tensor(taken[:], taken[:], ranks[:, GB, :], ALU.add).then_inc(s["rank_read"], 1)

            def route_slots(g):
                dve.wait_ge(s["ex_done"], g)
                dve.wait_ge(s["rank_read"], g)
                chain.link(v.tensor_scalar(gate[:, 0, :], ex[:], 1.0, None, ALU.add))
                chain.link(v.tensor_tensor(at[:], oh[:], pos[:].unsqueeze(1).broadcast_to([T, 2, GB, X]), ALU.mult))
                chain.link(v.reciprocal(gate[:, 0, :], gate[:, 0, :]))
                chain.link(v.tensor_reduce(place[:], at[:], AX_X, ALU.add))
                chain.link(v.tensor_tensor(gate[:, 1, :], ex[:], gate[:, 0, :], ALU.mult))
                v.tensor_scalar(first[:], r12[:], -float(CAP), float(X * CAP), ALU.mult, ALU.add)
                chain.link(v.tensor_scalar(over[:], place[:], float(CAP), None, ALU.is_ge))
                chain.link(v.tensor_tensor(slot_f[:], first[:], place[:], ALU.add))
                v.tensor_scalar(routed[:, :, :, D + 1], gate[:], 1.0, None, ALU.mult)
                v.tensor_scalar(routed[:, :, :, D].bitcast(I32), result_row[:], 1.0, None, ALU.mult)
                v.scalar_tensor_tensor(slot[:], over[:], float(SKIP), slot_f[:], ALU.mult, ALU.add).then_inc(s["slots_done"], 1)
                dve.wait_ge(s["slots_done"], g)
                chain.link(v.tensor_scalar(result_row[:], result_row[:], float(K2 * GB * T), None, ALU.add))

            def group(g):
                for k in range(GB):
                    c, p, q = live(g, k)
                    cnt = 2 * GB * g + 2 * k
                    if p:
                        sum_probs(cnt, (k + 1) % 2, 1)
                    if k == 3 and more(g):
                        self_stats(g + 1)
                    if c:
                        shift(c, cnt, 0, p)
                    if k == 2 and routes(g):
                        dve.wait_ge(s["x2_rstd"], g)
                        if not isinstance(g, int) or g >= 2:
                            dve.wait_ge(s["scattered"], g * (32 * GB) - 32 * GB)
                            dve.wait_ge(s["x2_saved"], g * 16 - 16)
                        for b in range(GB):
                            last = v.tensor_scalar(x2[:, b, :], r2[:, b, :], mv2[:, b, 0:1], rs2[:, b:b + 1],
                                                   ALU.subtract, ALU.mult)
                        last.then_inc(s["x2_done"], 1)
                    if k == 0 and places(g):
                        route_ranks(g - 1)
                    if q:
                        dve.wait_ge(s["wout_done"], GB * g + (k - 1))
                        chain.link(v.bn_stats(st_o[:], ps_w[:, W, 0:D]))
                        alone(dve)
                        v.bn_aggr(mv_o[:], st_o[:]).then_inc(s["out_var"], 1)
                        dve.wait_ge(s["out_var"], GB * g + (k - 1))
                        v.scalar_tensor_tensor(centred[:], ps_w[:, W, 0:D], mv_o[:, 0:1], g_out_bc[:], ALU.subtract,
                                               ALU.mult).then_inc(s["out_centred"], 1)
                    if k == 3 and more(g):
                        dve.wait_ge(s["x1_saved"], g + 1)
                        self_apply(g + 1)
                    if k == 1 and more(g):
                        self_mask(g + 1)
                    if c:
                        sum_probs(cnt + 1, k % 2, 0)
                    if k == 3 and more(g):
                        x1T_rest(g + 1)
                    if q:
                        dve.wait_ge(s["out_rstd"], GB * g + (k - 1))
                        dve.wait_ge(s["out_centred"], GB * g + (k - 1))
                        if k == 3:
                            dve.wait_ge(s["x1_saved"], g + 1)
                        res = x1[:, 0, :] if k == 2 else x1_of(g, k)
                        j = (k + 2) % GB
                        v.scalar_tensor_tensor(r2[:, j, :], centred[:], rs_o[:, 0:1], res, ALU.mult,
                                               ALU.add).then_inc(s["r2_done"], 1)
                        dve.wait_ge(s["r2_done"], GB * g + (k - 1))
                        chain.link(v.bn_stats(st_o[:], r2[:, j, :]))
                        alone(dve)
                        last = v.bn_aggr(mv2[:, j, :], st_o[:])
                        if k == 1:
                            last.then_inc(s["r2_var"], 1)
                        else:
                            chain.link(last)
                    if c:
                        shift(c, cnt, 1, p)
                    if k == 0 and places(g):
                        route_slots(g - 1)
                    if k == 0 and more(g):
                        dve.wait_ge(s["ctxT_done"], g + 1)
                        mask_col(g + 1)
                    if k == 2 and more(g):
                        self_residual(g + 1)
                    if k == 3 and more(g):
                        keep_ctxT(g + 1)
                    if k == 3 and routes(g):
                        route_top2(g)

            def x1_of(g, k):
                return x1_late[:, {3: 0, 0: 1, 1: 2}[k], :]

            all_groups(dve, group, chain, DVE_LINKS)
            route_ranks(NG)
            route_slots(NG)

            def rows_lo(t):
                dve.wait_ge(s["xg_hi_kept"], t + 1)
                v.tensor_tensor(xgT_lo[:], ps_t[:, 0, :], xgT_hi[:].bitcast(F32), ALU.subtract).then_inc(s["xg_lo_kept"], 1)

            def weights_lo(e, par):
                dve.wait_ge(s["w1_hi_kept"], e + 1)
                alone(dve)
                one = slice(e, e + 1) if isinstance(e, int) else bass.ds(e, 1)
                v.tensor_tensor(w1_lo[par][:], w1_all[:, one].rearrange("p o f -> p (o f)"), w1_hi[par][:].bitcast(F32),
                                ALU.subtract).then_inc(s["w_split"], 1)

            def keep_y(t, u):
                dve.wait_ge(s["y_done"], t + 1)
                if not isinstance(t, int) or t >= 2:
                    dve.wait_ge(s[f"yg_out{u % 2}"], scatter_count(t - 2, u % 2))
                v.tensor_tensor(yg[u % 2], ps_s[:, u % 2, :].rearrange("p (r d) -> p r d", r=4),
                                xg[u % RING][:, :, D + 1:D + 2].broadcast_to([128, 4, D]), ALU.mult).then_inc(s["y_kept"], 1)

            def expert_pair(i):
                for u in range(2 * GPX):
                    t = 2 * GPX * i + u
                    dve.wait_ge(s["gates_done"], t + 1)
                    dve.wait_ge(s["gelu_done"], t + 1)
                    v.tensor_tensor(hid[u % 2], act_u, ps_w[:], ALU.mult).then_inc(s["hid_done"], 1)
                    if not (isinstance(t, int) and t + 1 == X * GPX):
                        rows_lo(t + 1)
                    e = 2 * i + (u // GPX + 1)
                    if u % GPX == 1 and not (isinstance(e, int) and e == X):
                        weights_lo(e, (u // GPX + 1) % 2)
                    if not isinstance(t, int) or t >= 1:
                        keep_y(t - 1, (u - 1) % (2 * GPX))

            weights_lo(0, 0)
            rows_lo(0)
            expert_pair(0)
            with dve.Fori(1, X // 2 - 1) as i:
                expert_pair(i)
            expert_pair(X // 2 - 1)
            keep_y(X * GPX - 1, 2 * GPX - 1)

            def token_groups(i):
                for u in range(TRING):
                    t = TRING * i + u
                    dve.wait_ge(s[f"y_back{u}"], i * 16 + 16)
                    dve.wait_ge(s[f"x2_back{u}"], i * 16 + 16)
                    if not isinstance(t, int) or t >= TRING:
                        dve.wait_ge(s["out_ready"], t - (TRING - 1))
                    chain.link(v.tensor_tensor(r3[u][:], x2b[u], yb[u][:, :, 0, :], ALU.add))
                    v.tensor_tensor(r3[u][:], r3[u][:], yb[u][:, :, 1, :], ALU.add).then_inc(s["r3_summed"], 1)
                    dve.wait_ge(s["r3_summed"], t + 1)
                    for b in range(GB):
                        last = v.bn_stats(st6[:, b, :], r3[u][:, b, :])
                    chain.link(last)
                    alone(dve)
                    for b in range(GB):
                        last = v.bn_aggr(mv3[u][:, b, :], st6[:, b, :])
                    last.then_inc(s["r3_var"], 1)

            token_groups(0)
            with dve.Fori(1, NG // TRING) as i:
                chain.enter(i, 1, 2 * TRING)
                token_groups(i)
            chain.leave(NG // TRING - 1)

        @block.tensor
        def _(pe):
            mm = nc.tensor.matmul

            def turn(dst, src):
                rows = src.shape[0]
                return nc.tensor.transpose(dst, src, ident[:rows, :rows])

            def mm3(dst, a, b):
                mm(dst, a[0], b[0], start=True, stop=False)
                mm(dst, a[1], b[0], start=False, stop=False)
                return mm(dst, a[0], b[1], start=False, stop=True)

            def self_xT(g):
                pe.wait_ge(s["x_in"], g * 16 + 16)
                for b in range(GB):
                    last = turn(ps_w[:, F, T * b:T * (b + 1)], x_raw[:, b, :])
                last.then_inc(s["xT_done"], 1)

            def self_AV(g):
                pe.wait_ge(s["xT_kept"], g + 1)
                mm(ps_w[:, F, :], wqk[:], xT[:].rearrange("p b t -> p (b t)"), start=True, stop=True).then_inc(s["sA_done"], 1)
                for b in range(GB):
                    last = mm(ps_w[:, W, T * b:T * (b + 1)], xT[:, b, :], wv_self[:], start=True, stop=True)
                last.then_inc(s["sV_done"], 1)

            def self_S(g):
                pe.wait_ge(s["sA_kept"], g + 1)
                for b in range(GB):
                    last = mm(ps_w[:, F, T * b:T * (b + 1)], sA[:, b, :], xT[:, b, :], start=True, stop=True)
                last.then_inc(s["sS_done"], 1)

            def self_PT(g):
                pe.wait_ge(s["sS_masked"], g + 1)
                pe.wait_ge(s["sP_done"], g + 1)
                for b in range(GB):
                    last = turn(ps_w[:, F, T * b:T * (b + 1)], sP[:, b, :])
                last.then_inc(s["sPT_done"], 1)

            def self_PV(g):
                pe.wait_ge(s["sPT_kept"], g + 1)
                pe.wait_ge(s["sV_kept"], g + 1)
                for b in range(GB):
                    last = mm(ps_w[:, F, T * b:T * (b + 1)], sPT[:, b, :], sV[:, b, :], start=True, stop=True)
                last.then_inc(s["sPV_done"], 1)

            def turn_x1(g):
                pe.wait_ge(s["x1_done"], g + 1)
                for b in range(GB):
                    last = turn(ps_w[:, F, T * b:T * (b + 1)], x1[:, b, :])
                last.then_inc(s["x1T_done"], 1)

            def turn_ctx(g):
                pe.wait_ge(s["ctx_in"], g * 16 + 16)
                pe.wait_ge(s["mask_col"], g + 1)
                for b in range(GB):
                    last = turn(bank(CTX_SLOT)[:, KEYS * b:KEYS * (b + 1)], ctx_rows[:, b, :])
                last.then_inc(s["ctxT_done"], 1)

            def project(g, heads):
                for h in heads:
                    before_it = slot_of(h) - 4
                    if before_it == CTX_SLOT:
                        pe.wait_ge(s["ctxT_kept"], g + 1)
                    elif before_it >= 0:
                        pe.wait_ge(s["a_kept"], g * H + (before_it + (1 if before_it < CTX_SLOT else 0)))
                    mm3(bank(slot_of(h)), (G_hi[:, h, :], G_lo[:, h, :]),
                        (x1T_hi[:].rearrange("p b t -> p (b t)"),
                         x1T_lo[:].rearrange("p b t -> p (b t)"))).then_inc(s["a_done"], 1)

            pe.wait_ge(s["ident_set"], 1)
            pe.wait_ge(s["self_in"], 16 * 4)
            turn(ps_s[:, 0, 0:128], wq_a[:])
            turn(ps_s[:, 0, 128:256], wk_a[:])
            turn(ps_s[:, 0, 256:256 + X], wg_sb[:]).then_inc(s["setup_T"], 1)
            self_xT(0)
            pe.wait_ge(s["setup_Ts"], 1)
            mm(ps_s[:, 1, 0:D], wqT_a[:], wkT_a[:], start=True, stop=True).then_inc(s["setup_qk"], 1)
            pe.wait_ge(s["setup_done"], 1)
            self_AV(0)
            pe.wait_ge(s["cross_in"], 16 * 2)
            for j in range(8):
                last = turn(ps_v[:, j // 4, 128 * (j % 4):128 * (j % 4 + 1)], wq_sb[:, 128 * j:128 * (j + 1)])
            last.then_inc(s["setup_T"], 1)
            pe.wait_ge(s["small_in"], 16 * 5)
            for j in range(8):
                last = turn(ps_t[:, j // 4, CA * (j % 4):CA * (j % 4 + 1)], wk_aug[:, 128 * j:128 * (j + 1)])
            last.then_inc(s["setup_T"], 1)
            self_S(0)
            pe.wait_ge(s["setup_mask"], 1)
            turn(ps_s[:S2, 1, 128:128 + B], mask_f[:]).then_inc(s["setup_T"], 1)
            pe.wait_ge(s["consts"], 1)
            mm(ps_s[:, 0, 0:1], before[:], ones_b[:, 0:1], start=True, stop=True).then_inc(s["token_no"], 1)
            pe.wait_ge(s["setup_Ts"], 3)
            for half in range(2):
                ps = ps_v if half == 0 else ps_t
                for i in range(HB):
                    for b in range(2):
                        h = HH * half + 2 * i + b
                        last = mm(ps[:, b, CA * i:CA * (i + 1)], wqT[E * b:E * (b + 1), h // 2, :],
                                  wkT[E * b:E * (b + 1), h // 2, :], start=True, stop=True)
                last.then_inc(s["setup_G"], 1)
            self_PT(0)
            self_PV(0)
            turn_x1(0)
            pe.wait_ge(s["setup_Gs"], 2)
            turn_ctx(0)
            pe.wait_ge(s["x1T_split"], 1)
            project(0, (0, 1))
            pe.wait_ge(s["ctxT_kept"], 1)
            project(0, range(2, H))

            def score(k, half, i):
                last = mm(ps_s[:, i // HB, KEYS * (i % HB):KEYS * (i % HB + 1)], A[:CA, HH * half + i, k, :], ctxT[:, k, :],
                          start=True, stop=True)
                if i == HH - 1:
                    last.then_inc(s["scores_done"], 1)

            def turn_probs(par, half):
                for i in range(HH):
                    last = turn(ps_t[:KEYS, i // HB, T * (i % HB):T * (i % HB + 1)], P[par][:, HH * half + i, :])
                last.then_inc(s["PT_done"], 1)

            def weigh(par, half, first, end):
                for i in range(first, end):
                    last = mm(ps_v[E * (i % 2):E * (i % 2 + 1), half, T * (i // 2):T * (i // 2 + 1)],
                              V[par][:, HH * half + i, :], PT[:, i, :], start=True, stop=True)
                if end == HH:
                    last.then_inc(s["pv_done"], 1)

            def group(g):
                for k in range(GB):
                    c, p, q = live(g, k)
                    cnt = 2 * GB * g + 2 * k
                    done = GB * g + k
                    if p:
                        pe.wait_ge(s["probs_normed"], cnt - 1)
                        wait(pe, s["PT_kept"], cnt - 2)
                        if k == 0 and c:
                            pe.wait_ge(s["a_kept"], g * H + (H - 1))
                        turn_probs((k + 1) % 2, 0)
                    if c:
                        if k == 0:
                            pe.wait_ge(s["a_kept"], g * H + H)
                            pe.wait_ge(s["ctxT_kept"], g + 1)
                        wait(pe, s["shifted_done"], cnt)
                        for i in range(HH):
                            score(k, 0, i)
                        if k == 0:
                            pe.wait_ge(s["ctxT_split"], g + 1)
                    if k == 3 and routes(g):
                        pe.wait_ge(s["x2T_kept"], g)
                        if more(g):
                            pe.wait_ge(s["r1_done"], g + 2)
                        elif places(g):
                            pe.wait_ge(s["rank_read"], g - 1)
                        for b in range(GB):
                            last = mm(ps_w[:, F, X * b:X * (b + 1)], x2T[:, b, :], wgT[:], start=True, stop=True)
                        last.then_inc(s["logits_done"], 1)
                    if p or q:
                        wait(pe, s["OT_kept"], cnt - 2)
                    if c:
                        for j in range(2):
                            last = mm3(ps_v[:KEYS, j, :], (ctxT_hi[:, k, :], ctxT_lo[:, k, :]),
                                       (wv_hi[:, BANK * j:BANK * (j + 1)], wv_lo[:, BANK * j:BANK * (j + 1)]))
                        last.then_inc(s["v_done"], 1)
                    if k == 1 and more(g):
                        pe.wait_ge(s["sV_kept"], g + 2)
                    if q:
                        wait(pe, s["out_centred"], done - 2)
                        for j in range(8):
                            last = mm(ps_w[:, W, 0:D], OT[:, j, :], wout_sb[:, j, :], start=(j == 0), stop=(j == 7))
                        last.then_inc(s["wout_done"], 1)
                    if k == 0 and more(g):
                        if places(g):
                            pe.wait_ge(s["rank_read"], g - 1)
                        self_xT(g + 1)
                    if k == 1 and more(g):
                        self_S(g + 1)
                    if k == 2 and more(g):
                        self_PV(g + 1)
                    if p:
                        if c:
                            pe.wait_ge(s["v_kept"], done + 1)
                        pe.wait_ge(s["PT_kept"], cnt - 1)
                        weigh((k + 1) % 2, 0, 0, HH)
                        pe.wait_ge(s["probs_normed"], cnt)
                        turn_probs((k + 1) % 2, 1)
                    if c:
                        pe.wait_ge(s["shifted_done"], cnt + 1)
                        for i in range(HH):
                            score(k, 1, i)
                            if k == 3 and more(g) and i == 1:
                                if routes(g):
                                    pe.wait_ge(s["logits_kept"], g)
                                turn_x1(g + 1)
                    if k == 0 and more(g):
                        if q:
                            pe.wait_ge(s["out_centred"], done - 1)
                        self_AV(g + 1)
                    if k == 1 and more(g):
                        self_PT(g + 1)
                    if k == 2 and routes(g):
                        if q:
                            pe.wait_ge(s["out_centred"], done - 1)
                        pe.wait_ge(s["x2_done"], g)
                        for b in range(GB):
                            last = turn(ps_w[:, W, T * b:T * (b + 1)], x2[:, b, :])
                        last.then_inc(s["x2T_done"], 1)
                    if p:
                        pe.wait_ge(s["PT_kept"], cnt)
                        weigh((k + 1) % 2, 1, 0, HB)
                        if k == 3 and more(g):
                            pe.wait_ge(s["x1T_split"], g + 2)
                            if q:
                                pe.wait_ge(s["out_centred"], done - 1)
                            project(g + 1, range(0, 4))
                        weigh((k + 1) % 2, 1, HB, HH)
                    if k == 3 and more(g):
                        project(g + 1, range(4, CTX_SLOT))
                        pe.wait_ge(s["a_kept"], g * H + (H + CTX_SLOT - 3))
                        turn_ctx(g + 1)
                        project(g + 1, range(CTX_SLOT, H))
                        pe.wait_ge(s["a_kept"], g * H + (H + 13))
                    if k == 3 and routes(g):
                        pe.wait_ge(s["picked_done"], g)
                        if not more(g):
                            pe.wait_ge(s["logits_kept"], g)
                        ranks = ps_w[:, F, 0:(GB + 1) * X]
                        for b in range(GB + 1):
                            for a in range(min(b + 1, GB)):
                                last = mm(ranks[:, X * b:X * (b + 1)], (before if a == b else ones_b)[:], picked[:, a, :],
                                          start=(a == 0), stop=(a == min(b, GB - 1)))
                        last.then_inc(s["rank_done"], 1)

            pe.wait_ge(s["wv_split"], 1)
            pe.wait_ge(s["rows_set"], 1)
            pe.wait_ge(s["wout_in"], 16)
            all_groups(pe, group)

            def load_count(i, u):
                return i * (16 * 2) + 16 * (u // RING + 1)

            def turn_rows(i, u):
                t = 2 * GPX * i + u
                pe.wait_ge(s[f"xg_in{u % RING}"], load_count(i, u))
                if not isinstance(t, int) or t >= 1:
                    pe.wait_ge(s["xg_lo_kept"], t)
                for r in range(4):
                    last = turn(ps_t[:, 0, 128 * r:128 * (r + 1)], xg[u % RING][:, r, 0:D])
                last.then_inc(s["xgT_done"], 1)

            def up(t, u):
                e = u // GPX
                pe.wait_ge(s["xg_lo_kept"], t + 1)
                if not isinstance(t, int) or t >= 1:
                    pe.wait_ge(s["hid_done"], t)
                for b in range(4):
                    ps = ps_v if b < 2 else ps_w
                    last = mm3(ps[:, b % 2, :], (w1_hi[e][:, 128 * b:128 * (b + 1)], w1_lo[e][:, 128 * b:128 * (b + 1)]),
                               (xgT_hi[:], xgT_lo[:]))
                    if b == 1:
                        last.then_inc(s["inp_done"], 1)
                last.then_inc(s["gates_done"], 1)

            def down(t, u):
                e = u // GPX
                pe.wait_ge(s["hid_done"], t + 1)
                if not isinstance(t, int) or t >= 2:
                    pe.wait_ge(s["y_kept"], t - 1)
                for r in range(4):
                    for j in range(2):
                        last = mm(ps_s[:, u % 2, D * r:D * (r + 1)], hid[u % 2][:, j, 128 * r:128 * (r + 1)], w2_e[e][:, j, :],
                                  start=(j == 0), stop=(j == 1))
                last.then_inc(s["y_done"], 1)

            def expert_pair(i):
                for u in range(2 * GPX):
                    t = 2 * GPX * i + u
                    if u % GPX == 0:
                        pe.wait_ge(s["w_split"], 2 * i + (u // GPX + 1))
                    up(t, u)
                    if not (isinstance(t, int) and t + 1 == X * GPX):
                        turn_rows(i + (u + 1) // (2 * GPX), (u + 1) % (2 * GPX))
                    if not isinstance(t, int) or t >= 1:
                        down(t - 1, (u - 1) % (2 * GPX))

            turn_rows(0, 0)
            expert_pair(0)
            with pe.Fori(1, X // 2 - 1) as i:
                expert_pair(i)
            expert_pair(X // 2 - 1)
            down(X * GPX - 1, 2 * GPX - 1)


POOL_LINKS = 10
DVE_LINKS = 51

_INS = ["x", "ctx_768", "mask_BxS2_bf1", "L0_attn_Wq", "L0_attn_Wk", "L0_attn_Wv", "L0_xattn_g_norm",
        "L0_xattn_null_kv", "L0_xattn_Wq", "L0_xattn_Wkv", "L0_xattn_Wout", "L0_xattn_g_out",
        "L0_ffn_Wg", "L0_ffn_W1", "L0_ffn_W2"]


def kernel(**inputs):
    import numpy as _np
    import concourse.bacc as _bacc
    from concourse import mybir as _mybir
    from concourse.bass_utils import run_bass_kernel_spmd as _run

    nc = _bacc.Bacc("TRN2", target_bir_lowering=False, num_devices=1)
    arrays, args = {}, []
    for name in _INS:
        a = _np.ascontiguousarray(inputs[name])
        arrays[f"in_{name}_dram"] = a
        args.append(nc.dram_tensor(f"in_{name}_dram", a.shape, _mybir.dt.from_np(a.dtype), kind="ExternalInput").ap())
    args.append(nc.dram_tensor("out_0_dram", (B, T, D), F32, kind="ExternalOutput").ap())
    decoder(nc, *args)
    r = _run(nc, [arrays], core_ids=[0])
    return r.results[0]["out_0_dram"]
```
